# Optimizing a Trainium2 kernel written in Bass

```python
import numpy as np
import jax
import jax.numpy as jnp

def _softmax(x, axis=-1):
    return jax.nn.softmax(x, axis=axis)

def _gelu(x):
    return jax.nn.gelu(x, approximate=True)

def _silu(x):
    return jax.nn.silu(x)

def _sigmoid(x):
    return jax.nn.sigmoid(x)

def _layernorm(x, axis=-1, eps=1e-05):
    m = jnp.mean(x, axis=axis, keepdims=True)
    v = jnp.var(x, axis=axis, keepdims=True)
    return (x - m) / jnp.sqrt(v + eps)

def _scatter_add(tgt, idx, src, axis=0):
    return tgt.at[idx].add(src)

def _segment_sum(src, seg, n):
    return jax.ops.segment_sum(src, seg, n)
kernel_name = 'mk_vit_tower_d1_tok_img768_r4_e442e7'

def setup_inputs(seed: int=0):
    np.random.seed(seed)
    _w = jnp.asarray

    def _rec_inputs():
        import jax
        import jax.numpy as jnp
        _rk = jax.random.key(seed)
        x = -0.000356955 + 1 * jax.random.normal(jax.random.fold_in(_rk, 1), (64, 3, 224, 224), jnp.float32)
        return x
    x = _rec_inputs()

    def _L0_tok_setup():
        import jax, jax.numpy as jnp
        import numpy as np
        IMAGE_SIZE = 224
        PATCH = 16
        EMBED = 192
        IN_FEAT = 3 * PATCH * PATCH
        NUM_PATCHES = (IMAGE_SIZE // PATCH) ** 2
        BATCH = 128

        def _patchify(x):
            B, C, H, Wd = x.shape
            p = PATCH
            Hp, Wp = (H // p, Wd // p)
            x = x.reshape(B, C, H, Wp, p)
            x = x.reshape(B, C, Hp, p, Wp, p)
            x = jnp.transpose(x, (0, 1, 2, 4, 5, 3))
            return x.reshape(B, NUM_PATCHES, IN_FEAT)
        key = jax.random.key(seed)
        k1, k2, k3 = jax.random.split(key, 3)
        x = jax.random.normal(k1, (BATCH, 3, IMAGE_SIZE, IMAGE_SIZE), dtype=jnp.float32)
        W = jax.random.normal(k2, (EMBED, IN_FEAT), dtype=jnp.float32) * (1.0 / np.sqrt(IN_FEAT))
        b = jax.random.normal(k3, (EMBED,), dtype=jnp.float32) * 0.01
        return {'x': x, 'W': W, 'b': b}
    _L0_tok_all = _L0_tok_setup()
    _L0_tok_in = {k: v for k, v in _L0_tok_all.items() if k in ('W', 'b')}
    del _L0_tok_all

    def _L0_attn_setup():
        import jax, jax.numpy as jnp
        import numpy as np
        from jax import lax
        NUM_HEADS = 12
        BETA = 0.2
        KS = 3
        LN_EPS = 1e-05
        key = jax.random.key(seed)
        k1, k2 = jax.random.split(key)
        B, N, C = (4, 256, 192)
        x = jax.random.normal(k1, (B, N, C), dtype=jnp.float32)
        qkv_w = jax.random.normal(k2, (3 * C, C), dtype=jnp.float32) * 0.02
        qkv_b = jnp.zeros((3 * C,), dtype=jnp.float32)
        ln_g = jnp.ones((C,), dtype=jnp.float32)
        ln_b = jnp.zeros((C,), dtype=jnp.float32)
        return {'x': x, 'qkv_w': qkv_w, 'qkv_b': qkv_b, 'ln_g': ln_g, 'ln_b': ln_b}
    _L0_attn_all = _L0_attn_setup()
    _L0_attn_in = {k: v for k, v in _L0_attn_all.items() if k in ('qkv_w', 'qkv_b', 'ln_g', 'ln_b')}
    del _L0_attn_all

    def _L0_ffn_setup():
        import jax, jax.numpy as jnp
        import numpy as np
        E = 8
        K = 2
        D = 192
        F = 4 * D
        key = jax.random.key(seed)
        ks = jax.random.split(key, 10)
        s_exp = 0.02
        return {'x': jax.random.normal(ks[0], (4, 256, D), jnp.float32), 'W1': jax.random.normal(ks[1], (E, F, D), jnp.float32) * s_exp, 'b1': jax.random.normal(ks[2], (E, F), jnp.float32) * s_exp, 'W2': jax.random.normal(ks[3], (E, D, F), jnp.float32) * s_exp, 'b2': jax.random.normal(ks[4], (E, D), jnp.float32) * s_exp, 'Wr1': jax.random.normal(ks[5], (D, D), jnp.float32) * s_exp, 'br1': jax.random.normal(ks[6], (D,), jnp.float32) * s_exp, 'Wr2': jax.random.normal(ks[7], (E, D), jnp.float32) * s_exp, 'br2': jax.random.normal(ks[8], (E,), jnp.float32) * s_exp}
    _L0_ffn_all = _L0_ffn_setup()
    _L0_ffn_in = {k: v for k, v in _L0_ffn_all.items() if k in ('W1', 'b1', 'W2', 'b2', 'Wr1', 'br1', 'Wr2', 'br2')}
    del _L0_ffn_all
    return {'x': x, 'L0_tok_W': _L0_tok_in['W'], 'L0_tok_b': _L0_tok_in['b'], 'L0_attn_qkv_w': _L0_attn_in['qkv_w'], 'L0_attn_qkv_b': _L0_attn_in['qkv_b'], 'L0_attn_ln_g': _L0_attn_in['ln_g'], 'L0_attn_ln_b': _L0_attn_in['ln_b'], 'L0_ffn_W1': _L0_ffn_in['W1'], 'L0_ffn_b1': _L0_ffn_in['b1'], 'L0_ffn_W2': _L0_ffn_in['W2'], 'L0_ffn_b2': _L0_ffn_in['b2'], 'L0_ffn_Wr1': _L0_ffn_in['Wr1'], 'L0_ffn_br1': _L0_ffn_in['br1'], 'L0_ffn_Wr2': _L0_ffn_in['Wr2'], 'L0_ffn_br2': _L0_ffn_in['br2']}

def reference(x, L0_tok_W, L0_tok_b, L0_attn_qkv_w, L0_attn_qkv_b, L0_attn_ln_g, L0_attn_ln_b, L0_ffn_W1, L0_ffn_b1, L0_ffn_W2, L0_ffn_b2, L0_ffn_Wr1, L0_ffn_br1, L0_ffn_Wr2, L0_ffn_br2):
    import jax
    import jax.numpy as jnp

    def _L0_tok_ref(x, W, b):
        import jax, jax.numpy as jnp
        import numpy as np
        IMAGE_SIZE = 224
        PATCH = 16
        EMBED = 192
        IN_FEAT = 3 * PATCH * PATCH
        NUM_PATCHES = (IMAGE_SIZE // PATCH) ** 2
        BATCH = 128

        def _patchify(x):
            B, C, H, Wd = x.shape
            p = PATCH
            Hp, Wp = (H // p, Wd // p)
            x = x.reshape(B, C, H, Wp, p)
            x = x.reshape(B, C, Hp, p, Wp, p)
            x = jnp.transpose(x, (0, 1, 2, 4, 5, 3))
            return x.reshape(B, NUM_PATCHES, IN_FEAT)
        patches = _patchify(x)
        return jnp.einsum('bnf,ef->bne', patches, W) + b

    def _L0_attn_ref(x, qkv_w, qkv_b, ln_g, ln_b):
        import jax, jax.numpy as jnp
        import numpy as np
        from jax import lax
        NUM_HEADS = 12
        BETA = 0.2
        KS = 3
        LN_EPS = 1e-05
        B, N, C = x.shape
        H = NUM_HEADS
        D = C // H
        mu = jnp.mean(x, axis=-1, keepdims=True)
        var = jnp.mean(jnp.square(x - mu), axis=-1, keepdims=True)
        xn = (x - mu) * lax.rsqrt(var + LN_EPS) * ln_g + ln_b
        qkv = xn @ qkv_w.T + qkv_b
        qkv = qkv.reshape(B, N, 3, H, D).transpose(2, 0, 3, 1, 4)
        q, k, v = (qkv[0], qkv[1], qkv[2])
        attn = jnp.einsum('bhnd,bhmd->bhnm', q, k) * D ** (-0.5)
        kernel = jnp.ones((KS, KS), dtype=attn.dtype).at[KS // 2, KS // 2].set(0.0)
        kernel = kernel.reshape(1, 1, KS, KS)
        neigh = lax.conv_general_dilated(attn.reshape(B * H, 1, N, N), kernel, window_strides=(1, 1), padding='SAME', dimension_numbers=('NCHW', 'OIHW', 'NCHW'))
        attn = attn - BETA * neigh.reshape(B, H, N, N)
        attn = jax.nn.softmax(attn - jnp.max(attn, axis=-1, keepdims=True), axis=-1)
        out = jnp.einsum('bhnm,bhmd->bhnd', attn, v)
        return out.transpose(0, 2, 1, 3).reshape(B, N, C)

    def _L0_ffn_ref(x, W1, b1, W2, b2, Wr1, br1, Wr2, br2):
        import jax, jax.numpy as jnp
        import numpy as np
        E = 8
        K = 2
        D = 192
        F = 4 * D
        h = jax.nn.relu(jnp.einsum('bsd,hd->bsh', x, Wr1) + br1)
        score = jnp.einsum('bsd,ed->bse', h, Wr2) + br2
        _, idx = jax.lax.top_k(score, K)
        mask = (jax.nn.one_hot(idx, E) > 0).any(axis=-2)
        w = jax.nn.softmax(jnp.where(mask, score, -jnp.inf), axis=-1)
        out = jnp.zeros_like(x)
        for e in range(E):
            mid = jax.nn.relu(jnp.einsum('bsd,fd->bsf', x, W1[e]) + b1[e])
            ye = jnp.einsum('bsf,df->bsd', mid, W2[e]) + b2[e]
            out = out + w[..., e:e + 1] * ye
        return out
    h = _L0_tok_ref(x, L0_tok_W, L0_tok_b)
    h = h + _L0_attn_ref(_layernorm(h, axis=-1), L0_attn_qkv_w, L0_attn_qkv_b, L0_attn_ln_g, L0_attn_ln_b)
    h = h + _L0_ffn_ref(_layernorm(h, axis=-1), L0_ffn_W1, L0_ffn_b1, L0_ffn_W2, L0_ffn_b2, L0_ffn_Wr1, L0_ffn_br1, L0_ffn_Wr2, L0_ffn_br2)
    return h

_drawn_inputs = setup_inputs


def setup_inputs(seed=0):
    import zlib

    import numpy as np

    out = dict(_drawn_inputs(seed))
    spreads = {'L0_attn_qkv_b': (0.0, 0.1), 'L0_attn_ln_g': (1.0, 0.6), 'L0_attn_ln_b': (0.0, 0.274)}
    factors = {'L0_tok_b': 4.61, 'L0_ffn_b1': 8.0, 'L0_ffn_b2': 4.072, 'L0_ffn_br1': 3.125}
    for name, (base, spread) in spreads.items():
        noise = np.random.default_rng([zlib.crc32(name.encode()), seed]).standard_normal(out[name].shape)
        drawn = base * np.exp(spread * noise) if base else spread * noise
        out[name] = jnp.asarray(drawn.astype(out[name].dtype))
    for name, factor in factors.items():
        out[name] = (out[name] * factor).astype(out[name].dtype)
    return out
```

```python
from contextlib import ExitStack

import concourse.bass as bass
from concourse import mybir

F32 = mybir.dt.float32
F16 = mybir.dt.float16
BF16 = mybir.dt.bfloat16
U32 = mybir.dt.uint32
ALU = mybir.AluOpType
ACT = mybir.ActivationFunctionType
AX = mybir.AxisListType

P = 128
IMAGES = 64
TOKENS = 196
DIM = 192
HI = DIM - P
PATCH_DIM = 768
PCH = PATCH_DIM // P
HEADS = 12
HEAD_DIM = 16
HG = 4
GROUPS = HEADS // HG
ROWS = 2 * HEAD_DIM
HALF = TOKENS // 2
PAIR = 2
PAIRS = IMAGES // PAIR
COLS = PAIR * TOKENS
TILES = PAIR * 2
STEPS = GROUPS * PAIR
ALL_STEPS = PAIRS * STEPS
BETA = 0.2
EPS = 1e-5
SCALE = HEAD_DIM ** -0.5
PW = TOKENS + 2

BODY_PAIRS = 2
BODY_STEPS = BODY_PAIRS * STEPS
BODIES = PAIRS // BODY_PAIRS

EXPERTS = 8
HIDDEN = 768
FCH = HIDDEN // P
UNITS = FCH // 2
GT = 256
GTILES = GT // P
FGROUPS = IMAGES * TOKENS // GT
EU = EXPERTS * UNITS
LAG = 2
MID = 4


def wait(eng, sem, value):
    if not isinstance(value, int) or value > 0:
        eng.wait_ge(sem, value)


class Step:

    def __init__(self, body, kk, ahead):
        k = kk + ahead
        self.s = body * BODY_STEPS + k
        self.pair = body * BODY_PAIRS + k // STEPS
        self.there = not isinstance(body, int) or 0 <= self.s < ALL_STEPS
        self.q = (k // STEPS) % 2
        self.odd = k % 2
        self.group = k % GROUPS
        self.image = (k // GROUPS) % PAIR
        self.first = k % STEPS == 0
        self.before = body + (k // STEPS) // 2


class Pair:

    def __init__(self, body, kk, ahead):
        k = kk // STEPS + ahead
        self.u = body * BODY_PAIRS + k
        self.there = not isinstance(body, int) or 0 <= self.u < PAIRS
        self.q = k % 2
        self.before = body + k // 2


def run_bodies(eng, step):
    step(0, -1)
    for kk in range(BODY_STEPS):
        step(0, kk)
    with eng.Fori(1, BODIES - 1) as body:
        for kk in range(BODY_STEPS):
            step(body, kk)
    for kk in range(BODY_STEPS + 2):
        step(BODIES - 1, kk)


def attention_phase(nc, x_t, w_tok, w_qk_a, w_qk_b, w_v_a, w_v_b, b_tok, b_qk, b_v, ln_cols, row_consts, ident_in,
                    h_dram, att_dram):
    ctx = ExitStack()
    with ctx:
        def sb(name, shape, dt=F32):
            return ctx.enter_context(nc.sbuf_tensor(name, shape, dt))

        def ps(name, shape, dt=F32):
            return ctx.enter_context(nc.psum_tensor(name, shape, dt))

        def sem(name):
            return ctx.enter_context(nc.semaphore(name))

        wtok = sb("wtok", [P, PCH, DIM])
        wqk_a = sb("wqk_a", [P, 2 * GROUPS, P])
        wqk_b = sb("wqk_b", [HI, 2 * GROUPS, P])
        wv_a = sb("wv_a", [P, DIM])
        wv_b = sb("wv_b", [HI, DIM])
        btok = sb("btok", [HALF, DIM])
        bqk = sb("bqk", [P, 2 * GROUPS])
        bq_scaled = sb("bq_scaled", [P, GROUPS])
        bv = sb("bv", [HALF, DIM])
        lnc = sb("lnc", [P, 4])
        rowc = sb("rowc", [P, 2 + HG])
        ident = sb("ident", [P, P])
        ident16 = sb("ident16", [P, P], BF16)
        max_sel = sb("max_sel", [P, HG, HALF], BF16)
        minus_half = sb("minus_half", [HALF, TILES])
        one_eps = sb("one_eps", [HALF, TILES])
        eps_sq = sb("eps_sq", [HALF, TILES])
        spacer = sb("spacer", [HALF, 1])
        x_buf = [sb(f"x_buf{i}", [P, PCH, COLS]) for i in range(2)]
        h_buf = sb("h_buf", [HALF, TILES, DIM])
        stats = sb("stats", [HALF, TILES, 6])
        meanvar = sb("meanvar", [HALF, TILES, 2])
        var_eps = [sb(f"var_eps{i}", [HALF, TILES]) for i in range(2)]
        rstd = sb("rstd", [HALF, TILES])
        xn = sb("xn", [HALF, TILES, DIM])
        xt_a = sb("xt_a", [P, COLS])
        xt_b = sb("xt_b", [HI, COLS])
        padded = sb("padded", [P, 2 * GROUPS * PAIR, PW])
        beside = sb("beside", [P, 2 * GROUPS * PAIR, TOKENS])
        qk = sb("qk", [P, 2 * GROUPS * PAIR, TOKENS])
        qk_hi = sb("qk_hi", [P, 2 * GROUPS * PAIR, TOKENS], F16)
        qk_lo = sb("qk_lo", [P, 2 * GROUPS * PAIR, TOKENS], F16)
        q_stack = [sb(f"q_stack{i}", [P, HEADS, PAIR * TOKENS], F16) for i in range(2)]
        k_stack = [sb(f"k_stack{i}", [P, HEADS, PAIR * TOKENS], F16) for i in range(2)]
        v_buf = [sb(f"v_buf{i}", [HALF, TILES, HEADS, 32]) for i in range(2)]
        row_max = [sb(f"row_max{i}", [HALF, 2, HG]) for i in range(2)]
        max_parts = [sb(f"max_parts{i}", [HALF, 2, P], BF16) for i in range(2)]
        max_rows = [sb(f"max_rows{i}", [P, 2, HALF], BF16) for i in range(2)]
        probs = [sb(f"probs{i}", [HALF, HG, 2, TOKENS]) for i in range(2)]
        mixed = [sb(f"mixed{i}", [P, TOKENS]) for i in range(2)]
        recip = sb("recip", [HALF, 2, HG, 1])
        att = [sb(f"att{i}", [HALF, TILES, DIM]) for i in range(2)]

        s_bank = [ps(f"s_bank{i}", [P, 2, 256]) for i in range(2)]
        t_bank = [ps(f"t_bank{i}", [P, 2, 256]) for i in range(2)]
        o_bank = ps("o_bank", [P, 512])
        m_bank = ps("m_bank", [P, 512])
        p_bank = [ps(f"p_bank{i}", [P, 512]) for i in range(2)]
        back_tr = m_bank[0:HALF, 0:2 * P].rearrange("p (u h d) -> p u h d", u=2, h=HG)
        max_tr = m_bank[:, 2 * P:512].bitcast(BF16).rearrange("p (u n) -> p u n", u=2)

        weights_in = sem("weights_in")
        consts_set = sem("consts_set")
        x_in = [sem(f"x_in{i}") for i in range(2)]
        p_ready = [sem(f"p_ready{i}") for i in range(2)]
        h_ready = sem("h_ready")
        h_stored = sem("h_stored")
        stats_ready = sem("stats_ready")
        meanvar_ready = sem("meanvar_ready")
        var_ready = sem("var_ready")
        rstd_ready = sem("rstd_ready")
        xn_ready = sem("xn_ready")
        xt_a_ready = sem("xt_a_ready")
        xt_b_ready = sem("xt_b_ready")
        v_ready = sem("v_ready")
        padded_ready = sem("padded_ready")
        beside_ready = sem("beside_ready")
        qk_ready = sem("qk_ready")
        hi_ready = sem("hi_ready")
        lo_ready = sem("lo_ready")
        q_stacked = sem("q_stacked")
        k_stacked = sem("k_stacked")
        s_ready = sem("s_ready")
        max_ready = sem("max_ready")
        max_hi_ready = sem("max_hi_ready")
        max_parts_ready = sem("max_parts_ready")
        max_tr_ready = sem("max_tr_ready")
        max_rows_ready = sem("max_rows_ready")
        t_ready = sem("t_ready")
        probs_ready = sem("probs_ready")
        o_ready = sem("o_ready")
        mixed_ready = sem("mixed_ready")
        back_ready = sem("back_ready")
        recip_ready = sem("recip_ready")
        att_ready = sem("att_ready")
        att_stored = [sem(f"att_stored{i}") for i in range(2)]

        LOADS = [(wtok, w_tok), (wqk_a, w_qk_a), (wqk_b, w_qk_b), (wv_a, w_v_a), (wv_b, w_v_b), (btok, b_tok),
                 (bqk, b_qk), (bv, b_v), (lnc, ln_cols), (rowc, row_consts), (ident, ident_in)]
        STACKED = 16 * 4 * HG
        USES = 6
        CONSTS = 10 + HG + 2

        block = ctx.enter_context(nc.Block())

        @block.sync
        def _(sp):
            for dst, src in LOADS:
                sp.dma_start(dst[:], src).then_inc(weights_in, 16)

            def load_x(pr):
                if pr.there:
                    wait(sp, p_ready[1], USES * (pr.u - 2) + 1)
                    sp.dma_start(x_buf[pr.q][:], x_t[bass.ds(pr.u, 1)].rearrange("o p c n -> (o p) c n")
                                 ).then_inc(x_in[pr.q], 16)

            def stack(pr, which):
                if pr.there:
                    sp.wait_ge(lo_ready, 2 * pr.u + which + 1)
                    dst = (q_stack, k_stack)[which][pr.q]
                    tiles = slice(which * GROUPS * PAIR, (which + 1) * GROUPS * PAIR)
                    order = ((qk_hi, qk_lo, qk_hi, qk_lo), (qk_hi, qk_hi, qk_lo, qk_lo))[which]
                    for r, part in enumerate(order):
                        for hh in range(HG):
                            sp.dma_start(dst[32 * r:32 * r + 32, hh::HG, :],
                                         part[32 * hh:32 * hh + 32, tiles, :].rearrange("p (g i) n -> p g (i n)",
                                                                                      i=PAIR)
                                         ).then_inc((q_stacked, k_stacked)[which], 16)

            def rows(dram, pr):
                return dram[bass.ds(pr.u, 1)].rearrange("o c p e -> p (o c) e")

            def store_h(pr):
                if pr.there:
                    sp.wait_ge(h_ready, 2 * pr.u + 2)
                    sp.dma_start(rows(h_dram, pr), h_buf[:]).then_inc(h_stored, 16)

            def store_att(pr):
                if pr.there:
                    sp.wait_ge(att_ready, (pr.u + 1) * STEPS)
                    sp.dma_start(rows(att_dram, pr), att[pr.q][:]).then_inc(att_stored[pr.q], 16)

            def step(body, kk):
                k = kk % STEPS
                if kk == -1:
                    load_x(Pair(0, 0, 0))
                    load_x(Pair(0, 0, 1))
                    store_h(Pair(0, 0, 0))
                    stack(Pair(0, 0, 0), 0)
                    stack(Pair(0, 0, 0), 1)
                    store_h(Pair(0, 0, 1))
                elif k == 1:
                    load_x(Pair(body, kk, 2))
                    store_att(Pair(body, kk, -1))
                elif k == 2:
                    stack(Pair(body, kk, 1), 0)
                elif k == 3:
                    stack(Pair(body, kk, 1), 1)
                elif k == 5:
                    store_h(Pair(body, kk, 2))
            run_bodies(sp, step)
            sp.wait_ge(h_stored, 16 * PAIRS)
            for i in range(2):
                sp.wait_ge(att_stored[i], 16 * PAIRS // 2)

        @block.tensor
        def _(pe):
            pe.wait_ge(weights_in, 16 * len(LOADS))
            pe.wait_ge(consts_set, CONSTS)

            def project_patches(pr, half):
                if pr.there:
                    if half == 0:
                        pe.wait_ge(x_in[pr.q], 16 * (pr.before + 1))
                    wait(pe, padded_ready, USES * (pr.u - 1) + 5 + half)
                    for c in range(2):
                        t0 = (2 * half + c) * HALF
                        for f in range(PCH):
                            last = nc.tensor.matmul(p_bank[half][0:HALF, c * DIM:(c + 1) * DIM],
                                                    x_buf[pr.q][:, f, t0:t0 + HALF], wtok[:, f, :],
                                                    start=(f == 0), stop=(f == PCH - 1))
                    last.then_inc(p_ready[half], 1)

            def claim(pr, n):
                if 2 <= n < 4:
                    pe.wait_ge((xt_a_ready, xt_b_ready)[n - 2], pr.u + 1)
                elif 4 <= n < 6:
                    pe.wait_ge(v_ready, PAIR * pr.u + n - 3)
                elif n >= 6:
                    pe.wait_ge(padded_ready, USES * pr.u + n - 5)
                return p_bank[n % 2], p_ready[n % 2]

            def transpose_xn(pr):
                if pr.there:
                    pe.wait_ge(xn_ready, pr.u + 1)
                    for n, (f0, nf) in enumerate(((0, P), (P, HI))):
                        bank, ready = claim(pr, n)
                        for c in range(TILES):
                            last = nc.tensor.transpose(bank[0:nf, c * HALF:(c + 1) * HALF], xn[:, c, f0:f0 + nf],
                                                       ident[0:HALF, 0:HALF])
                        last.then_inc(ready, 1)

            def project_v(pr):
                if pr.there:
                    pe.wait_ge(xt_a_ready, pr.u + 1)
                    pe.wait_ge(xt_b_ready, pr.u + 1)
                    for im in range(PAIR):
                        bank, ready = claim(pr, 2 + im)
                        for c in range(2):
                            t0 = (2 * im + c) * HALF
                            out = bank[0:HALF, c * DIM:(c + 1) * DIM]
                            nc.tensor.matmul(out, xt_a[:, t0:t0 + HALF], wv_a[:], start=True, stop=False)
                            last = nc.tensor.matmul(out, xt_b[:, t0:t0 + HALF], wv_b[:], start=False, stop=True)
                        last.then_inc(ready, 1)

            def project_qk(pr, which):
                if pr.there:
                    for i in range(which * GROUPS, (which + 1) * GROUPS):
                        bank, ready = claim(pr, 4 + i)
                        nc.tensor.matmul(bank[:, 0:COLS], wqk_a[:, i, :], xt_a[:], start=True, stop=False)
                        nc.tensor.matmul(bank[:, 0:COLS], wqk_b[:, i, :], xt_b[:], start=False, stop=True
                                         ).then_inc(ready, 1)

            def transpose_back(st):
                if st.there:
                    pe.wait_ge(mixed_ready, st.s + 1)
                    pe.wait_ge(max_rows_ready, min(st.s + 3, ALL_STEPS) if isinstance(st.s, int) else st.s + 3)
                    wait(pe, att_ready, st.s)
                    for u in range(2):
                        last = nc.tensor.transpose(m_bank[0:HALF, u * P:(u + 1) * P],
                                                   mixed[st.odd][:, u * HALF:(u + 1) * HALF], ident[:])
                    last.then_inc(back_ready, 1)

            def head_cols(st, u=None):
                t0 = st.image * TOKENS + (0 if u is None else u * HALF)
                return slice(t0, t0 + (TOKENS if u is None else HALF))

            def scores(st):
                if st.there:
                    if st.first:
                        pe.wait_ge(q_stacked, (st.pair + 1) * STACKED)
                        pe.wait_ge(k_stacked, (st.pair + 1) * STACKED)
                    for hh in range(HG):
                        head = HG * st.group + hh
                        wait(pe, max_ready, HG * st.s + hh - 1)
                        for u in range(2):
                            last = nc.tensor.matmul(s_bank[hh % 2][0:HALF, u, 0:TOKENS],
                                                    q_stack[st.q][:, head, head_cols(st, u)],
                                                    k_stack[st.q][:, head, head_cols(st)], start=True, stop=True)
                        last.then_inc(s_ready, 1)

            def scores_less_max(st):
                if st.there:
                    pe.wait_ge(max_rows_ready, st.s + 1)
                    for hh in range(HG):
                        head = HG * st.group + hh
                        wait(pe, probs_ready, HG * st.s + hh - 1)
                        for v in range(2):
                            out = t_bank[hh % 2][0:HALF, v, 0:TOKENS]
                            nc.tensor.matmul(out, k_stack[st.q][:, head, head_cols(st, v)],
                                             q_stack[st.q][:, head, head_cols(st)], start=True, stop=False)
                            last = nc.tensor.matmul(out, max_sel[:, hh, :],
                                                    max_rows[st.odd][:].rearrange("p u n -> p (u n)"),
                                                    start=False, stop=True)
                        last.then_inc(t_ready, 1)

            def mix(st):
                if st.there:
                    pe.wait_ge(probs_ready, HG * (st.s + 1))
                    if st.first:
                        pe.wait_ge(v_ready, PAIR * (st.pair + 1))
                    wait(pe, mixed_ready, st.s)
                    for v in range(2):
                        for hh in range(HG):
                            last = nc.tensor.matmul(o_bank[32 * hh:32 * hh + 32, 0:TOKENS],
                                                    v_buf[st.q][:, 2 * st.image + v, HG * st.group + hh, :],
                                                    probs[st.odd][:, hh, v, :], start=(v == 0), stop=(v == 1))
                    last.then_inc(o_ready, 1)

            def transpose_max(st):
                if st.there:
                    pe.wait_ge(max_parts_ready, st.s + 1)
                    wait(pe, att_ready, st.s - 2)
                    for u in range(2):
                        last = nc.tensor.transpose(max_tr[:, u, 0:HALF], max_parts[st.odd][:, u, :],
                                                   ident16[0:HALF, 0:HALF])
                    last.then_inc(max_tr_ready, 1)

            def step(body, kk):
                k = kk % STEPS
                transpose_back(Step(body, kk, -2))
                if kk == -1:
                    first = Pair(0, 0, 0)
                    project_patches(first, 0)
                    project_patches(first, 1)
                    transpose_xn(first)
                    project_v(first)
                    project_qk(first, 0)
                    project_qk(first, 1)
                    project_patches(Pair(0, 0, 1), 0)
                    project_patches(Pair(0, 0, 1), 1)
                scores(Step(body, kk, 1))
                scores_less_max(Step(body, kk, 0))
                mix(Step(body, kk, -1))
                if kk >= 0:
                    if k == 0:
                        transpose_xn(Pair(body, kk, 1))
                        project_v(Pair(body, kk, 1))
                    elif k in (1, 2):
                        project_qk(Pair(body, kk, 1), k - 1)
                    elif k in (4, 5):
                        project_patches(Pair(body, kk, 2), k - 4)
                transpose_max(Step(body, kk, 1))
            run_bodies(pe, step)

        @block.vector
        def _(dve):
            for i in range(2):
                nc.vector.memset(v_buf[i][:], 0.0).then_inc(consts_set, 1)
                nc.vector.memset(max_parts[i][:], 0.0).then_inc(consts_set, 1)
            nc.vector.memset(padded[:], 0.0).then_inc(consts_set, 1)
            nc.vector.memset(minus_half[:], -0.5).then_inc(consts_set, 1)
            nc.vector.memset(one_eps[:], 1.0 + EPS).then_inc(consts_set, 1)
            nc.vector.memset(eps_sq[:], EPS * EPS).then_inc(consts_set, 1)
            dve.wait_ge(consts_set, 8)
            for i in range(2):
                nc.vector.memset(v_buf[i][:, :, :, HEAD_DIM:HEAD_DIM + 1], 1.0).then_inc(consts_set, 1)
            dve.wait_ge(weights_in, 16 * len(LOADS))
            for hh in range(HG):
                nc.vector.tensor_copy(max_sel[:, hh, :], rowc[:, 2 + hh:3 + hh].to_broadcast([P, HALF])
                                      ).then_inc(consts_set, 1)
            nc.vector.tensor_scalar(bq_scaled[:], bqk[:, 0:GROUPS], rowc[:, 0:1], None, ALU.mult
                                    ).then_inc(consts_set, 1)
            nc.vector.tensor_copy(ident16[:], ident[:]).then_inc(consts_set, 1)
            def row_maxima(st):
                if st.there:
                    for hh in range(HG):
                        dve.wait_ge(s_ready, HG * st.s + hh + 1)
                        nc.vector.reduce_max(row_max[st.odd][:, :, hh:hh + 1], s_bank[hh % 2][0:HALF, :, 0:TOKENS],
                                             AX.X).then_inc(max_ready, 1)
                    dve.wait_ge(max_ready, HG * (st.s + 1))
                    wait(dve, max_tr_ready, st.s - 1)
                    parts = max_parts[st.odd][:].rearrange("p u (h r) -> p u h r", h=HG)
                    nc.vector.tensor_copy(parts[:, :, :, 0], row_max[st.odd][:]).then_inc(max_hi_ready, 1)
                    dve.wait_ge(max_hi_ready, st.s + 1)
                    nc.vector.tensor_tensor(parts[:, :, :, 1], row_max[st.odd][:], parts[:, :, :, 0], ALU.subtract
                                            ).then_inc(max_parts_ready, 1)

            def normalise(st):
                if st.there:
                    dve.wait_ge(back_ready, st.s + 1)
                    wait(dve, att_ready, st.s)
                    if st.first:
                        wait(dve, att_stored[st.q], 16 * st.before)
                    nc.vector.reciprocal(recip[:], back_tr[:, :, :, HEAD_DIM:HEAD_DIM + 1]).then_inc(recip_ready, 1)
                    dve.wait_ge(recip_ready, st.s + 1)
                    width = HG * HEAD_DIM
                    out = att[st.q][:, 2 * st.image:2 * st.image + 2, st.group * width:(st.group + 1) * width]
                    nc.vector.tensor_tensor(out.rearrange("p u (h d) -> p u h d", h=HG),
                                            back_tr[:, :, :, 0:HEAD_DIM],
                                            recip[:].to_broadcast([HALF, 2, HG, HEAD_DIM]), ALU.mult
                                            ).then_inc(att_ready, 1)

            def take_h(pr, half):
                if pr.there:
                    dve.wait_ge(p_ready[half], USES * pr.u + 1)
                    if half == 0:
                        wait(dve, h_stored, 16 * pr.u)
                        wait(dve, xn_ready, pr.u)
                    h2 = h_buf[:, 2 * half:2 * half + 2, :]
                    nc.vector.tensor_tensor(h2, p_bank[half][0:HALF, 0:2 * DIM].rearrange("p (c e) -> p c e", c=2),
                                            btok[:].unsqueeze(1).to_broadcast([HALF, 2, DIM]), ALU.add
                                            ).then_inc(h_ready, 1)
                    dve.wait_ge(h_ready, 2 * pr.u + half + 1)
                    for c in (2 * half, 2 * half + 1):
                        nc.vector.bn_stats(stats[:, c, :], h_buf[:, c, :]).then_inc(stats_ready, 1)
                    if half == 1:
                        dve.wait_ge(stats_ready, TILES * (pr.u + 1))
                        wait(dve, rstd_ready, pr.u)
                        nc.vector.memset(spacer[:], 0.0)
                        for c in range(TILES):
                            nc.vector.bn_aggr(meanvar[:, c, :], stats[:, c, :]).then_inc(meanvar_ready, 1)

            def layernorm(pr):
                if pr.there:
                    dve.wait_ge(rstd_ready, pr.u + 1)
                    wait(dve, xt_b_ready, pr.u)
                    for c in range(TILES):
                        ins = nc.vector.tensor_scalar(xn[:, c, :], h_buf[:, c, :], meanvar[:, c, 0:1], rstd[:, c:c + 1],
                                                      ALU.subtract, ALU.mult)
                    ins.then_inc(xn_ready, 1)

            def take_xt_a(pr):
                if pr.there:
                    dve.wait_ge(p_ready[0], USES * pr.u + 2)
                    nc.vector.tensor_scalar(xt_a[:], p_bank[0][:, 0:COLS], lnc[:, 0:1], lnc[:, 1:2], ALU.mult, ALU.add
                                            ).then_inc(xt_a_ready, 1)

            def take_v(pr):
                if pr.there:
                    wait(dve, o_ready, STEPS * (pr.u - 1))
                    for im in range(PAIR):
                        dve.wait_ge(p_ready[im], USES * pr.u + 3)
                        out = v_buf[pr.q][:, 2 * im:2 * im + 2, :, 0:HEAD_DIM]
                        nc.vector.tensor_tensor(
                            out, p_bank[im][0:HALF, 0:2 * DIM].rearrange("p (c h d) -> p c h d", c=2, h=HEADS),
                            bv[:].rearrange("p (h d) -> p h d", h=HEADS).unsqueeze(1)
                            .to_broadcast([HALF, 2, HEADS, HEAD_DIM]), ALU.add).then_inc(v_ready, 1)

            def add_tilde(pr, which):
                if pr.there:
                    tiles = slice(which * GROUPS * PAIR, (which + 1) * GROUPS * PAIR)
                    dve.wait_ge(beside_ready, 2 * pr.u + which + 1)
                    wait(dve, lo_ready, 2 * pr.u + which - 1)
                    nc.vector.scalar_tensor_tensor(qk[:, tiles, :], beside[:, tiles, :], rowc[:, 1:2],
                                                   padded[:, tiles, 1:TOKENS + 1], ALU.mult, ALU.add
                                                   ).then_inc(qk_ready, 1)

            def step(body, kk):
                k = kk % STEPS
                if kk == -1:
                    first, second = Pair(0, 0, 0), Pair(0, 0, 1)
                    take_h(first, 0)
                    take_h(first, 1)
                    layernorm(first)
                    take_xt_a(first)
                    take_v(first)
                    add_tilde(first, 0)
                    add_tilde(first, 1)
                    take_h(second, 0)
                    take_h(second, 1)
                row_maxima(Step(body, kk, 1))
                if kk >= 0 and k == 0:
                    layernorm(Pair(body, kk, 1))
                normalise(Step(body, kk, -2))
                if kk >= 0:
                    if k == 0:
                        take_xt_a(Pair(body, kk, 1))
                        take_v(Pair(body, kk, 1))
                    elif k in (2, 3):
                        add_tilde(Pair(body, kk, 1), k - 2)
                    elif k in (4, 5):
                        take_h(Pair(body, kk, 2), k - 4)
            run_bodies(dve, step)

        @block.scalar
        def _(act):
            act.wait_ge(weights_in, 16 * len(LOADS))
            act.wait_ge(consts_set, CONSTS)

            def exponentials(st):
                if st.there:
                    wait(act, o_ready, st.s - 1)
                    for hh in range(HG):
                        act.wait_ge(t_ready, HG * st.s + hh + 1)
                        nc.scalar.activation(probs[st.odd][:, hh], t_bank[hh % 2][0:HALF, :, 0:TOKENS], ACT.Exp
                                             ).then_inc(probs_ready, 1)

            def copy_mixed(st):
                if st.there:
                    act.wait_ge(o_ready, st.s + 1)
                    wait(act, back_ready, st.s - 1)
                    nc.scalar.copy(mixed[st.odd][:], o_bank[:, 0:TOKENS]).then_inc(mixed_ready, 1)

            def copy_max_rows(st):
                if st.there:
                    act.wait_ge(max_tr_ready, st.s + 1)
                    wait(act, t_ready, HG * (st.s - 1))
                    nc.scalar.copy(max_rows[st.odd][:], max_tr[:, :, 0:HALF]).then_inc(max_rows_ready, 1)

            def take_xt_b(pr):
                if pr.there:
                    act.wait_ge(p_ready[1], USES * pr.u + 2)
                    nc.scalar.activation(xt_b[:], p_bank[1][0:HI, 0:COLS], ACT.Identity, bias=lnc[0:HI, 3:4],
                                         scale=lnc[0:HI, 2:3]).then_inc(xt_b_ready, 1)

            def take_qk(pr, which):
                if pr.there:
                    wait(act, qk_ready, 2 * pr.u + which - 1)
                    for i in range(which * GROUPS, (which + 1) * GROUPS):
                        n = 4 + i
                        act.wait_ge(p_ready[n % 2], USES * pr.u + 2 + n // 2)
                        out = padded[:, PAIR * i:PAIR * (i + 1), 1:TOKENS + 1]
                        src = p_bank[n % 2][:, 0:COLS].rearrange("p (i n) -> p i n", i=PAIR)
                        if which == 0:
                            ins = nc.scalar.activation(out, src, ACT.Identity, bias=bq_scaled[:, i:i + 1],
                                                       scale=rowc[:, 0:1])
                        else:
                            ins = nc.scalar.activation(out, src, ACT.Identity, bias=bqk[:, i:i + 1])
                        ins.then_inc(padded_ready, 1)

            def take_high(pr, which):
                if pr.there:
                    tiles = slice(which * GROUPS * PAIR, (which + 1) * GROUPS * PAIR)
                    act.wait_ge(qk_ready, 2 * pr.u + which + 1)
                    wait(act, (q_stacked, k_stacked)[which], STACKED * pr.u)
                    nc.scalar.copy(qk_hi[:, tiles, :], qk[:, tiles, :]).then_inc(hi_ready, 1)

            def step(body, kk):
                k = kk % STEPS
                if kk == -1:
                    first = Pair(0, 0, 0)
                    take_xt_b(first)
                    take_qk(first, 0)
                    take_qk(first, 1)
                    take_high(first, 0)
                    take_high(first, 1)
                exponentials(Step(body, kk, 0))
                copy_mixed(Step(body, kk, -1))
                if kk >= 0:
                    if k == 0:
                        take_xt_b(Pair(body, kk, 1))
                    elif k in (1, 2):
                        take_qk(Pair(body, kk, 1), k - 1)
                copy_max_rows(Step(body, kk, 1))
                if kk >= 0 and k in (2, 3):
                    take_high(Pair(body, kk, 1), k - 2)
            run_bodies(act, step)

        @block.gpsimd
        def _(pool):
            pool.wait_ge(consts_set, CONSTS)

            def inverse_deviation(pr):
                if pr.there:
                    pool.wait_ge(meanvar_ready, TILES * (pr.u + 1))
                    wait(pool, rstd_ready, pr.u)
                    nc.gpsimd.tensor_tensor(var_eps[0][:], meanvar[:, :, 1], one_eps[:], ALU.mult
                                            ).then_inc(var_ready, 1)
                    pool.wait_ge(var_ready, 2 * pr.u + 1)
                    nc.gpsimd.tensor_tensor(var_eps[1][:], var_eps[0][:], eps_sq[:], ALU.add).then_inc(var_ready, 1)
                    pool.wait_ge(var_ready, 2 * pr.u + 2)
                    wait(pool, xn_ready, pr.u)
                    nc.gpsimd.tensor_tensor(rstd[:], var_eps[1][:], minus_half[:], ALU.pow).then_inc(rstd_ready, 1)

            def add_beside(pr, which):
                if pr.there:
                    tiles = slice(which * GROUPS * PAIR, (which + 1) * GROUPS * PAIR)
                    pool.wait_ge(padded_ready, 2 * GROUPS * pr.u + GROUPS * (which + 1))
                    wait(pool, qk_ready, 2 * pr.u + which - 1)
                    nc.gpsimd.tensor_tensor(beside[:, tiles, :], padded[:, tiles, 0:TOKENS], padded[:, tiles, 2:PW],
                                            ALU.add).then_inc(beside_ready, 1)

            def take_low(pr, which):
                if pr.there:
                    tiles = slice(which * GROUPS * PAIR, (which + 1) * GROUPS * PAIR)
                    pool.wait_ge(hi_ready, 2 * pr.u + which + 1)
                    wait(pool, (q_stacked, k_stacked)[which], STACKED * pr.u)
                    nc.gpsimd.tensor_tensor(qk_lo[:, tiles, :], qk[:, tiles, :], qk_hi[:, tiles, :], ALU.subtract
                                            ).then_inc(lo_ready, 1)

            def step(body, kk):
                k = kk % STEPS
                if kk == -1:
                    first = Pair(0, 0, 0)
                    inverse_deviation(first)
                    add_beside(first, 0)
                    add_beside(first, 1)
                    take_low(first, 0)
                    take_low(first, 1)
                    inverse_deviation(Pair(0, 0, 1))
                elif k in (1, 2):
                    add_beside(Pair(body, kk, 1), k - 1)
                elif k == 3:
                    take_low(Pair(body, kk, 1), 0)
                    take_low(Pair(body, kk, 1), 1)
                elif k == 5:
                    inverse_deviation(Pair(body, kk, 2))
            run_bodies(pool, step)


def expert_phase(nc, h_dram, att_dram, w1_a, w1_b, w2, b1, wr1_a, wr1_b, br1, wr2_a, wr2_b, br2, b2, expert_ids,
                 ident_in, b1_parts, out):
    ctx = ExitStack()
    with ctx:
        def sb(name, shape, dt=F32):
            return ctx.enter_context(nc.sbuf_tensor(name, shape, dt))

        def ps(name, shape, dt=F32):
            return ctx.enter_context(nc.psum_tensor(name, shape, dt))

        def sem(name):
            return ctx.enter_context(nc.semaphore(name))

        w1h_a = sb("w1h_a", [P, EXPERTS, HIDDEN], BF16)
        w1l_a = sb("w1l_a", [P, EXPERTS, HIDDEN], BF16)
        w1h_b = sb("w1h_b", [P, EXPERTS, HIDDEN], BF16)
        w1l_b = sb("w1l_b", [HI + 3, EXPERTS, HIDDEN], BF16)
        w2h = sb("w2h", [P, EXPERTS, FCH, DIM], BF16)
        w2l = sb("w2l", [P, EXPERTS, FCH, DIM], BF16)
        stage_a = [sb(f"stage_a{i}", [P, HIDDEN]) for i in range(2)]
        stage_b = [sb(f"stage_b{i}", [P, HIDDEN]) for i in range(2)]
        stage_2 = [sb(f"stage_2{i}", [P, FCH, DIM]) for i in range(2)]
        b1_rows = sb("b1_rows", [EXPERTS * FCH, P])
        b1_rest = [sb(f"b1_rest{i}", [EXPERTS * FCH, P]) for i in range(2)]
        b1_split = sb("b1_split", [EXPERTS * FCH, 3, P], BF16)
        r1_a = sb("r1_a", [P, DIM])
        r1_b = sb("r1_b", [HI, DIM])
        r1_bias = sb("r1_bias", [P, 2])
        r2_a = sb("r2_a", [P, EXPERTS])
        r2_b = sb("r2_b", [HI, EXPERTS])
        r2_bias = sb("r2_bias", [P, GTILES, EXPERTS])
        b2_sb = sb("b2_sb", [EXPERTS, DIM])
        ids = sb("ids", [P, EXPERTS])
        ident = sb("ident2", [P, P])
        minus_half = sb("minus_half2", [P, GTILES])
        eps = sb("eps", [P, GTILES])
        spacer = sb("spacer2", [P, 1])

        h_in = [sb(f"h_in{i}", [P, GTILES, DIM]) for i in range(2)]
        a_in = [sb(f"a_in{i}", [P, GTILES, DIM]) for i in range(2)]
        y_buf = [sb(f"y_buf{i}", [P, GTILES, DIM]) for i in range(2)]
        stats = sb("stats2", [P, GTILES, 6])
        meanvar = sb("meanvar2", [P, GTILES, 2])
        var_eps = sb("var_eps2", [P, GTILES])
        rstd = sb("rstd2", [P, GTILES])
        xn = sb("xn2", [P, GTILES, 2, P])
        xt = sb("xt2", [P, 2, GT])
        xh = [sb(f"xh{i}", [P, 2, GT], BF16) for i in range(2)]
        xl = [sb(f"xl{i}", [P, GT], BF16) for i in range(2)]
        xe = [sb(f"xe{i}", [HI + 3, GT], BF16) for i in range(2)]
        rh = sb("rh", [P, 2, GT])
        score = sb("score", [P, GTILES, EXPERTS])
        best = sb("best", [P, GTILES, 1])
        top = sb("top", [P, GTILES, 8])
        top_at = sb("top_at", [P, GTILES, 8], U32)
        top_id = sb("top_id", [P, GTILES, 8])
        chosen = sb("chosen", [P, GTILES, EXPERTS])
        less_top = sb("less_top", [P, GTILES, EXPERTS])
        expd = sb("expd", [P, GTILES, EXPERTS])
        kept = sb("kept", [P, GTILES, EXPERTS])
        total = sb("total", [P, GTILES, 1])
        share = sb("share", [P, GTILES, 1])
        gate = [sb(f"gate{i}", [P, GTILES, EXPERTS]) for i in range(2)]
        gate_t = sb("gate_t", [EXPERTS, GT])
        mh = [sb(f"mh{i}", [P, 2, GT], BF16) for i in range(MID)]
        ml = [sb(f"ml{i}", [P, 2, GT], BF16) for i in range(MID)]
        acc = [sb(f"acc{i}", [P, GTILES, DIM]) for i in range(2)]

        mid_bank = [ps(f"mid_bank{i}", [P, 2, GT]) for i in range(MID)]
        y_bank = [ps(f"y_bank{i}", [P, GTILES, 256]) for i in range(2)]
        x_bank = ps("x_bank", [P, 2, GT])
        r_bank = ps("r_bank", [P, 2, GT])

        small_in = sem("small_in")
        b1_in = sem("b1_in")
        b1_parts_ready = sem("b1_parts_ready")
        b1_parts_stored = sem("b1_parts_stored")
        bias_in = sem("bias_in")
        stage_in = [sem(f"stage_in{i}") for i in range(2)]
        w_hi_ready = sem("w_hi_ready")
        w_lo_ready = sem("w_lo_ready")
        consts_set = sem("consts_set2")
        rows_in = [sem(f"rows_in{i}") for i in range(2)]
        y_ready = sem("y_ready")
        stats_ready = sem("stats_ready2")
        meanvar_ready = sem("meanvar_ready2")
        var_ready = sem("var_ready2")
        rstd_ready = sem("rstd_ready2")
        xn_ready = sem("xn_ready2")
        xt_ps_ready = sem("xt_ps_ready")
        xt_ready = sem("xt_ready")
        xh_ready = sem("xh_ready")
        xl_ready = sem("xl_ready")
        r1_ready = sem("r1_ready")
        rh_ready = sem("rh_ready")
        score_ps_ready = sem("score_ps_ready")
        routed = sem("routed")
        expd_ready = sem("expd_ready")
        gate_ready = sem("gate_ready")
        gate_ps_ready = sem("gate_ps_ready")
        gate_t_ready = sem("gate_t_ready")
        mid_ready = sem("mid_ready")
        mh_ready = sem("mh_ready")
        ml_ready = sem("ml_ready")
        mixed_in = sem("mixed_in")
        ye_ready = sem("ye_ready")
        ye_taken = sem("ye_taken")
        out_stored = [sem(f"out_stored{i}") for i in range(2)]

        SMALL = [(r1_a, wr1_a), (r1_b, wr1_b), (r1_bias, br1), (r2_a, wr2_a), (r2_b, wr2_b), (r2_bias, br2), (b2_sb, b2),
                 (ids, expert_ids), (ident, ident_in)]
        YU = 1 + EXPERTS
        ROUTE_OPS = 12
        CONSTS = 4

        block = ctx.enter_context(nc.Block())

        def run_groups(eng, group):
            for q in range(2):
                group(0, q)
            with eng.Fori(1, FGROUPS // 2) as body:
                for q in range(2):
                    group(body, q)
            group(FGROUPS // 2, 0)

        def in_range(g):
            return not isinstance(g, int) or g < FGROUPS

        def rows(dram, g):
            return dram[bass.ds(g, 1)].rearrange("o (p j) e -> p (o j) e", p=P)

        @block.sync
        def _(sp):
            sp.dma_start(b1_rows[:], b1).then_inc(b1_in, 16)
            for dst, src in SMALL:
                sp.dma_start(dst[:], src).then_inc(small_in, 16)

            def load_rows(body, q):
                g = 2 * body + q
                if in_range(g):
                    wait(sp, y_ready, g - 1)
                    sp.dma_start(h_in[q][:], rows(h_dram, g)).then_inc(rows_in[q], 16)
                    sp.dma_start(a_in[q][:], rows(att_dram, g)).then_inc(rows_in[q], 16)

            def load_expert(e):
                if e >= 2:
                    sp.wait_ge(w_lo_ready, 3 * (e - 1))
                i = e % 2
                sp.dma_start(stage_a[i][:], w1_a[:, e]).then_inc(stage_in[i], 16)
                sp.dma_start(stage_b[i][:], w1_b[:, e]).then_inc(stage_in[i], 16)
                sp.dma_start(stage_2[i][:], w2[:, e]).then_inc(stage_in[i], 16)

            load_expert(0)
            load_expert(1)
            sp.wait_ge(b1_parts_ready, 5)
            sp.dma_start(b1_parts.rearrange("r (c f) -> c r f", f=P), b1_split[:]).then_inc(b1_parts_stored, 16)
            sp.wait_ge(b1_parts_stored, 16)
            sp.dma_start(w1l_b[HI:HI + 3].rearrange("r e f -> r (e f)"), b1_parts).then_inc(bias_in, 16)
            load_rows(0, 0)
            load_rows(0, 1)
            for e in range(2, EXPERTS):
                load_expert(e)

            def group(body, q):
                g = 2 * body + q
                if not isinstance(g, int) or g > 0:
                    load_rows(body + q, 1 - q)
                sp.wait_ge(ye_taken, YU * (g + 1))
                sp.dma_start(rows(out, g), acc[q][:]).then_inc(out_stored[q], 16)
            run_groups(sp, group)
            sp.wait_ge(out_stored[0], 16 * ((FGROUPS + 1) // 2))
            sp.wait_ge(out_stored[1], 16 * (FGROUPS // 2))

        @block.tensor
        def _(pe):
            pe.wait_ge(small_in, 16 * len(SMALL))
            pe.wait_ge(bias_in, 16)

            def transpose_x(body, q):
                g = 2 * body + q
                if in_range(g):
                    pe.wait_ge(xn_ready, g + 1)
                    wait(pe, routed, ROUTE_OPS * (g - 1) + 1)
                    for b in range(2):
                        for j in range(GTILES):
                            last = nc.tensor.transpose(x_bank[:, b, j * P:(j + 1) * P], xn[:, j, b, :], ident[:])
                    last.then_inc(xt_ps_ready, 1)

            def router_hidden(body, q):
                g = 2 * body + q
                if in_range(g):
                    pe.wait_ge(xt_ready, g + 1)
                    wait(pe, gate_t_ready, g)
                    for b, (f0, nf) in enumerate(((0, P), (P, HI))):
                        nc.tensor.matmul(r_bank[0:nf, b, :], r1_a[:, f0:f0 + nf], xt[:, 0, :], start=True, stop=False)
                        last = nc.tensor.matmul(r_bank[0:nf, b, :], r1_b[:, f0:f0 + nf], xt[0:HI, 1, :], start=False,
                                                stop=True)
                    last.then_inc(r1_ready, 1)

            def router_scores(body, q):
                g = 2 * body + q
                if in_range(g):
                    pe.wait_ge(rh_ready, 2 * (g + 1))
                    pe.wait_ge(xh_ready, 3 * (g + 1))
                    for j in range(GTILES):
                        cols = slice(j * P, (j + 1) * P)
                        nc.tensor.matmul(x_bank[:, 0, j * 8:(j + 1) * 8], rh[:, 0, cols], r2_a[:], start=True,
                                         stop=False)
                        last = nc.tensor.matmul(x_bank[:, 0, j * 8:(j + 1) * 8], rh[0:HI, 1, cols], r2_b[:],
                                                start=False, stop=True)
                    last.then_inc(score_ps_ready, 1)

            def transpose_gates(body, q):
                g = 2 * body + q
                if in_range(g):
                    pe.wait_ge(gate_ready, g + 1)
                    for j in range(GTILES):
                        last = nc.tensor.transpose(r_bank[0:EXPERTS, 0, j * P:(j + 1) * P], gate[q][:, j, :], ident[:])
                    last.then_inc(gate_ps_ready, 1)

            def gated_bias(g, q):
                pe.wait_ge(gate_t_ready, g + 1)
                use, bank = YU * g, y_bank[q * YU % 2]
                wait(pe, ye_taken, use - 1)
                for j in range(GTILES):
                    last = nc.tensor.matmul(bank[:, j, 0:DIM], gate_t[:, j * P:(j + 1) * P], b2_sb[:], start=True,
                                            stop=True)
                last.then_inc(ye_ready, 1)

            def hidden(g, q, n):
                e, c0 = n // UNITS, 2 * (n % UNITS)
                if n % UNITS == 0:
                    pe.wait_ge(w_hi_ready, 3 * (e + 1))
                    pe.wait_ge(w_lo_ready, 3 * (e + 1))
                if n == 0:
                    pe.wait_ge(xl_ready, 2 * (g + 1))
                    pe.wait_ge(xh_ready, 3 * (g + 1))
                wait(pe, ml_ready, EU * g + n - MID + 1)
                for c in range(2):
                    f = slice((c0 + c) * P, (c0 + c + 1) * P)
                    o = mid_bank[n % MID][:, c, :]
                    nc.tensor.matmul(o, w1h_a[:, e, f], xh[q][:, 0, :], start=True, stop=False)
                    nc.tensor.matmul(o, w1h_a[:, e, f], xl[q][:], start=False, stop=False)
                    nc.tensor.matmul(o, w1l_a[:, e, f], xh[q][:, 0, :], start=False, stop=False)
                    nc.tensor.matmul(o, w1h_b[:, e, f], xh[q][:, 1, :], start=False, stop=False)
                    last = nc.tensor.matmul(o, w1l_b[:, e, f], xe[q][:], start=False, stop=True)
                last.then_inc(mid_ready, 1)

            def project(g, q, n):
                e, c0 = n // UNITS, 2 * (n % UNITS)
                use, bank = YU * g + 1 + e, y_bank[(q * YU + 1 + e) % 2]
                pe.wait_ge(ml_ready, EU * g + n + 1)
                if n % UNITS == 0:
                    wait(pe, ye_taken, use - 1)
                for j in range(GTILES):
                    cols = slice(j * P, (j + 1) * P)
                    for c in range(2):
                        first = n % UNITS == 0 and c == 0 and j == 0
                        end = n % UNITS == UNITS - 1 and c == 1
                        o = bank[:, j, 0:DIM]
                        nc.tensor.matmul(o, mh[n % MID][:, c, cols], w2h[:, e, c0 + c, :], start=first, stop=False,
                                         skip_group_check=True)
                        nc.tensor.matmul(o, mh[n % MID][:, c, cols], w2l[:, e, c0 + c, :], start=False, stop=False,
                                         skip_group_check=True)
                        last = nc.tensor.matmul(o, ml[n % MID][:, c, cols], w2h[:, e, c0 + c, :], start=False,
                                                stop=end, skip_group_check=True)
                last.then_inc(mixed_in, 1)
                if n % UNITS == UNITS - 1:
                    pe.wait_ge(mixed_in, EU * g + n + 1)
                    pe.sem_inc(ye_ready, 1)

            def group(body, q):
                g = 2 * body + q
                nxt = (body + q, 1 - q)
                gated_bias(g, q)
                for n in range(EU):
                    if n == 7:
                        transpose_x(*nxt)
                    elif n == 10:
                        router_hidden(*nxt)
                    elif n == 13:
                        router_scores(*nxt)
                    elif n == 19:
                        transpose_gates(*nxt)
                    hidden(g, q, n)
                    if n >= LAG:
                        project(g, q, n - LAG)
                for n in range(EU - LAG, EU):
                    project(g, q, n)

            transpose_x(0, 0)
            router_hidden(0, 0)
            router_scores(0, 0)
            transpose_gates(0, 0)
            run_groups(pe, group)

        @block.vector
        def _(dve):
            def b1_split_op(ins, n):
                ins.then_inc(b1_parts_ready, 1)
                dve.wait_ge(b1_parts_ready, n)

            dve.wait_ge(b1_in, 16)
            b1_split_op(nc.vector.tensor_copy(b1_split[:, 0], b1_rows[:]), 1)
            b1_split_op(nc.vector.tensor_tensor(b1_rest[0][:], b1_rows[:], b1_split[:, 0], ALU.subtract), 2)
            b1_split_op(nc.vector.tensor_copy(b1_split[:, 1], b1_rest[0][:]), 3)
            b1_split_op(nc.vector.tensor_tensor(b1_rest[1][:], b1_rest[0][:], b1_split[:, 1], ALU.subtract), 4)
            b1_split_op(nc.vector.tensor_copy(b1_split[:, 2], b1_rest[1][:]), 5)
            for i in range(2):
                nc.vector.memset(xe[i][HI:HI + 3, :], 1.0).then_inc(consts_set, 1)
            nc.vector.memset(minus_half[:], -0.5).then_inc(consts_set, 1)
            nc.vector.memset(eps[:], EPS).then_inc(consts_set, 1)

            def split_low(e):
                i = e % 2
                dve.wait_ge(w_hi_ready, 3 * (e + 1))
                nc.vector.tensor_tensor(w1l_a[:, e], stage_a[i][:], w1h_a[:, e], ALU.subtract).then_inc(w_lo_ready, 1)
                nc.vector.tensor_tensor(w1l_b[0:HI, e], stage_b[i][0:HI], w1h_b[0:HI, e], ALU.subtract
                                        ).then_inc(w_lo_ready, 1)
                nc.vector.tensor_tensor(w2l[:, e], stage_2[i][:], w2h[:, e], ALU.subtract).then_inc(w_lo_ready, 1)

            def statistics(body, q):
                g = 2 * body + q
                if in_range(g):
                    dve.wait_ge(y_ready, g + 1)
                    for j in range(GTILES):
                        nc.vector.bn_stats(stats[:, j, :], y_buf[q][:, j, :]).then_inc(stats_ready, 1)
                    dve.wait_ge(stats_ready, GTILES * (g + 1))
                    wait(dve, rstd_ready, g)
                    nc.vector.memset(spacer[:], 0.0)
                    for j in range(GTILES):
                        nc.vector.bn_aggr(meanvar[:, j, :], stats[:, j, :]).then_inc(meanvar_ready, 1)

            def layernorm(body, q):
                g = 2 * body + q
                if in_range(g):
                    dve.wait_ge(rstd_ready, g + 1)
                    wait(dve, xt_ps_ready, g)
                    for j in range(GTILES):
                        for b, f0, c0, nf in ((0, 0, 0, P), (1, P, 0, HI), (1, P, HI, HI)):
                            last = nc.vector.tensor_scalar(xn[:, j, b, c0:c0 + nf], y_buf[q][:, j, f0:f0 + nf],
                                                           meanvar[:, j, 0:1], rstd[:, j:j + 1],
                                                           ALU.subtract, ALU.mult)
                    last.then_inc(xn_ready, 1)

            def split_x(body, q):
                g = 2 * body + q
                if in_range(g):
                    dve.wait_ge(xt_ready, g + 1)
                    dve.wait_ge(xh_ready, 3 * (g + 1))
                    wait(dve, mid_ready, EU * (g - 1))
                    nc.vector.tensor_tensor(xl[q][:], xt[:, 0, :], xh[q][:, 0, :], ALU.subtract).then_inc(xl_ready, 1)
                    low = xh[q][HI:P, 1, :]
                    nc.vector.tensor_tensor(low, xt[HI:P, 1, :], low, ALU.subtract).then_inc(xl_ready, 1)

            def route(body, q):
                g = 2 * body + q
                if in_range(g):
                    dve.wait_ge(score_ps_ready, g + 1)
                    nc.vector.tensor_tensor(score[:], x_bank[:, 0, 0:GTILES * 8].rearrange(
                        "p (j e) -> p j e", j=GTILES), r2_bias[:], ALU.add).then_inc(routed, 1)
                    dve.wait_ge(routed, ROUTE_OPS * g + 1)
                    nc.vector.reduce_max(best[:], score[:], AX.X).then_inc(routed, 1)
                    for j in range(GTILES):
                        nc.vector.max(top[:, j, :], score[:, j, :]).then_inc(routed, 1)
                    dve.wait_ge(routed, ROUTE_OPS * g + 4)
                    wait(dve, expd_ready, 4 * g)
                    nc.vector.tensor_tensor(less_top[:], score[:], best[:].to_broadcast([P, GTILES, EXPERTS]),
                                            ALU.subtract).then_inc(routed, 1)
                    for j in range(GTILES):
                        nc.vector.max_index(top_at[:, j, :], top[:, j, :], score[:, j, :]).then_inc(routed, 1)
                    dve.wait_ge(routed, ROUTE_OPS * g + 7)
                    nc.vector.tensor_copy(top_id[:], top_at[:]).then_inc(routed, 1)
                    dve.wait_ge(routed, ROUTE_OPS * g + 8)
                    for j in range(GTILES):
                        nc.vector.tensor_scalar(chosen[:, j, :], ids[:], top_id[:, j, 0:1], None, ALU.is_equal
                                                ).then_inc(routed, 1)
                    dve.wait_ge(routed, ROUTE_OPS * g + 10)
                    for j in range(GTILES):
                        nc.vector.scalar_tensor_tensor(chosen[:, j, :], ids[:], top_id[:, j, 1:2], chosen[:, j, :],
                                                       ALU.is_equal, ALU.add).then_inc(routed, 1)

            def gates(body, q):
                g = 2 * body + q
                if in_range(g):
                    dve.wait_ge(expd_ready, 4 * g + 1)
                    dve.wait_ge(routed, ROUTE_OPS * (g + 1))
                    nc.vector.tensor_tensor(kept[:], expd[:], chosen[:], ALU.mult).then_inc(expd_ready, 1)
                    dve.wait_ge(expd_ready, 4 * g + 2)
                    nc.vector.reduce_sum(total[:], kept[:], AX.X).then_inc(expd_ready, 1)
                    dve.wait_ge(expd_ready, 4 * g + 3)
                    nc.vector.reciprocal(share[:], total[:]).then_inc(expd_ready, 1)
                    dve.wait_ge(expd_ready, 4 * g + 4)
                    nc.vector.tensor_tensor(gate[q][:], kept[:], share[:].to_broadcast([P, GTILES, EXPERTS]),
                                            ALU.mult).then_inc(gate_ready, 1)

            def take_bias(g, q, body):
                dve.wait_ge(ye_ready, YU * g + 1)
                wait(dve, ye_taken, YU * g)
                wait(dve, out_stored[q], 16 * body)
                nc.vector.tensor_tensor(acc[q][:], y_bank[q * YU % 2][:, :, 0:DIM], y_buf[q][:], ALU.add
                                        ).then_inc(ye_taken, 1)

            def take_expert(g, q, e):
                dve.wait_ge(ye_ready, YU * g + 2 + e)
                dve.wait_ge(ye_taken, YU * g + 1 + e)
                for j in range(GTILES):
                    last = nc.vector.scalar_tensor_tensor(acc[q][:, j, :], y_bank[(q * YU + 1 + e) % 2][:, j, 0:DIM],
                                                          gate[q][:, j, e:e + 1], acc[q][:, j, :], ALU.mult, ALU.add)
                last.then_inc(ye_taken, 1)

            def take_low(g, n):
                dve.wait_ge(mh_ready, EU * g + n + 1)
                wait(dve, mixed_in, EU * g + n - MID + 1)
                nc.vector.scalar_tensor_tensor(ml[n % MID][:], mid_bank[n % MID][:], 0.0, mh[n % MID][:],
                                               ALU.max, ALU.subtract).then_inc(ml_ready, 1)

            def group(body, q):
                g = 2 * body + q
                nxt = (body + q, 1 - q)
                take_bias(g, q, body)
                for n in range(EU):
                    if isinstance(g, int) and g == 0 and n % UNITS == 0:
                        split_low(n // UNITS)
                    take_low(g, n)
                    e = (n - LAG - UNITS + 1) // UNITS
                    if n >= LAG + UNITS and (n - LAG) % UNITS == 0:
                        take_expert(g, q, e)
                    if n == 2:
                        statistics(*nxt)
                    elif n == 4:
                        layernorm(*nxt)
                    elif n == 8:
                        split_x(*nxt)
                    elif n == 13:
                        route(*nxt)
                    elif n == 16:
                        gates(*nxt)
                take_expert(g, q, EXPERTS - 1)

            dve.wait_ge(small_in, 16 * len(SMALL))
            statistics(0, 0)
            layernorm(0, 0)
            split_x(0, 0)
            route(0, 0)
            gates(0, 0)
            run_groups(dve, group)

        @block.scalar
        def _(act):
            act.wait_ge(small_in, 16 * len(SMALL))

            def split_high(e):
                i = e % 2
                act.wait_ge(stage_in[i], 48 * (e // 2 + 1))
                nc.scalar.copy(w1h_a[:, e], stage_a[i][:]).then_inc(w_hi_ready, 1)
                nc.scalar.copy(w1h_b[:, e], stage_b[i][:]).then_inc(w_hi_ready, 1)
                nc.scalar.copy(w2h[:, e], stage_2[i][:]).then_inc(w_hi_ready, 1)

            def take_xt(body, q):
                g = 2 * body + q
                if in_range(g):
                    act.wait_ge(xt_ps_ready, g + 1)
                    wait(act, r1_ready, g)
                    wait(act, xl_ready, 2 * g)
                    nc.scalar.copy(xt[:], x_bank[:]).then_inc(xt_ready, 1)
                    wait(act, mid_ready, EU * (g - 1))
                    for b in range(2):
                        nc.scalar.copy(xh[q][:, b, :], x_bank[:, b, :]).then_inc(xh_ready, 1)
                    nc.scalar.copy(xe[q][0:HI, :], x_bank[0:HI, 1, :]).then_inc(xh_ready, 1)

            def router_relu(body, q):
                g = 2 * body + q
                if in_range(g):
                    act.wait_ge(r1_ready, g + 1)
                    wait(act, score_ps_ready, g)
                    for b, nf in enumerate((P, HI)):
                        nc.scalar.activation(rh[0:nf, b, :], r_bank[0:nf, b, :], ACT.Relu, bias=r1_bias[0:nf, b:b + 1]
                                             ).then_inc(rh_ready, 1)

            def exponentials(body, q):
                g = 2 * body + q
                if in_range(g):
                    act.wait_ge(routed, ROUTE_OPS * g + 5)
                    nc.scalar.activation(expd[:], less_top[:], ACT.Exp).then_inc(expd_ready, 1)

            def take_gates(body, q):
                g = 2 * body + q
                if in_range(g):
                    act.wait_ge(gate_ps_ready, g + 1)
                    wait(act, ye_ready, YU * (g - 1) + 1)
                    nc.scalar.copy(gate_t[:], r_bank[0:EXPERTS, 0, :]).then_inc(gate_t_ready, 1)

            def take_high(g, n):
                act.wait_ge(mid_ready, EU * g + n + 1)
                wait(act, mixed_in, EU * g + n - MID + 1)
                nc.scalar.activation(mh[n % MID][:], mid_bank[n % MID][:], ACT.Relu).then_inc(mh_ready, 1)

            def group(body, q):
                g = 2 * body + q
                nxt = (body + q, 1 - q)
                for n in range(EU):
                    if isinstance(g, int) and g == 0 and n % UNITS == 0 and n // UNITS + 2 < EXPERTS:
                        split_high(n // UNITS + 2)
                    take_high(g, n)
                    if n == 6:
                        take_xt(*nxt)
                    elif n == 10:
                        router_relu(*nxt)
                    elif n == 14:
                        exponentials(*nxt)
                    elif n == 19:
                        take_gates(*nxt)

            split_high(0)
            split_high(1)
            take_xt(0, 0)
            router_relu(0, 0)
            exponentials(0, 0)
            take_gates(0, 0)
            run_groups(act, group)

        @block.gpsimd
        def _(pool):
            pool.wait_ge(consts_set, CONSTS)

            def sum_rows(body, q):
                g = 2 * body + q
                if in_range(g):
                    pool.wait_ge(rows_in[q], 32 * (body + 1))
                    wait(pool, ye_taken, YU * (g - 2) + 1)
                    nc.gpsimd.tensor_tensor(y_buf[q][:], h_in[q][:], a_in[q][:], ALU.add).then_inc(y_ready, 1)

            def inverse_deviation(body, q):
                g = 2 * body + q
                if in_range(g):
                    pool.wait_ge(meanvar_ready, GTILES * (g + 1))
                    nc.gpsimd.tensor_tensor(var_eps[:], meanvar[:, :, 1], eps[:], ALU.add).then_inc(var_ready, 1)
                    pool.wait_ge(var_ready, g + 1)
                    wait(pool, xn_ready, g)
                    nc.gpsimd.tensor_tensor(rstd[:], var_eps[:], minus_half[:], ALU.pow).then_inc(rstd_ready, 1)

            def prepare(body, q):
                sum_rows(body, q)
                inverse_deviation(body, q)

            prepare(0, 0)
            run_groups(pool, lambda body, q: prepare(body + q, 1 - q))


def build(nc, x_t, w_tok, w_qk_a, w_qk_b, w_v_a, w_v_b, b_tok, b_qk, b_v, ln_cols, row_consts, ident, w1_a, w1_b, w2, b1,
          wr1_a, wr1_b, br1, wr2_a, wr2_b, br2, b2, expert_ids, out):
    h_rows = nc.dram_tensor("h_rows", (PAIRS, TILES, HALF, DIM), F32).ap()
    att_rows = nc.dram_tensor("att_rows", (PAIRS, TILES, HALF, DIM), F32).ap()
    b1_parts = nc.dram_tensor("b1_parts", (3, EXPERTS * HIDDEN), BF16).ap()
    attention_phase(nc, x_t, w_tok, w_qk_a, w_qk_b, w_v_a, w_v_b, b_tok, b_qk, b_v, ln_cols, row_consts, ident,
                    h_rows, att_rows)

    def by_group(t):
        return t.rearrange("u c p e -> (u c p) e").rearrange("(g t) e -> g t e", t=GT)

    expert_phase(nc, by_group(h_rows), by_group(att_rows), w1_a, w1_b, w2, b1, wr1_a, wr1_b, br1, wr2_a, wr2_b, br2, b2,
                 expert_ids, ident, b1_parts, out.rearrange("(g t) e -> g t e", t=GT))


def layout(x, L0_tok_W, L0_tok_b, L0_attn_qkv_w, L0_attn_qkv_b, L0_attn_ln_g, L0_attn_ln_b, L0_ffn_W1, L0_ffn_b1,
           L0_ffn_W2, L0_ffn_b2, L0_ffn_Wr1, L0_ffn_br1, L0_ffn_Wr2, L0_ffn_br2):
    import numpy as np

    x = np.asarray(x).reshape(IMAGES, 3, 14, 16, 14, 16).transpose(0, 1, 2, 4, 5, 3)
    x = x.reshape(PAIRS, COLS, PCH, P).transpose(0, 3, 2, 1)
    order = np.arange(2 * DIM).reshape(2 * GROUPS, HG, 1, HEAD_DIM)
    order = np.broadcast_to(order, (2 * GROUPS, HG, 2, HEAD_DIM)).reshape(2 * GROUPS, P)
    qkv_w, qkv_b = np.asarray(L0_attn_qkv_w), np.asarray(L0_attn_qkv_b)
    w_qk = qkv_w[order].transpose(2, 0, 1)
    w_v = qkv_w[2 * DIM:].T
    g, b = np.asarray(L0_attn_ln_g), np.asarray(L0_attn_ln_b)
    ln_cols = np.stack([g[:P], b[:P], np.tile(g[P:], 2), np.tile(b[P:], 2)], axis=1)
    row_consts = np.zeros((P, 2 + HG), np.float32)
    tilde = np.arange(P) % ROWS >= HEAD_DIM
    row_consts[:, 0] = np.where(tilde, -BETA * SCALE, (1.0 + BETA) * SCALE)
    row_consts[:, 1] = tilde
    for hh in range(HG):
        row_consts[ROWS * hh:ROWS * hh + 2, 2 + hh] = -1.0
    w1 = np.asarray(L0_ffn_W1).transpose(2, 0, 1)
    w2 = np.asarray(L0_ffn_W2).reshape(EXPERTS, DIM, FCH, P).transpose(3, 0, 2, 1)
    wr1, wr2 = np.asarray(L0_ffn_Wr1).T, np.asarray(L0_ffn_Wr2).T
    br1 = np.asarray(L0_ffn_br1)
    return {
        "x_t": x,
        "w_tok": np.asarray(L0_tok_W).T.reshape(PCH, P, DIM).transpose(1, 0, 2),
        "w_qk_a": w_qk[:P], "w_qk_b": w_qk[P:], "w_v_a": w_v[:P], "w_v_b": w_v[P:],
        "b_tok": np.tile(np.asarray(L0_tok_b), (HALF, 1)),
        "b_qk": qkv_b[order].T,
        "b_v": np.tile(qkv_b[2 * DIM:], (HALF, 1)),
        "ln_cols": ln_cols, "row_consts": row_consts, "ident": np.eye(P, dtype=np.float32),
        "w1_a": w1[:P], "w1_b": np.concatenate([w1[P:], w1[P:]]), "w2": w2,
        "b1": np.asarray(L0_ffn_b1).reshape(EXPERTS * FCH, P),
        "wr1_a": wr1[:P], "wr1_b": wr1[P:],
        "br1": np.stack([br1[:P], np.tile(br1[P:], 2)], axis=1),
        "wr2_a": wr2[:P], "wr2_b": wr2[P:],
        "br2": np.tile(np.asarray(L0_ffn_br2), (P, GTILES, 1)),
        "b2": np.asarray(L0_ffn_b2),
        "expert_ids": np.tile(np.arange(EXPERTS, dtype=np.float32), (P, 1)),
    }


def kernel(**inputs):
    import numpy as np
    import concourse.bacc as bacc
    from concourse.bass_utils import run_bass_kernel_spmd

    nc = bacc.Bacc("TRN2", target_bir_lowering=False, num_devices=1)
    arrays, args = {}, {}
    for name, a in layout(**inputs).items():
        a = np.ascontiguousarray(a)
        arrays[f"in_{name}"] = a
        args[name] = nc.dram_tensor(f"in_{name}", a.shape, mybir.dt.from_np(a.dtype), kind="ExternalInput").ap()
    out = nc.dram_tensor("out_rows", (IMAGES * TOKENS, DIM), F32, kind="ExternalOutput").ap()
    build(nc, out=out, **args)
    result = run_bass_kernel_spmd(nc, [arrays], core_ids=[0])
    return result.results[0]["out_rows"].reshape(IMAGES, TOKENS, DIM)
```

```python
from contextlib import ExitStack

import concourse.bass as bass
from concourse import mybir

F32 = mybir.dt.float32
F16 = mybir.dt.float16
BF16 = mybir.dt.bfloat16
U32 = mybir.dt.uint32
ALU = mybir.AluOpType
ACT = mybir.ActivationFunctionType
AX = mybir.AxisListType

P = 128
IMAGES = 64
TOKENS = 196
DIM = 192
HI = DIM - P
PATCH_DIM = 768
PCH = PATCH_DIM // P
HEADS = 12
HEAD_DIM = 16
HG = 4
GROUPS = HEADS // HG
ROWS = 2 * HEAD_DIM
HALF = TOKENS // 2
PAIR = 2
PAIRS = IMAGES // PAIR
COLS = PAIR * TOKENS
TILES = PAIR * 2
STEPS = GROUPS * PAIR
ALL_STEPS = PAIRS * STEPS
BETA = 0.2
EPS = 1e-5
SCALE = HEAD_DIM ** -0.5
PW = TOKENS + 2

BODY_PAIRS = 2
BODY_STEPS = BODY_PAIRS * STEPS
BODIES = PAIRS // BODY_PAIRS
DRAIN = 3

EXPERTS = 8
HIDDEN = 768
FCH = HIDDEN // P
UNITS = FCH // 2
GT = 256
GTILES = GT // P
FGROUPS = IMAGES * TOKENS // GT
EU = EXPERTS * UNITS
LAG = 2
MID = 4


def wait(eng, sem, value):
    if not isinstance(value, int) or value > 0:
        eng.wait_ge(sem, value)


class Step:

    def __init__(self, body, kk, ahead):
        k = kk + ahead
        self.s = body * BODY_STEPS + k
        self.pair = body * BODY_PAIRS + k // STEPS
        self.there = not isinstance(body, int) or 0 <= self.s < ALL_STEPS
        self.q = (k // STEPS) % 2
        self.odd = k % 2
        self.group = k % GROUPS
        self.image = (k // GROUPS) % PAIR
        self.first = k % STEPS == 0
        self.before = body + (k // STEPS) // 2


class Pair:

    def __init__(self, body, kk, ahead):
        k = kk // STEPS + ahead
        self.u = body * BODY_PAIRS + k
        self.there = not isinstance(body, int) or 0 <= self.u < PAIRS
        self.q = k % 2
        self.before = body + k // 2


def run_bodies(eng, step):
    step(0, -1)
    for kk in range(BODY_STEPS):
        step(0, kk)
    with eng.Fori(1, BODIES - 1) as body:
        for kk in range(BODY_STEPS):
            step(body, kk)
    for kk in range(BODY_STEPS + DRAIN):
        step(BODIES - 1, kk)


def attention_phase(nc, x_t, w_tok, w_qk_a, w_qk_b, w_v_a, w_v_b, b_tok, b_qk, b_v, ln_cols, row_consts, ident_in,
                    h_dram, att_dram):
    ctx = ExitStack()
    with ctx:
        def sb(name, shape, dt=F32):
            return ctx.enter_context(nc.sbuf_tensor(name, shape, dt))

        def ps(name, shape, dt=F32):
            return ctx.enter_context(nc.psum_tensor(name, shape, dt))

        def sem(name):
            return ctx.enter_context(nc.semaphore(name))

        wtok = sb("wtok", [P, PCH, DIM])
        wqk_a = sb("wqk_a", [P, 2 * GROUPS, P])
        wqk_b = sb("wqk_b", [P, 2 * GROUPS, P])
        wv_a = sb("wv_a", [P, DIM])
        wv_b = sb("wv_b", [P, DIM])
        wqk_ah = sb("wqk_ah", [P, 2 * GROUPS, P], BF16)
        wqk_al = sb("wqk_al", [P, 2 * GROUPS, P], BF16)
        wqk_bh = sb("wqk_bh", [P, 2 * GROUPS, P], BF16)
        wqk_bl = sb("wqk_bl", [HI, 2 * GROUPS, P], BF16)
        wv_ah = sb("wv_ah", [P, DIM], BF16)
        wv_al = sb("wv_al", [P, DIM], BF16)
        wv_bh = sb("wv_bh", [P, DIM], BF16)
        wv_bl = sb("wv_bl", [HI, DIM], BF16)
        btok = sb("btok", [HALF, DIM])
        bqk = sb("bqk", [P, 2 * GROUPS])
        bq_scaled = sb("bq_scaled", [P, GROUPS])
        bv = sb("bv", [HALF, DIM])
        lnc = sb("lnc", [P, 4])
        rowc = sb("rowc", [P, 2 + HG])
        ident = sb("ident", [P, P])
        ident16 = sb("ident16", [P, P], BF16)
        max_sel = sb("max_sel", [P, HG, HALF], BF16)
        minus_half = sb("minus_half", [HALF, TILES])
        one_eps = sb("one_eps", [HALF, TILES])
        eps_sq = sb("eps_sq", [HALF, TILES])
        spacer = sb("spacer", [HALF, 1])
        x_buf = [sb(f"x_buf{i}", [P, PCH, COLS]) for i in range(2)]
        h_buf = sb("h_buf", [HALF, TILES, DIM])
        stats = sb("stats", [HALF, TILES, 6])
        meanvar = sb("meanvar", [HALF, TILES, 2])
        var_eps = [sb(f"var_eps{i}", [HALF, TILES]) for i in range(2)]
        rstd = sb("rstd", [HALF, TILES])
        xn = sb("xn", [HALF, TILES, 2, P])
        xt_a = sb("xt_a", [P, COLS])
        xt_b = sb("xt_b", [P, COLS])
        x_ah = sb("x_ah", [P, COLS], BF16)
        x_al = sb("x_al", [P, COLS], BF16)
        x_b = sb("x_b", [P, COLS], BF16)
        padded = sb("padded", [P, 2 * GROUPS * PAIR, PW])
        beside = sb("beside", [P, 2 * GROUPS * PAIR, TOKENS])
        qk = sb("qk", [P, 2 * GROUPS * PAIR, TOKENS])
        qk_hi = sb("qk_hi", [P, 2 * GROUPS * PAIR, TOKENS], F16)
        qk_lo = sb("qk_lo", [P, 2 * GROUPS * PAIR, TOKENS], F16)
        q_stack = [sb(f"q_stack{i}", [P, HEADS, PAIR * TOKENS], F16) for i in range(2)]
        k_stack = [sb(f"k_stack{i}", [P, HEADS, PAIR * TOKENS], F16) for i in range(2)]
        v_buf = [sb(f"v_buf{i}", [HALF, TILES, HEADS, 32]) for i in range(2)]
        row_max = [sb(f"row_max{i}", [HALF, 2, HG]) for i in range(2)]
        max_parts = [sb(f"max_parts{i}", [HALF, 2, P], BF16) for i in range(2)]
        max_rows = [sb(f"max_rows{i}", [P, 2, HALF], BF16) for i in range(2)]
        probs = [sb(f"probs{i}", [HALF, HG, 2, TOKENS]) for i in range(2)]
        mixed = [sb(f"mixed{i}", [P, TOKENS]) for i in range(2)]
        recip = sb("recip", [HALF, 2, HG, 1])
        att = [sb(f"att{i}", [HALF, TILES, DIM]) for i in range(2)]

        s_bank = [ps(f"s_bank{i}", [P, 2, 256]) for i in range(2)]
        t_bank = [ps(f"t_bank{i}", [P, 2, 256]) for i in range(2)]
        o_bank = ps("o_bank", [P, 512])
        m_bank = ps("m_bank", [P, 512])
        p_bank = [ps(f"p_bank{i}", [P, 512]) for i in range(2)]
        back_tr = m_bank[0:HALF, 0:2 * P].rearrange("p (u h d) -> p u h d", u=2, h=HG)
        max_tr = m_bank[:, 2 * P:512].bitcast(BF16).rearrange("p (u n) -> p u n", u=2)

        weights_in = sem("weights_in")
        consts_set = sem("consts_set")
        x_in = [sem(f"x_in{i}") for i in range(2)]
        p_ready = [sem(f"p_ready{i}") for i in range(2)]
        h_ready = sem("h_ready")
        h_stored = sem("h_stored")
        stats_ready = sem("stats_ready")
        meanvar_ready = sem("meanvar_ready")
        var_ready = sem("var_ready")
        rstd_ready = sem("rstd_ready")
        xn_ready = sem("xn_ready")
        xt_a_ready = sem("xt_a_ready")
        xt_b_ready = sem("xt_b_ready")
        x_high = sem("x_high")
        x_split = sem("x_split")
        v_ready = sem("v_ready")
        padded_ready = sem("padded_ready")
        beside_ready = sem("beside_ready")
        qk_ready = sem("qk_ready")
        hi_ready = sem("hi_ready")
        lo_ready = sem("lo_ready")
        q_stacked = sem("q_stacked")
        k_stacked = sem("k_stacked")
        s_ready = sem("s_ready")
        max_ready = sem("max_ready")
        max_hi_ready = sem("max_hi_ready")
        max_parts_ready = sem("max_parts_ready")
        max_tr_ready = sem("max_tr_ready")
        max_rows_ready = sem("max_rows_ready")
        t_ready = sem("t_ready")
        probs_ready = sem("probs_ready")
        o_ready = sem("o_ready")
        mixed_ready = sem("mixed_ready")
        back_ready = sem("back_ready")
        recip_ready = sem("recip_ready")
        att_ready = sem("att_ready")
        att_stored = [sem(f"att_stored{i}") for i in range(2)]

        LOADS = [(wtok, w_tok), (wqk_a, w_qk_a), (wqk_b, w_qk_b), (wv_a, w_v_a), (wv_b, w_v_b), (btok, b_tok),
                 (bqk, b_qk), (bv, b_v), (lnc, ln_cols), (rowc, row_consts), (ident, ident_in)]
        STACKED = 16 * 4 * HG
        USES = 6

        def patch_uses(u):
            return 1 if isinstance(u, int) and u == 0 else USES * u

        def v_uses(u):
            return USES * PAIRS if isinstance(u, int) and u == PAIRS - 1 else USES * u + USES + 1
        CONSTS = 10 + HG + 2 + 8

        block = ctx.enter_context(nc.Block())

        @block.sync
        def _(sp):
            for dst, src in LOADS:
                sp.dma_start(dst[:], src).then_inc(weights_in, 16)

            def load_x(pr):
                if pr.there:
                    if not isinstance(pr.u, int) or pr.u >= 2:
                        sp.wait_ge(p_ready[1], patch_uses(pr.u - 2))
                    sp.dma_start(x_buf[pr.q][:], x_t[bass.ds(pr.u, 1)].rearrange("o p c n -> (o p) c n")
                                 ).then_inc(x_in[pr.q], 16)

            def stack(pr, which):
                if pr.there:
                    sp.wait_ge(lo_ready, 2 * pr.u + which + 1)
                    dst = (q_stack, k_stack)[which][pr.q]
                    tiles = slice(which * GROUPS * PAIR, (which + 1) * GROUPS * PAIR)
                    order = ((qk_hi, qk_lo, qk_hi, qk_lo), (qk_hi, qk_hi, qk_lo, qk_lo))[which]
                    for r, part in enumerate(order):
                        for hh in range(HG):
                            sp.dma_start(dst[32 * r:32 * r + 32, hh::HG, :],
                                         part[32 * hh:32 * hh + 32, tiles, :].rearrange("p (g i) n -> p g (i n)",
                                                                                      i=PAIR)
                                         ).then_inc((q_stacked, k_stacked)[which], 16)

            def rows(dram, pr):
                return dram[bass.ds(pr.u, 1)].rearrange("o c p e -> p (o c) e")

            def store_h(pr):
                if pr.there:
                    sp.wait_ge(h_ready, 2 * pr.u + 2)
                    sp.dma_start(rows(h_dram, pr), h_buf[:]).then_inc(h_stored, 16)

            def store_att(pr):
                if pr.there:
                    sp.wait_ge(att_ready, (pr.u + 1) * STEPS)
                    sp.dma_start(rows(att_dram, pr), att[pr.q][:]).then_inc(att_stored[pr.q], 16)

            def step(body, kk):
                k = kk % STEPS
                if kk == -1:
                    load_x(Pair(0, 0, 0))
                    load_x(Pair(0, 0, 1))
                    store_h(Pair(0, 0, 0))
                    stack(Pair(0, 0, 0), 0)
                    stack(Pair(0, 0, 0), 1)
                    store_h(Pair(0, 0, 1))
                elif k == 0:
                    load_x(Pair(body, kk, 2))
                elif k == 1:
                    stack(Pair(body, kk, 1), 0)
                    stack(Pair(body, kk, 1), 1)
                elif k == 2:
                    store_att(Pair(body, kk, -1))
                elif k == 4:
                    store_h(Pair(body, kk, 2))
            run_bodies(sp, step)
            sp.wait_ge(h_stored, 16 * PAIRS)
            for i in range(2):
                sp.wait_ge(att_stored[i], 16 * PAIRS // 2)

        @block.tensor
        def _(pe):
            pe.wait_ge(weights_in, 16 * len(LOADS))
            pe.wait_ge(consts_set, CONSTS)

            def project_patches(pr, half, c):
                if pr.there:
                    if c == 0:
                        if half == 0:
                            pe.wait_ge(x_in[pr.q], 16 * (pr.before + 1))
                        wait(pe, padded_ready, 2 * GROUPS * (pr.u - 1) + 5 + half)
                    t0 = (2 * half + c) * HALF
                    for f in range(PCH):
                        ins = nc.tensor.matmul(p_bank[half][0:HALF, c * DIM:(c + 1) * DIM],
                                               x_buf[pr.q][:, f, t0:t0 + HALF], wtok[:, f, :],
                                               start=(f == 0), stop=(f == PCH - 1))
                    if c == 1:
                        ins.then_inc(p_ready[half], 1)

            def claim(pr, n):
                if n < 2:
                    wait(pe, v_ready, PAIR * (pr.u - 1) + n + 1)
                elif n < 4:
                    pe.wait_ge((xt_a_ready, xt_b_ready)[n - 2], pr.u + 1)
                else:
                    pe.wait_ge(padded_ready, 2 * GROUPS * pr.u + n - 3)
                return p_bank[n % 2], p_ready[n % 2]

            def transpose_xn(pr, n):
                if pr.there:
                    if n == 0:
                        pe.wait_ge(xn_ready, pr.u + 1)
                    bank, ready = claim(pr, n)
                    for c in range(TILES):
                        last = nc.tensor.transpose(bank[:, c * HALF:(c + 1) * HALF], xn[:, c, n, :],
                                                   ident[0:HALF, 0:HALF])
                    last.then_inc(ready, 1)

            def project_qk(pr, i):
                if pr.there:
                    if i == 0:
                        pe.wait_ge(x_split, 4 * (pr.u + 1))
                    bank, ready = claim(pr, 2 + i)
                    out = bank[:, 0:COLS]
                    nc.tensor.matmul(out, wqk_ah[:, i, :], x_ah[:], start=True, stop=False)
                    nc.tensor.matmul(out, wqk_ah[:, i, :], x_al[:], start=False, stop=False)
                    nc.tensor.matmul(out, wqk_al[:, i, :], x_ah[:], start=False, stop=False)
                    nc.tensor.matmul(out, wqk_bh[:, i, :], x_b[:], start=False, stop=False)
                    nc.tensor.matmul(out, wqk_bl[:, i, :], x_b[0:HI, :], start=False, stop=True).then_inc(ready, 1)

            def project_v(pr, im):
                if pr.there:
                    if isinstance(pr.u, int) and pr.u == PAIRS - 1:
                        pe.wait_ge(padded_ready, 2 * GROUPS * pr.u + 5 + im)
                    else:
                        pe.wait_ge(h_ready, 2 * (pr.u + 1) + im + 1)
                    for c in range(2):
                        t0 = (2 * im + c) * HALF
                        tokens = slice(t0, t0 + HALF)
                        out = p_bank[im][0:HALF, c * DIM:(c + 1) * DIM]
                        nc.tensor.matmul(out, x_ah[:, tokens], wv_ah[:], start=True, stop=False)
                        nc.tensor.matmul(out, x_ah[:, tokens], wv_al[:], start=False, stop=False)
                        nc.tensor.matmul(out, x_al[:, tokens], wv_ah[:], start=False, stop=False)
                        nc.tensor.matmul(out, x_b[:, tokens], wv_bh[:], start=False, stop=False)
                        last = nc.tensor.matmul(out, x_b[0:HI, tokens], wv_bl[:], start=False, stop=True)
                    last.then_inc(p_ready[im], 1)

            def transpose_back(st):
                if st.there:
                    pe.wait_ge(mixed_ready, st.s + 1)
                    pe.wait_ge(max_rows_ready, min(st.s + 3, ALL_STEPS) if isinstance(st.s, int) else st.s + 3)
                    wait(pe, att_ready, st.s)
                    for u in range(2):
                        last = nc.tensor.transpose(m_bank[0:HALF, u * P:(u + 1) * P],
                                                   mixed[st.odd][:, u * HALF:(u + 1) * HALF], ident[:])
                    last.then_inc(back_ready, 1)

            def head_cols(st, u=None):
                t0 = st.image * TOKENS + (0 if u is None else u * HALF)
                return slice(t0, t0 + (TOKENS if u is None else HALF))

            def scores(st, heads):
                if st.there:
                    if st.first and heads[0] == 0:
                        pe.wait_ge(q_stacked, (st.pair + 1) * STACKED)
                        pe.wait_ge(k_stacked, (st.pair + 1) * STACKED)
                    for hh in heads:
                        head = HG * st.group + hh
                        wait(pe, max_ready, HG * st.s + hh - 1)
                        for u in range(2):
                            last = nc.tensor.matmul(s_bank[hh % 2][0:HALF, u, 0:TOKENS],
                                                    q_stack[st.q][:, head, head_cols(st, u)],
                                                    k_stack[st.q][:, head, head_cols(st)], start=True, stop=True)
                        last.then_inc(s_ready, 1)

            def scores_less_max(st, heads):
                if st.there:
                    if heads[0] == 0:
                        pe.wait_ge(max_rows_ready, st.s + 1)
                    for hh in heads:
                        head = HG * st.group + hh
                        wait(pe, probs_ready, HG * st.s + hh - 1)
                        for v in range(2):
                            out = t_bank[hh % 2][0:HALF, v, 0:TOKENS]
                            nc.tensor.matmul(out, k_stack[st.q][:, head, head_cols(st, v)],
                                             q_stack[st.q][:, head, head_cols(st)], start=True, stop=False)
                            last = nc.tensor.matmul(out, max_sel[:, hh, :],
                                                    max_rows[st.odd][:].rearrange("p u n -> p (u n)"),
                                                    start=False, stop=True)
                        last.then_inc(t_ready, 1)

            def mix(st):
                if st.there:
                    pe.wait_ge(probs_ready, HG * (st.s + 1))
                    if st.first:
                        pe.wait_ge(v_ready, PAIR * (st.pair + 1))
                    wait(pe, mixed_ready, st.s)
                    for v in range(2):
                        for hh in range(HG):
                            last = nc.tensor.matmul(o_bank[32 * hh:32 * hh + 32, 0:TOKENS],
                                                    v_buf[st.q][:, 2 * st.image + v, HG * st.group + hh, :],
                                                    probs[st.odd][:, hh, v, :], start=(v == 0), stop=(v == 1))
                    last.then_inc(o_ready, 1)

            def transpose_max(st):
                if st.there:
                    pe.wait_ge(max_parts_ready, st.s + 1)
                    wait(pe, att_ready, st.s - 2)
                    for u in range(2):
                        last = nc.tensor.transpose(max_tr[:, u, 0:HALF], max_parts[st.odd][:, u, :],
                                                   ident16[0:HALF, 0:HALF])
                    last.then_inc(max_tr_ready, 1)

            def before_max(body, kk):
                k = kk % STEPS
                if k == 0:
                    project_qk(Pair(body, kk, 1), 3)
                    project_qk(Pair(body, kk, 1), 4)
                elif k in (1, 2):
                    project_patches(Pair(body, kk, 2), k - 1, 0)
                elif k == 3:
                    project_v(Pair(body, kk, 1), 0)
                elif k == 4:
                    project_v(Pair(body, kk, 1), 1)
                    transpose_xn(Pair(body, kk, 2), 0)
                elif k == 5:
                    project_qk(Pair(body, kk, 2), 0)

            def after_max(body, kk):
                k = kk % STEPS
                if k == 0:
                    project_qk(Pair(body, kk, 1), 5)
                elif k in (1, 2):
                    project_patches(Pair(body, kk, 2), k - 1, 1)
                elif k == 4:
                    transpose_xn(Pair(body, kk, 2), 1)
                elif k == 5:
                    project_qk(Pair(body, kk, 2), 1)
                    project_qk(Pair(body, kk, 2), 2)

            def fill_pipeline():
                first, second = Pair(0, 0, 0), Pair(0, 0, 1)
                for pr in (first, second):
                    for half in range(2):
                        for c in range(2):
                            project_patches(pr, half, c)
                    if pr is second:
                        project_v(first, 0)
                        project_v(first, 1)
                    transpose_xn(pr, 0)
                    transpose_xn(pr, 1)
                    for i in range(2 * GROUPS if pr is first else GROUPS):
                        project_qk(pr, i)

            def step(body, kk):
                if kk == -1:
                    fill_pipeline()
                transpose_back(Step(body, kk, -2))
                scores(Step(body, kk, 1), (0, 1))
                scores_less_max(Step(body, kk, 0), (0, 1))
                mix(Step(body, kk, -1))
                scores(Step(body, kk, 1), (2, 3))
                scores_less_max(Step(body, kk, 0), (2, 3))
                if kk >= 0:
                    before_max(body, kk)
                transpose_max(Step(body, kk, 1))
                if kk >= 0:
                    after_max(body, kk)
            run_bodies(pe, step)

        @block.vector
        def _(dve):
            for i in range(2):
                nc.vector.memset(v_buf[i][:], 0.0).then_inc(consts_set, 1)
                nc.vector.memset(max_parts[i][:], 0.0).then_inc(consts_set, 1)
            nc.vector.memset(padded[:], 0.0).then_inc(consts_set, 1)
            nc.vector.memset(minus_half[:], -0.5).then_inc(consts_set, 1)
            nc.vector.memset(one_eps[:], 1.0 + EPS).then_inc(consts_set, 1)
            nc.vector.memset(eps_sq[:], EPS * EPS).then_inc(consts_set, 1)
            dve.wait_ge(consts_set, 8)
            for i in range(2):
                nc.vector.memset(v_buf[i][:, :, :, HEAD_DIM:HEAD_DIM + 1], 1.0).then_inc(consts_set, 1)
            dve.wait_ge(weights_in, 16 * len(LOADS))
            for hh in range(HG):
                nc.vector.tensor_copy(max_sel[:, hh, :], rowc[:, 2 + hh:3 + hh].to_broadcast([P, HALF])
                                      ).then_inc(consts_set, 1)
            nc.vector.tensor_scalar(bq_scaled[:], bqk[:, 0:GROUPS], rowc[:, 0:1], None, ALU.mult
                                    ).then_inc(consts_set, 1)
            nc.vector.tensor_copy(ident16[:], ident[:]).then_inc(consts_set, 1)
            parts = ((wqk_a, wqk_ah, wqk_al, P), (wqk_b, wqk_bh, wqk_bl, HI), (wv_a, wv_ah, wv_al, P),
                     (wv_b, wv_bh, wv_bl, HI))
            for whole, high, low, n in parts:
                nc.vector.tensor_copy(high[:], whole[:]).then_inc(consts_set, 1)
            dve.wait_ge(consts_set, CONSTS - 4)
            for whole, high, low, n in parts:
                nc.vector.tensor_tensor(low[:], whole[0:n], high[0:n], ALU.subtract).then_inc(consts_set, 1)


            def row_maxima(st, heads):
                if st.there:
                    for hh in heads:
                        dve.wait_ge(s_ready, HG * st.s + hh + 1)
                        nc.vector.reduce_max(row_max[st.odd][:, :, hh:hh + 1], s_bank[hh % 2][0:HALF, :, 0:TOKENS],
                                             AX.X).then_inc(max_ready, 1)

            def split_maxima(st):
                if st.there:
                    dve.wait_ge(max_ready, HG * (st.s + 1))
                    wait(dve, max_tr_ready, st.s - 1)
                    parts = max_parts[st.odd][:].rearrange("p u (h r) -> p u h r", h=HG)
                    nc.vector.tensor_copy(parts[:, :, :, 0], row_max[st.odd][:]).then_inc(max_hi_ready, 1)
                    dve.wait_ge(max_hi_ready, st.s + 1)
                    nc.vector.tensor_tensor(parts[:, :, :, 1], row_max[st.odd][:], parts[:, :, :, 0], ALU.subtract
                                            ).then_inc(max_parts_ready, 1)

            def normalise(st):
                if st.there:
                    dve.wait_ge(back_ready, st.s + 1)
                    wait(dve, att_ready, st.s)
                    if st.first:
                        wait(dve, att_stored[st.q], 16 * st.before)
                    nc.vector.reciprocal(recip[:], back_tr[:, :, :, HEAD_DIM:HEAD_DIM + 1]).then_inc(recip_ready, 1)
                    dve.wait_ge(recip_ready, st.s + 1)
                    width = HG * HEAD_DIM
                    out = att[st.q][:, 2 * st.image:2 * st.image + 2, st.group * width:(st.group + 1) * width]
                    nc.vector.tensor_tensor(out.rearrange("p u (h d) -> p u h d", h=HG),
                                            back_tr[:, :, :, 0:HEAD_DIM],
                                            recip[:].to_broadcast([HALF, 2, HG, HEAD_DIM]), ALU.mult
                                            ).then_inc(att_ready, 1)

            def take_h(pr, half):
                if pr.there:
                    dve.wait_ge(p_ready[half], patch_uses(pr.u))
                    if half == 0:
                        wait(dve, h_stored, 16 * pr.u)
                        wait(dve, xn_ready, pr.u)
                    h2 = h_buf[:, 2 * half:2 * half + 2, :]
                    nc.vector.tensor_tensor(h2, p_bank[half][0:HALF, 0:2 * DIM].rearrange("p (c e) -> p c e", c=2),
                                            btok[:].unsqueeze(1).to_broadcast([HALF, 2, DIM]), ALU.add
                                            ).then_inc(h_ready, 1)
                    dve.wait_ge(h_ready, 2 * pr.u + half + 1)
                    for c in (2 * half, 2 * half + 1):
                        nc.vector.bn_stats(stats[:, c, :], h_buf[:, c, :]).then_inc(stats_ready, 1)
                    if half == 1:
                        dve.wait_ge(stats_ready, TILES * (pr.u + 1))
                        wait(dve, rstd_ready, pr.u)
                        nc.vector.memset(spacer[:], 0.0)
                        for c in range(TILES):
                            nc.vector.bn_aggr(meanvar[:, c, :], stats[:, c, :]).then_inc(meanvar_ready, 1)

            def layernorm(pr):
                if pr.there:
                    dve.wait_ge(rstd_ready, pr.u + 1)
                    wait(dve, xt_b_ready, pr.u)
                    for c in range(TILES):
                        for n, f0, c0, nf in ((0, 0, 0, P), (1, P, 0, HI), (1, P, HI, HI)):
                            ins = nc.vector.tensor_scalar(xn[:, c, n, c0:c0 + nf], h_buf[:, c, f0:f0 + nf],
                                                          meanvar[:, c, 0:1], rstd[:, c:c + 1],
                                                          ALU.subtract, ALU.mult)
                    ins.then_inc(xn_ready, 1)

            def take_xt_a(pr):
                if pr.there:
                    dve.wait_ge(p_ready[0], USES * pr.u + 2)
                    wait(dve, x_split, 4 * pr.u)
                    nc.vector.tensor_scalar(xt_a[:], p_bank[0][:, 0:COLS], lnc[:, 0:1], lnc[:, 1:2], ALU.mult, ALU.add
                                            ).then_inc(xt_a_ready, 1)

            def split_low(pr):
                if pr.there:
                    dve.wait_ge(x_high, 2 * (pr.u + 1))
                    nc.vector.tensor_tensor(x_al[:], xt_a[:], x_ah[:], ALU.subtract).then_inc(x_split, 2)
                    nc.vector.tensor_tensor(x_b[HI:P, :], xt_b[HI:P, :], x_b[HI:P, :], ALU.subtract
                                            ).then_inc(x_split, 2)

            def take_v(pr, im):
                if pr.there:
                    if im == 0:
                        wait(dve, o_ready, STEPS * (pr.u - 1))
                    dve.wait_ge(p_ready[im], v_uses(pr.u))
                    out = v_buf[pr.q][:, 2 * im:2 * im + 2, :, 0:HEAD_DIM]
                    nc.vector.tensor_tensor(
                        out, p_bank[im][0:HALF, 0:2 * DIM].rearrange("p (c h d) -> p c h d", c=2, h=HEADS),
                        bv[:].rearrange("p (h d) -> p h d", h=HEADS).unsqueeze(1)
                        .to_broadcast([HALF, 2, HEADS, HEAD_DIM]), ALU.add).then_inc(v_ready, 1)

            def add_tilde(pr, which):
                if pr.there:
                    tiles = slice(which * GROUPS * PAIR, (which + 1) * GROUPS * PAIR)
                    dve.wait_ge(beside_ready, 2 * pr.u + which + 1)
                    wait(dve, lo_ready, 2 * pr.u + which - 1)
                    nc.vector.scalar_tensor_tensor(qk[:, tiles, :], beside[:, tiles, :], rowc[:, 1:2],
                                                   padded[:, tiles, 1:TOKENS + 1], ALU.mult, ALU.add
                                                   ).then_inc(qk_ready, 1)

            def fill_pipeline():
                first, second = Pair(0, 0, 0), Pair(0, 0, 1)
                for pr in (first, second):
                    take_h(pr, 0)
                    take_h(pr, 1)
                    layernorm(pr)
                    if pr is second:
                        take_v(first, 0)
                        take_v(first, 1)
                    take_xt_a(pr)
                    split_low(pr)
                    if pr is first:
                        add_tilde(pr, 0)
                        add_tilde(pr, 1)

            def step(body, kk):
                k = kk % STEPS
                if kk == -1:
                    fill_pipeline()
                row_maxima(Step(body, kk, 1), (0, 1))
                normalise(Step(body, kk, -2))
                if kk >= 0:
                    if k in (2, 3):
                        take_h(Pair(body, kk, 2), k - 2)
                    elif k == 5:
                        split_low(Pair(body, kk, 2))
                row_maxima(Step(body, kk, 1), (2, 3))
                split_maxima(Step(body, kk, 1))
                if kk >= 0:
                    if k in (0, 1):
                        add_tilde(Pair(body, kk, 1), k)
                    elif k == 3:
                        take_v(Pair(body, kk, 1), 0)
                        layernorm(Pair(body, kk, 2))
                    elif k == 4:
                        take_v(Pair(body, kk, 1), 1)
                        take_xt_a(Pair(body, kk, 2))
            run_bodies(dve, step)

        @block.scalar
        def _(act):
            act.wait_ge(weights_in, 16 * len(LOADS))
            act.wait_ge(consts_set, CONSTS)

            def exponentials(st, heads):
                if st.there:
                    if heads[0] == 0:
                        wait(act, o_ready, st.s - 1)
                    for hh in heads:
                        act.wait_ge(t_ready, HG * st.s + hh + 1)
                        nc.scalar.activation(probs[st.odd][:, hh], t_bank[hh % 2][0:HALF, :, 0:TOKENS], ACT.Exp
                                             ).then_inc(probs_ready, 1)

            def copy_mixed(st):
                if st.there:
                    act.wait_ge(o_ready, st.s + 1)
                    wait(act, back_ready, st.s - 1)
                    nc.scalar.copy(mixed[st.odd][:], o_bank[:, 0:TOKENS]).then_inc(mixed_ready, 1)

            def copy_max_rows(st):
                if st.there:
                    act.wait_ge(max_tr_ready, st.s + 1)
                    wait(act, t_ready, HG * (st.s - 1))
                    nc.scalar.copy(max_rows[st.odd][:], max_tr[:, :, 0:HALF]).then_inc(max_rows_ready, 1)

            def take_xt_b(pr):
                if pr.there:
                    act.wait_ge(p_ready[1], USES * pr.u + 2)
                    wait(act, x_split, 4 * pr.u)
                    nc.scalar.activation(xt_b[:], p_bank[1][:, 0:COLS], ACT.Identity, bias=lnc[:, 3:4],
                                         scale=lnc[:, 2:3]).then_inc(xt_b_ready, 1)

            def split_high(pr):
                if pr.there:
                    act.wait_ge(xt_a_ready, pr.u + 1)
                    nc.scalar.copy(x_ah[:], xt_a[:]).then_inc(x_high, 1)
                    act.wait_ge(xt_b_ready, pr.u + 1)
                    nc.scalar.copy(x_b[:], xt_b[:]).then_inc(x_high, 1)

            def take_qk(pr, i):
                if pr.there:
                    which, n = i // GROUPS, 2 + i
                    if i % GROUPS == 0:
                        wait(act, qk_ready, 2 * pr.u + which - 1)
                    act.wait_ge(p_ready[n % 2], USES * pr.u + 2 + n // 2)
                    out = padded[:, PAIR * i:PAIR * (i + 1), 1:TOKENS + 1]
                    src = p_bank[n % 2][:, 0:COLS].rearrange("p (i n) -> p i n", i=PAIR)
                    if which == 0:
                        ins = nc.scalar.activation(out, src, ACT.Identity, bias=bq_scaled[:, i:i + 1],
                                                   scale=rowc[:, 0:1])
                    else:
                        ins = nc.scalar.activation(out, src, ACT.Identity, bias=bqk[:, i:i + 1])
                    ins.then_inc(padded_ready, 1)

            def take_high(pr, which):
                if pr.there:
                    tiles = slice(which * GROUPS * PAIR, (which + 1) * GROUPS * PAIR)
                    act.wait_ge(qk_ready, 2 * pr.u + which + 1)
                    wait(act, (q_stacked, k_stacked)[which], STACKED * pr.u)
                    nc.scalar.copy(qk_hi[:, tiles, :], qk[:, tiles, :]).then_inc(hi_ready, 1)

            def fill_pipeline():
                for u in range(2):
                    pr = Pair(0, 0, u)
                    take_xt_b(pr)
                    split_high(pr)
                    for i in range((2 - u) * GROUPS):
                        take_qk(pr, i)
                    if u == 0:
                        take_high(pr, 0)
                        take_high(pr, 1)

            def step(body, kk):
                k = kk % STEPS
                if kk == -1:
                    fill_pipeline()
                exponentials(Step(body, kk, 0), (0, 1))
                copy_mixed(Step(body, kk, -1))
                exponentials(Step(body, kk, 0), (2, 3))
                if kk >= 0:
                    if k == 0:
                        take_qk(Pair(body, kk, 1), 3)
                        take_qk(Pair(body, kk, 1), 4)
                    elif k == 2:
                        take_high(Pair(body, kk, 1), 1)
                    elif k == 5:
                        take_qk(Pair(body, kk, 2), 0)
                copy_max_rows(Step(body, kk, 1))
                if kk >= 0:
                    if k == 0:
                        take_qk(Pair(body, kk, 1), 5)
                        take_high(Pair(body, kk, 1), 0)
                    elif k == 4:
                        take_xt_b(Pair(body, kk, 2))
                        split_high(Pair(body, kk, 2))
                    elif k == 5:
                        take_qk(Pair(body, kk, 2), 1)
                        take_qk(Pair(body, kk, 2), 2)
            run_bodies(act, step)

        @block.gpsimd
        def _(pool):
            pool.wait_ge(consts_set, CONSTS)

            def inverse_deviation(pr):
                if pr.there:
                    pool.wait_ge(meanvar_ready, TILES * (pr.u + 1))
                    wait(pool, rstd_ready, pr.u)
                    nc.gpsimd.tensor_tensor(var_eps[0][:], meanvar[:, :, 1], one_eps[:], ALU.mult
                                            ).then_inc(var_ready, 1)
                    pool.wait_ge(var_ready, 2 * pr.u + 1)
                    nc.gpsimd.tensor_tensor(var_eps[1][:], var_eps[0][:], eps_sq[:], ALU.add).then_inc(var_ready, 1)
                    pool.wait_ge(var_ready, 2 * pr.u + 2)
                    wait(pool, xn_ready, pr.u)
                    nc.gpsimd.tensor_tensor(rstd[:], var_eps[1][:], minus_half[:], ALU.pow).then_inc(rstd_ready, 1)

            def add_beside(pr, which):
                if pr.there:
                    tiles = slice(which * GROUPS * PAIR, (which + 1) * GROUPS * PAIR)
                    pool.wait_ge(padded_ready, 2 * GROUPS * pr.u + GROUPS * (which + 1))
                    wait(pool, qk_ready, 2 * pr.u + which - 1)
                    nc.gpsimd.tensor_tensor(beside[:, tiles, :], padded[:, tiles, 0:TOKENS], padded[:, tiles, 2:PW],
                                            ALU.add).then_inc(beside_ready, 1)

            def take_low(pr, which):
                if pr.there:
                    tiles = slice(which * GROUPS * PAIR, (which + 1) * GROUPS * PAIR)
                    wait(pool, t_ready, HG * STEPS * (pr.u - 1))
                    pool.wait_ge(hi_ready, 2 * pr.u + which + 1)
                    wait(pool, (q_stacked, k_stacked)[which], STACKED * pr.u)
                    nc.gpsimd.tensor_tensor(qk_lo[:, tiles, :], qk[:, tiles, :], qk_hi[:, tiles, :], ALU.subtract
                                            ).then_inc(lo_ready, 1)

            def step(body, kk):
                k = kk % STEPS
                if kk == -1:
                    first = Pair(0, 0, 0)
                    inverse_deviation(first)
                    add_beside(first, 0)
                    add_beside(first, 1)
                    take_low(first, 0)
                    take_low(first, 1)
                    inverse_deviation(Pair(0, 0, 1))
                elif k == 0:
                    add_beside(Pair(body, kk, 1), 0)
                    take_low(Pair(body, kk, 1), 0)
                elif k == 1:
                    add_beside(Pair(body, kk, 1), 1)
                    take_low(Pair(body, kk, 1), 1)
                elif k == 3:
                    inverse_deviation(Pair(body, kk, 2))
            run_bodies(pool, step)


def expert_phase(nc, h_dram, att_dram, w1_a, w1_b, w2, b1, wr1_a, wr1_b, br1, wr2_a, wr2_b, br2, b2, expert_ids,
                 ident_in, b1_parts, out):
    ctx = ExitStack()
    with ctx:
        def sb(name, shape, dt=F32):
            return ctx.enter_context(nc.sbuf_tensor(name, shape, dt))

        def ps(name, shape, dt=F32):
            return ctx.enter_context(nc.psum_tensor(name, shape, dt))

        def sem(name):
            return ctx.enter_context(nc.semaphore(name))

        w1h_a = sb("w1h_a", [P, EXPERTS, HIDDEN], BF16)
        w1l_a = sb("w1l_a", [P, EXPERTS, HIDDEN], BF16)
        w1h_b = sb("w1h_b", [P, EXPERTS, HIDDEN], BF16)
        w1l_b = sb("w1l_b", [HI + 3, EXPERTS, HIDDEN], BF16)
        w2h = sb("w2h", [P, EXPERTS, FCH, DIM], BF16)
        w2l = sb("w2l", [P, EXPERTS, FCH, DIM], BF16)
        stage_a = [sb(f"stage_a{i}", [P, HIDDEN]) for i in range(2)]
        stage_b = [sb(f"stage_b{i}", [P, HIDDEN]) for i in range(2)]
        stage_2 = [sb(f"stage_2{i}", [P, FCH, DIM]) for i in range(2)]
        b1_rows = sb("b1_rows", [EXPERTS * FCH, P])
        b1_rest = [sb(f"b1_rest{i}", [EXPERTS * FCH, P]) for i in range(2)]
        b1_split = sb("b1_split", [EXPERTS * FCH, 3, P], BF16)
        r1_a = sb("r1_a", [P, DIM])
        r1_b = sb("r1_b", [HI, DIM])
        r1_bias = sb("r1_bias", [P, 2])
        r2_a = sb("r2_a", [P, EXPERTS])
        r2_b = sb("r2_b", [HI, EXPERTS])
        r2_bias = sb("r2_bias", [P, GTILES, EXPERTS])
        b2_sb = sb("b2_sb", [EXPERTS, DIM])
        ids = sb("ids", [P, EXPERTS])
        ident = sb("ident2", [P, P])
        minus_half = sb("minus_half2", [P, GTILES])
        eps = sb("eps", [P, GTILES])
        spacer = sb("spacer2", [P, 1])

        h_in = [sb(f"h_in{i}", [P, GTILES, DIM]) for i in range(2)]
        a_in = [sb(f"a_in{i}", [P, GTILES, DIM]) for i in range(2)]
        y_buf = [sb(f"y_buf{i}", [P, GTILES, DIM]) for i in range(2)]
        stats = sb("stats2", [P, GTILES, 6])
        meanvar = sb("meanvar2", [P, GTILES, 2])
        var_eps = sb("var_eps2", [P, GTILES])
        rstd = sb("rstd2", [P, GTILES])
        xn = sb("xn2", [P, GTILES, 2, P])
        xt = sb("xt2", [P, 2, GT])
        xh = [sb(f"xh{i}", [P, 2, GT], BF16) for i in range(2)]
        xl = [sb(f"xl{i}", [P, GT], BF16) for i in range(2)]
        xe = [sb(f"xe{i}", [HI + 3, GT], BF16) for i in range(2)]
        rh = sb("rh", [P, 2, GT])
        score = sb("score", [P, GTILES, EXPERTS])
        best = sb("best", [P, GTILES, 1])
        top = sb("top", [P, GTILES, 8])
        top_at = sb("top_at", [P, GTILES, 8], U32)
        top_id = sb("top_id", [P, GTILES, 8])
        chosen = sb("chosen", [P, GTILES, EXPERTS])
        less_top = sb("less_top", [P, GTILES, EXPERTS])
        expd = sb("expd", [P, GTILES, EXPERTS])
        kept = sb("kept", [P, GTILES, EXPERTS])
        total = sb("total", [P, GTILES, 1])
        share = sb("share", [P, GTILES, 1])
        gate = [sb(f"gate{i}", [P, GTILES, EXPERTS]) for i in range(2)]
        gate_t = sb("gate_t", [EXPERTS, GT])
        mh = [sb(f"mh{i}", [P, 2, GT], BF16) for i in range(MID)]
        ml = [sb(f"ml{i}", [P, 2, GT], BF16) for i in range(MID)]
        acc = [sb(f"acc{i}", [P, GTILES, DIM]) for i in range(2)]

        mid_bank = [ps(f"mid_bank{i}", [P, 2, GT]) for i in range(MID)]
        y_bank = [ps(f"y_bank{i}", [P, GTILES, 256]) for i in range(2)]
        x_bank = ps("x_bank", [P, 2, GT])
        r_bank = ps("r_bank", [P, 2, GT])

        small_in = sem("small_in")
        b1_in = sem("b1_in")
        b1_parts_ready = sem("b1_parts_ready")
        b1_parts_stored = sem("b1_parts_stored")
        bias_in = sem("bias_in")
        stage_in = [sem(f"stage_in{i}") for i in range(2)]
        w_hi_ready = sem("w_hi_ready")
        w_lo_ready = sem("w_lo_ready")
        consts_set = sem("consts_set2")
        rows_in = [sem(f"rows_in{i}") for i in range(2)]
        y_ready = sem("y_ready")
        stats_ready = sem("stats_ready2")
        meanvar_ready = sem("meanvar_ready2")
        var_ready = sem("var_ready2")
        rstd_ready = sem("rstd_ready2")
        xn_ready = sem("xn_ready2")
        xt_ps_ready = sem("xt_ps_ready")
        xt_ready = sem("xt_ready")
        xh_ready = sem("xh_ready")
        xl_ready = sem("xl_ready")
        r1_ready = sem("r1_ready")
        rh_ready = sem("rh_ready")
        score_ps_ready = sem("score_ps_ready")
        routed = sem("routed")
        expd_ready = sem("expd_ready")
        gate_ready = sem("gate_ready")
        gate_ps_ready = sem("gate_ps_ready")
        gate_t_ready = sem("gate_t_ready")
        mid_ready = sem("mid_ready")
        mh_ready = sem("mh_ready")
        ml_ready = sem("ml_ready")
        mixed_in = sem("mixed_in")
        y_bias_ready = sem("y_bias_ready")
        ye_taken = sem("ye_taken")
        out_stored = [sem(f"out_stored{i}") for i in range(2)]

        SMALL = [(r1_a, wr1_a), (r1_b, wr1_b), (r1_bias, br1), (r2_a, wr2_a), (r2_b, wr2_b), (r2_bias, br2), (b2_sb, b2),
                 (ids, expert_ids), (ident, ident_in)]
        YU = 1 + EXPERTS
        ROUTE_OPS = 12
        CONSTS = 4

        block = ctx.enter_context(nc.Block())

        def run_groups(eng, group):
            for q in range(2):
                group(0, q)
            with eng.Fori(1, FGROUPS // 2) as body:
                for q in range(2):
                    group(body, q)
            group(FGROUPS // 2, 0)

        def in_range(g):
            return not isinstance(g, int) or g < FGROUPS

        def rows(dram, g):
            return dram[bass.ds(g, 1)].rearrange("o (p j) e -> p (o j) e", p=P)

        @block.sync
        def _(sp):
            sp.dma_start(b1_rows[:], b1).then_inc(b1_in, 16)
            for dst, src in SMALL:
                sp.dma_start(dst[:], src).then_inc(small_in, 16)

            def load_rows(body, q):
                g = 2 * body + q
                if in_range(g):
                    wait(sp, y_ready, g - 1)
                    sp.dma_start(h_in[q][:], rows(h_dram, g)).then_inc(rows_in[q], 16)
                    sp.dma_start(a_in[q][:], rows(att_dram, g)).then_inc(rows_in[q], 16)

            def load_expert(e):
                if e >= 2:
                    sp.wait_ge(w_lo_ready, 3 * (e - 1))
                i = e % 2
                sp.dma_start(stage_a[i][:], w1_a[:, e]).then_inc(stage_in[i], 16)
                sp.dma_start(stage_b[i][:], w1_b[:, e]).then_inc(stage_in[i], 16)
                sp.dma_start(stage_2[i][:], w2[:, e]).then_inc(stage_in[i], 16)

            load_expert(0)
            load_expert(1)
            sp.wait_ge(b1_parts_ready, 5)
            sp.dma_start(b1_parts.rearrange("r (c f) -> c r f", f=P), b1_split[:]).then_inc(b1_parts_stored, 16)
            sp.wait_ge(b1_parts_stored, 16)
            sp.dma_start(w1l_b[HI:HI + 3].rearrange("r e f -> r (e f)"), b1_parts).then_inc(bias_in, 16)
            load_rows(0, 0)
            load_rows(0, 1)
            for e in range(2, EXPERTS):
                load_expert(e)

            def group(body, q):
                g = 2 * body + q
                if not isinstance(g, int) or g > 0:
                    load_rows(body + q, 1 - q)
                sp.wait_ge(ye_taken, YU * (g + 1))
                sp.dma_start(rows(out, g), acc[q][:]).then_inc(out_stored[q], 16)
            run_groups(sp, group)
            sp.wait_ge(out_stored[0], 16 * ((FGROUPS + 1) // 2))
            sp.wait_ge(out_stored[1], 16 * (FGROUPS // 2))

        @block.tensor
        def _(pe):
            pe.wait_ge(small_in, 16 * len(SMALL))
            pe.wait_ge(bias_in, 16)

            def transpose_x(body, q):
                g = 2 * body + q
                if in_range(g):
                    pe.wait_ge(xn_ready, g + 1)
                    wait(pe, routed, ROUTE_OPS * (g - 1) + 1)
                    for b in range(2):
                        for j in range(GTILES):
                            last = nc.tensor.transpose(x_bank[:, b, j * P:(j + 1) * P], xn[:, j, b, :], ident[:])
                    last.then_inc(xt_ps_ready, 1)

            def router_hidden(body, q):
                g = 2 * body + q
                if in_range(g):
                    pe.wait_ge(xt_ready, g + 1)
                    wait(pe, gate_t_ready, g)
                    for b, (f0, nf) in enumerate(((0, P), (P, HI))):
                        nc.tensor.matmul(r_bank[0:nf, b, :], r1_a[:, f0:f0 + nf], xt[:, 0, :], start=True, stop=False)
                        last = nc.tensor.matmul(r_bank[0:nf, b, :], r1_b[:, f0:f0 + nf], xt[0:HI, 1, :], start=False,
                                                stop=True)
                    last.then_inc(r1_ready, 1)

            def router_scores(body, q):
                g = 2 * body + q
                if in_range(g):
                    pe.wait_ge(rh_ready, 2 * (g + 1))
                    pe.wait_ge(xh_ready, 3 * (g + 1))
                    for j in range(GTILES):
                        cols = slice(j * P, (j + 1) * P)
                        nc.tensor.matmul(x_bank[:, 0, j * 8:(j + 1) * 8], rh[:, 0, cols], r2_a[:], start=True,
                                         stop=False)
                        last = nc.tensor.matmul(x_bank[:, 0, j * 8:(j + 1) * 8], rh[0:HI, 1, cols], r2_b[:],
                                                start=False, stop=True)
                    last.then_inc(score_ps_ready, 1)

            def transpose_gates(body, q):
                g = 2 * body + q
                if in_range(g):
                    pe.wait_ge(gate_ready, g + 1)
                    for j in range(GTILES):
                        last = nc.tensor.transpose(r_bank[0:EXPERTS, 0, j * P:(j + 1) * P], gate[q][:, j, :], ident[:])
                    last.then_inc(gate_ps_ready, 1)

            def gated_bias(g, q):
                pe.wait_ge(gate_t_ready, g + 1)
                use, bank = YU * g, y_bank[q * YU % 2]
                wait(pe, ye_taken, use - 1)
                for j in range(GTILES):
                    last = nc.tensor.matmul(bank[:, j, 0:DIM], gate_t[:, j * P:(j + 1) * P], b2_sb[:], start=True,
                                            stop=True)
                last.then_inc(y_bias_ready, 1)

            def hidden(g, q, n):
                e, c0 = n // UNITS, 2 * (n % UNITS)
                if n % UNITS == 0:
                    pe.wait_ge(w_hi_ready, 3 * (e + 1))
                    pe.wait_ge(w_lo_ready, 3 * (e + 1))
                if n == 0:
                    pe.wait_ge(xl_ready, 2 * (g + 1))
                    pe.wait_ge(xh_ready, 3 * (g + 1))
                wait(pe, ml_ready, EU * g + n - MID + 1)
                for c in range(2):
                    f = slice((c0 + c) * P, (c0 + c + 1) * P)
                    o = mid_bank[n % MID][:, c, :]
                    nc.tensor.matmul(o, w1h_a[:, e, f], xh[q][:, 0, :], start=True, stop=False)
                    nc.tensor.matmul(o, w1h_a[:, e, f], xl[q][:], start=False, stop=False)
                    nc.tensor.matmul(o, w1l_a[:, e, f], xh[q][:, 0, :], start=False, stop=False)
                    nc.tensor.matmul(o, w1h_b[:, e, f], xh[q][:, 1, :], start=False, stop=False)
                    last = nc.tensor.matmul(o, w1l_b[:, e, f], xe[q][:], start=False, stop=True)
                last.then_inc(mid_ready, 1)

            def project(g, q, n):
                e, c0 = n // UNITS, 2 * (n % UNITS)
                use, bank = YU * g + 1 + e, y_bank[(q * YU + 1 + e) % 2]
                pe.wait_ge(ml_ready, EU * g + n + 1)
                if n % UNITS == 0:
                    wait(pe, ye_taken, use - 1)
                for j in range(GTILES):
                    cols = slice(j * P, (j + 1) * P)
                    for c in range(2):
                        first = n % UNITS == 0 and c == 0 and j == 0
                        end = n % UNITS == UNITS - 1 and c == 1
                        o = bank[:, j, 0:DIM]
                        nc.tensor.matmul(o, mh[n % MID][:, c, cols], w2h[:, e, c0 + c, :], start=first, stop=False,
                                         skip_group_check=True)
                        nc.tensor.matmul(o, mh[n % MID][:, c, cols], w2l[:, e, c0 + c, :], start=False, stop=False,
                                         skip_group_check=True)
                        last = nc.tensor.matmul(o, ml[n % MID][:, c, cols], w2h[:, e, c0 + c, :], start=False,
                                                stop=end, skip_group_check=True)
                last.then_inc(mixed_in, 1)

            def group(body, q):
                g = 2 * body + q
                nxt = (body + q, 1 - q)
                gated_bias(g, q)
                for n in range(EU):
                    if n == 7:
                        transpose_x(*nxt)
                    elif n == 10:
                        router_hidden(*nxt)
                    elif n == 13:
                        router_scores(*nxt)
                    elif n == 19:
                        transpose_gates(*nxt)
                    hidden(g, q, n)
                    if n >= LAG:
                        project(g, q, n - LAG)
                for n in range(EU - LAG, EU):
                    project(g, q, n)

            transpose_x(0, 0)
            router_hidden(0, 0)
            router_scores(0, 0)
            transpose_gates(0, 0)
            run_groups(pe, group)

        @block.vector
        def _(dve):
            def b1_split_op(ins, n):
                ins.then_inc(b1_parts_ready, 1)
                dve.wait_ge(b1_parts_ready, n)

            dve.wait_ge(b1_in, 16)
            b1_split_op(nc.vector.tensor_copy(b1_split[:, 0], b1_rows[:]), 1)
            b1_split_op(nc.vector.tensor_tensor(b1_rest[0][:], b1_rows[:], b1_split[:, 0], ALU.subtract), 2)
            b1_split_op(nc.vector.tensor_copy(b1_split[:, 1], b1_rest[0][:]), 3)
            b1_split_op(nc.vector.tensor_tensor(b1_rest[1][:], b1_rest[0][:], b1_split[:, 1], ALU.subtract), 4)
            b1_split_op(nc.vector.tensor_copy(b1_split[:, 2], b1_rest[1][:]), 5)
            for i in range(2):
                nc.vector.memset(xe[i][HI:HI + 3, :], 1.0).then_inc(consts_set, 1)
            nc.vector.memset(minus_half[:], -0.5).then_inc(consts_set, 1)
            nc.vector.memset(eps[:], EPS).then_inc(consts_set, 1)

            def split_low(e):
                i = e % 2
                dve.wait_ge(w_hi_ready, 3 * (e + 1))
                nc.vector.tensor_tensor(w1l_a[:, e], stage_a[i][:], w1h_a[:, e], ALU.subtract).then_inc(w_lo_ready, 1)
                nc.vector.tensor_tensor(w1l_b[0:HI, e], stage_b[i][0:HI], w1h_b[0:HI, e], ALU.subtract
                                        ).then_inc(w_lo_ready, 1)
                nc.vector.tensor_tensor(w2l[:, e], stage_2[i][:], w2h[:, e], ALU.subtract).then_inc(w_lo_ready, 1)

            def statistics(body, q):
                g = 2 * body + q
                if in_range(g):
                    dve.wait_ge(y_ready, g + 1)
                    for j in range(GTILES):
                        nc.vector.bn_stats(stats[:, j, :], y_buf[q][:, j, :]).then_inc(stats_ready, 1)
                    dve.wait_ge(stats_ready, GTILES * (g + 1))
                    wait(dve, rstd_ready, g)
                    nc.vector.memset(spacer[:], 0.0)
                    for j in range(GTILES):
                        nc.vector.bn_aggr(meanvar[:, j, :], stats[:, j, :]).then_inc(meanvar_ready, 1)

            def layernorm(body, q):
                g = 2 * body + q
                if in_range(g):
                    dve.wait_ge(rstd_ready, g + 1)
                    wait(dve, xt_ps_ready, g)
                    for j in range(GTILES):
                        for b, f0, c0, nf in ((0, 0, 0, P), (1, P, 0, HI), (1, P, HI, HI)):
                            last = nc.vector.tensor_scalar(xn[:, j, b, c0:c0 + nf], y_buf[q][:, j, f0:f0 + nf],
                                                           meanvar[:, j, 0:1], rstd[:, j:j + 1],
                                                           ALU.subtract, ALU.mult)
                    last.then_inc(xn_ready, 1)

            def split_x(body, q):
                g = 2 * body + q
                if in_range(g):
                    dve.wait_ge(xt_ready, g + 1)
                    dve.wait_ge(xh_ready, 3 * (g + 1))
                    wait(dve, mid_ready, EU * (g - 1))
                    nc.vector.tensor_tensor(xl[q][:], xt[:, 0, :], xh[q][:, 0, :], ALU.subtract).then_inc(xl_ready, 1)
                    low = xh[q][HI:P, 1, :]
                    nc.vector.tensor_tensor(low, xt[HI:P, 1, :], low, ALU.subtract).then_inc(xl_ready, 1)

            def route(body, q):
                g = 2 * body + q
                if in_range(g):
                    dve.wait_ge(score_ps_ready, g + 1)
                    nc.vector.tensor_tensor(score[:], x_bank[:, 0, 0:GTILES * 8].rearrange(
                        "p (j e) -> p j e", j=GTILES), r2_bias[:], ALU.add).then_inc(routed, 1)
                    dve.wait_ge(routed, ROUTE_OPS * g + 1)
                    nc.vector.reduce_max(best[:], score[:], AX.X).then_inc(routed, 1)
                    for j in range(GTILES):
                        nc.vector.max(top[:, j, :], score[:, j, :]).then_inc(routed, 1)
                    dve.wait_ge(routed, ROUTE_OPS * g + 4)
                    wait(dve, expd_ready, 4 * g)
                    nc.vector.tensor_tensor(less_top[:], score[:], best[:].to_broadcast([P, GTILES, EXPERTS]),
                                            ALU.subtract).then_inc(routed, 1)
                    for j in range(GTILES):
                        nc.vector.max_index(top_at[:, j, :], top[:, j, :], score[:, j, :]).then_inc(routed, 1)
                    dve.wait_ge(routed, ROUTE_OPS * g + 7)
                    nc.vector.tensor_copy(top_id[:], top_at[:]).then_inc(routed, 1)
                    dve.wait_ge(routed, ROUTE_OPS * g + 8)
                    for j in range(GTILES):
                        nc.vector.tensor_scalar(chosen[:, j, :], ids[:], top_id[:, j, 0:1], None, ALU.is_equal
                                                ).then_inc(routed, 1)
                    dve.wait_ge(routed, ROUTE_OPS * g + 10)
                    for j in range(GTILES):
                        nc.vector.scalar_tensor_tensor(chosen[:, j, :], ids[:], top_id[:, j, 1:2], chosen[:, j, :],
                                                       ALU.is_equal, ALU.add).then_inc(routed, 1)

            def gates(body, q):
                g = 2 * body + q
                if in_range(g):
                    dve.wait_ge(expd_ready, 4 * g + 1)
                    dve.wait_ge(routed, ROUTE_OPS * (g + 1))
                    nc.vector.tensor_tensor(kept[:], expd[:], chosen[:], ALU.mult).then_inc(expd_ready, 1)
                    dve.wait_ge(expd_ready, 4 * g + 2)
                    nc.vector.reduce_sum(total[:], kept[:], AX.X).then_inc(expd_ready, 1)
                    dve.wait_ge(expd_ready, 4 * g + 3)
                    nc.vector.reciprocal(share[:], total[:]).then_inc(expd_ready, 1)
                    dve.wait_ge(expd_ready, 4 * g + 4)
                    nc.vector.tensor_tensor(gate[q][:], kept[:], share[:].to_broadcast([P, GTILES, EXPERTS]),
                                            ALU.mult).then_inc(gate_ready, 1)

            def take_bias(g, q, body):
                dve.wait_ge(y_bias_ready, g + 1)
                wait(dve, ye_taken, YU * g)
                wait(dve, out_stored[q], 16 * body)
                nc.vector.tensor_tensor(acc[q][:], y_bank[q * YU % 2][:, :, 0:DIM], y_buf[q][:], ALU.add
                                        ).then_inc(ye_taken, 1)

            def take_expert(g, q, e):
                dve.wait_ge(mixed_in, EU * g + (e + 1) * UNITS)
                dve.wait_ge(ye_taken, YU * g + 1 + e)
                for j in range(GTILES):
                    last = nc.vector.scalar_tensor_tensor(acc[q][:, j, :], y_bank[(q * YU + 1 + e) % 2][:, j, 0:DIM],
                                                          gate[q][:, j, e:e + 1], acc[q][:, j, :], ALU.mult, ALU.add)
                last.then_inc(ye_taken, 1)

            def take_low(g, n):
                dve.wait_ge(mh_ready, EU * g + n + 1)
                wait(dve, mixed_in, EU * g + n - MID + 1)
                nc.vector.scalar_tensor_tensor(ml[n % MID][:], mid_bank[n % MID][:], 0.0, mh[n % MID][:],
                                               ALU.max, ALU.subtract).then_inc(ml_ready, 1)

            def group(body, q):
                g = 2 * body + q
                nxt = (body + q, 1 - q)
                take_bias(g, q, body)
                for n in range(EU):
                    if isinstance(g, int) and g == 0 and n % UNITS == 0:
                        split_low(n // UNITS)
                    take_low(g, n)
                    e = (n - LAG - UNITS + 1) // UNITS
                    if n >= LAG + UNITS and (n - LAG) % UNITS == 0:
                        take_expert(g, q, e)
                    if n == 2:
                        statistics(*nxt)
                    elif n == 4:
                        layernorm(*nxt)
                    elif n == 8:
                        split_x(*nxt)
                    elif n == 13:
                        route(*nxt)
                    elif n == 16:
                        gates(*nxt)
                take_expert(g, q, EXPERTS - 1)

            dve.wait_ge(small_in, 16 * len(SMALL))
            statistics(0, 0)
            layernorm(0, 0)
            split_x(0, 0)
            route(0, 0)
            gates(0, 0)
            run_groups(dve, group)

        @block.scalar
        def _(act):
            act.wait_ge(small_in, 16 * len(SMALL))

            def split_high(e):
                i = e % 2
                act.wait_ge(stage_in[i], 48 * (e // 2 + 1))
                nc.scalar.copy(w1h_a[:, e], stage_a[i][:]).then_inc(w_hi_ready, 1)
                nc.scalar.copy(w1h_b[:, e], stage_b[i][:]).then_inc(w_hi_ready, 1)
                nc.scalar.copy(w2h[:, e], stage_2[i][:]).then_inc(w_hi_ready, 1)

            def take_xt(body, q):
                g = 2 * body + q
                if in_range(g):
                    act.wait_ge(xt_ps_ready, g + 1)
                    wait(act, r1_ready, g)
                    wait(act, xl_ready, 2 * g)
                    nc.scalar.copy(xt[:], x_bank[:]).then_inc(xt_ready, 1)
                    wait(act, mid_ready, EU * (g - 1))
                    for b in range(2):
                        nc.scalar.copy(xh[q][:, b, :], x_bank[:, b, :]).then_inc(xh_ready, 1)
                    nc.scalar.copy(xe[q][0:HI, :], x_bank[0:HI, 1, :]).then_inc(xh_ready, 1)

            def router_relu(body, q):
                g = 2 * body + q
                if in_range(g):
                    act.wait_ge(r1_ready, g + 1)
                    wait(act, score_ps_ready, g)
                    for b, nf in enumerate((P, HI)):
                        nc.scalar.activation(rh[0:nf, b, :], r_bank[0:nf, b, :], ACT.Relu, bias=r1_bias[0:nf, b:b + 1]
                                             ).then_inc(rh_ready, 1)

            def exponentials(body, q):
                g = 2 * body + q
                if in_range(g):
                    act.wait_ge(routed, ROUTE_OPS * g + 5)
                    nc.scalar.activation(expd[:], less_top[:], ACT.Exp).then_inc(expd_ready, 1)

            def take_gates(body, q):
                g = 2 * body + q
                if in_range(g):
                    act.wait_ge(gate_ps_ready, g + 1)
                    wait(act, y_bias_ready, g)
                    nc.scalar.copy(gate_t[:], r_bank[0:EXPERTS, 0, :]).then_inc(gate_t_ready, 1)

            def take_high(g, n):
                act.wait_ge(mid_ready, EU * g + n + 1)
                wait(act, mixed_in, EU * g + n - MID + 1)
                nc.scalar.activation(mh[n % MID][:], mid_bank[n % MID][:], ACT.Relu).then_inc(mh_ready, 1)

            def group(body, q):
                g = 2 * body + q
                nxt = (body + q, 1 - q)
                for n in range(EU):
                    if isinstance(g, int) and g == 0 and n % UNITS == 0 and n // UNITS + 2 < EXPERTS:
                        split_high(n // UNITS + 2)
                    take_high(g, n)
                    if n == 6:
                        take_xt(*nxt)
                    elif n == 10:
                        router_relu(*nxt)
                    elif n == 14:
                        exponentials(*nxt)
                    elif n == 19:
                        take_gates(*nxt)

            split_high(0)
            split_high(1)
            take_xt(0, 0)
            router_relu(0, 0)
            exponentials(0, 0)
            take_gates(0, 0)
            run_groups(act, group)

        @block.gpsimd
        def _(pool):
            pool.wait_ge(consts_set, CONSTS)

            def sum_rows(body, q):
                g = 2 * body + q
                if in_range(g):
                    pool.wait_ge(rows_in[q], 32 * (body + 1))
                    wait(pool, ye_taken, YU * (g - 2) + 1)
                    nc.gpsimd.tensor_tensor(y_buf[q][:], h_in[q][:], a_in[q][:], ALU.add).then_inc(y_ready, 1)

            def inverse_deviation(body, q):
                g = 2 * body + q
                if in_range(g):
                    pool.wait_ge(meanvar_ready, GTILES * (g + 1))
                    nc.gpsimd.tensor_tensor(var_eps[:], meanvar[:, :, 1], eps[:], ALU.add).then_inc(var_ready, 1)
                    pool.wait_ge(var_ready, g + 1)
                    wait(pool, xn_ready, g)
                    nc.gpsimd.tensor_tensor(rstd[:], var_eps[:], minus_half[:], ALU.pow).then_inc(rstd_ready, 1)

            def prepare(body, q):
                sum_rows(body, q)
                inverse_deviation(body, q)

            prepare(0, 0)
            run_groups(pool, lambda body, q: prepare(body + q, 1 - q))


def build(nc, x_t, w_tok, w_qk_a, w_qk_b, w_v_a, w_v_b, b_tok, b_qk, b_v, ln_cols, row_consts, ident, w1_a, w1_b, w2, b1,
          wr1_a, wr1_b, br1, wr2_a, wr2_b, br2, b2, expert_ids, out):
    h_rows = nc.dram_tensor("h_rows", (PAIRS, TILES, HALF, DIM), F32).ap()
    att_rows = nc.dram_tensor("att_rows", (PAIRS, TILES, HALF, DIM), F32).ap()
    b1_parts = nc.dram_tensor("b1_parts", (3, EXPERTS * HIDDEN), BF16).ap()
    attention_phase(nc, x_t, w_tok, w_qk_a, w_qk_b, w_v_a, w_v_b, b_tok, b_qk, b_v, ln_cols, row_consts, ident,
                    h_rows, att_rows)

    def by_group(t):
        return t.rearrange("u c p e -> (u c p) e").rearrange("(g t) e -> g t e", t=GT)

    expert_phase(nc, by_group(h_rows), by_group(att_rows), w1_a, w1_b, w2, b1, wr1_a, wr1_b, br1, wr2_a, wr2_b, br2, b2,
                 expert_ids, ident, b1_parts, out.rearrange("(g t) e -> g t e", t=GT))


def layout(x, L0_tok_W, L0_tok_b, L0_attn_qkv_w, L0_attn_qkv_b, L0_attn_ln_g, L0_attn_ln_b, L0_ffn_W1, L0_ffn_b1,
           L0_ffn_W2, L0_ffn_b2, L0_ffn_Wr1, L0_ffn_br1, L0_ffn_Wr2, L0_ffn_br2):
    import numpy as np

    x = np.asarray(x).reshape(IMAGES, 3, 14, 16, 14, 16).transpose(0, 1, 2, 4, 5, 3)
    x = x.reshape(PAIRS, COLS, PCH, P).transpose(0, 3, 2, 1)
    order = np.arange(2 * DIM).reshape(2 * GROUPS, HG, 1, HEAD_DIM)
    order = np.broadcast_to(order, (2 * GROUPS, HG, 2, HEAD_DIM)).reshape(2 * GROUPS, P)
    qkv_w, qkv_b = np.asarray(L0_attn_qkv_w), np.asarray(L0_attn_qkv_b)
    w_qk = qkv_w[order].transpose(2, 0, 1)
    w_v = qkv_w[2 * DIM:].T
    g, b = np.asarray(L0_attn_ln_g), np.asarray(L0_attn_ln_b)
    ln_cols = np.stack([g[:P], b[:P], np.tile(g[P:], 2), np.tile(b[P:], 2)], axis=1)
    row_consts = np.zeros((P, 2 + HG), np.float32)
    tilde = np.arange(P) % ROWS >= HEAD_DIM
    row_consts[:, 0] = np.where(tilde, -BETA * SCALE, (1.0 + BETA) * SCALE)
    row_consts[:, 1] = tilde
    for hh in range(HG):
        row_consts[ROWS * hh:ROWS * hh + 2, 2 + hh] = -1.0
    w1 = np.asarray(L0_ffn_W1).transpose(2, 0, 1)
    w2 = np.asarray(L0_ffn_W2).reshape(EXPERTS, DIM, FCH, P).transpose(3, 0, 2, 1)
    wr1, wr2 = np.asarray(L0_ffn_Wr1).T, np.asarray(L0_ffn_Wr2).T
    br1 = np.asarray(L0_ffn_br1)
    return {
        "x_t": x,
        "w_tok": np.asarray(L0_tok_W).T.reshape(PCH, P, DIM).transpose(1, 0, 2),
        "w_qk_a": w_qk[:P], "w_qk_b": np.concatenate([w_qk[P:], w_qk[P:]]),
        "w_v_a": w_v[:P], "w_v_b": np.concatenate([w_v[P:], w_v[P:]]),
        "b_tok": np.tile(np.asarray(L0_tok_b), (HALF, 1)),
        "b_qk": qkv_b[order].T,
        "b_v": np.tile(qkv_b[2 * DIM:], (HALF, 1)),
        "ln_cols": ln_cols, "row_consts": row_consts, "ident": np.eye(P, dtype=np.float32),
        "w1_a": w1[:P], "w1_b": np.concatenate([w1[P:], w1[P:]]), "w2": w2,
        "b1": np.asarray(L0_ffn_b1).reshape(EXPERTS * FCH, P),
        "wr1_a": wr1[:P], "wr1_b": wr1[P:],
        "br1": np.stack([br1[:P], np.tile(br1[P:], 2)], axis=1),
        "wr2_a": wr2[:P], "wr2_b": wr2[P:],
        "br2": np.tile(np.asarray(L0_ffn_br2), (P, GTILES, 1)),
        "b2": np.asarray(L0_ffn_b2),
        "expert_ids": np.tile(np.arange(EXPERTS, dtype=np.float32), (P, 1)),
    }


def kernel(**inputs):
    import numpy as np
    import concourse.bacc as bacc
    from concourse.bass_utils import run_bass_kernel_spmd

    nc = bacc.Bacc("TRN2", target_bir_lowering=False, num_devices=1)
    arrays, args = {}, {}
    for name, a in layout(**inputs).items():
        a = np.ascontiguousarray(a)
        arrays[f"in_{name}"] = a
        args[name] = nc.dram_tensor(f"in_{name}", a.shape, mybir.dt.from_np(a.dtype), kind="ExternalInput").ap()
    out = nc.dram_tensor("out_rows", (IMAGES * TOKENS, DIM), F32, kind="ExternalOutput").ap()
    build(nc, out=out, **args)
    result = run_bass_kernel_spmd(nc, [arrays], core_ids=[0])
    return result.results[0]["out_rows"].reshape(IMAGES, TOKENS, DIM)
```

```python
from contextlib import ExitStack

import concourse.bass as bass
from concourse import mybir

F32 = mybir.dt.float32
F16 = mybir.dt.float16
BF16 = mybir.dt.bfloat16
U32 = mybir.dt.uint32
ALU = mybir.AluOpType
ACT = mybir.ActivationFunctionType
AX = mybir.AxisListType

P = 128
IMAGES = 64
TOKENS = 196
DIM = 192
HI = DIM - P
PATCH_DIM = 768
PCH = PATCH_DIM // P
HEADS = 12
HEAD_DIM = 16
HG = 4
GROUPS = HEADS // HG
ROWS = 2 * HEAD_DIM
HALF = TOKENS // 2
PAIR = 2
PAIRS = IMAGES // PAIR
COLS = PAIR * TOKENS
TILES = PAIR * 2
STEPS = GROUPS * PAIR
ALL_STEPS = PAIRS * STEPS
BETA = 0.2
EPS = 1e-5
SCALE = HEAD_DIM ** -0.5
PW = TOKENS + 2
PARTS = 3 * ROWS
STACK = PARTS + 2 * HG
MAX_SCALE = 64.0
W_SCALE = 2.0 ** 10

BODY_PAIRS = 2
BODY_STEPS = BODY_PAIRS * STEPS
BODIES = PAIRS // BODY_PAIRS
DRAIN = 3

EXPERTS = 8
HIDDEN = 768
FCH = HIDDEN // P
UNITS = FCH // 2
GT = 256
GTILES = GT // P
FGROUPS = IMAGES * TOKENS // GT
EU = EXPERTS * UNITS
LAG = 2
MID = 4
GATE_BLOCKS = 3
STAGES = 4


def wait(eng, sem, value):
    if not isinstance(value, int) or value > 0:
        eng.wait_ge(sem, value)


class Step:

    def __init__(self, body, kk, ahead):
        k = kk + ahead
        self.s = body * BODY_STEPS + k
        self.pair = body * BODY_PAIRS + k // STEPS
        self.there = not isinstance(body, int) or 0 <= self.s < ALL_STEPS
        self.q = (k // STEPS) % 2
        self.odd = k % 2
        self.group = k % GROUPS
        self.image = (k // GROUPS) % PAIR
        self.first = k % STEPS == 0
        self.before = body + (k // STEPS) // 2


class Pair:

    def __init__(self, body, kk, ahead):
        k = kk // STEPS + ahead
        self.u = body * BODY_PAIRS + k
        self.there = not isinstance(body, int) or 0 <= self.u < PAIRS
        self.q = k % 2
        self.before = body + k // 2


def run_bodies(eng, step):
    step(0, -1)
    for kk in range(BODY_STEPS):
        step(0, kk)
    with eng.Fori(1, BODIES - 1) as body:
        for kk in range(BODY_STEPS):
            step(body, kk)
    for kk in range(BODY_STEPS + DRAIN):
        step(BODIES - 1, kk)


def attention_phase(nc, x_t, w_tok, w_qk_a, w_qk_b, w_v_a, w_v_b, b_tok, b_qk, b_v, ln_cols, row_consts, ident_in,
                    h_dram, att_dram):
    ctx = ExitStack()
    with ctx:
        def sb(name, shape, dt=F32):
            return ctx.enter_context(nc.sbuf_tensor(name, shape, dt))

        def ps(name, shape, dt=F32):
            return ctx.enter_context(nc.psum_tensor(name, shape, dt))

        def sem(name):
            return ctx.enter_context(nc.semaphore(name))

        wtok = sb("wtok", [P, PCH, DIM])
        wtok_h = sb("wtok_h", [P, PCH, DIM], F16)
        wtok_l = sb("wtok_l", [P, PCH, DIM], F16)
        wqk_a = sb("wqk_a", [P, 2 * GROUPS, P])
        wqk_b = sb("wqk_b", [P, 2 * GROUPS, P])
        wv_a = sb("wv_a", [P, DIM])
        wv_b = sb("wv_b", [P, DIM])
        wqk_ah = sb("wqk_ah", [P, 2 * GROUPS, P], BF16)
        wqk_al = sb("wqk_al", [P, 2 * GROUPS, P], BF16)
        wqk_bh = sb("wqk_bh", [P, 2 * GROUPS, P], BF16)
        wqk_bl = sb("wqk_bl", [HI, 2 * GROUPS, P], BF16)
        wv_ah = sb("wv_ah", [P, DIM], BF16)
        wv_al = sb("wv_al", [P, DIM], BF16)
        wv_bh = sb("wv_bh", [P, DIM], BF16)
        wv_bl = sb("wv_bl", [HI, DIM], BF16)
        btok = sb("btok", [HALF, DIM])
        bqk = sb("bqk", [P, 2 * GROUPS])
        bq_scaled = sb("bq_scaled", [P, GROUPS])
        bv = sb("bv", [HALF, DIM])
        lnc = sb("lnc", [P, 4])
        rowc = sb("rowc", [P, 2 + HG])
        ident = sb("ident", [P, P])
        ident16 = sb("ident16", [P, P], F16)
        minus_half = sb("minus_half", [HALF, TILES])
        one_eps = sb("one_eps", [HALF, TILES])
        eps_sq = sb("eps_sq", [HALF, TILES])
        spacer = sb("spacer", [HALF, 1])
        x_buf = [sb(f"x_buf{i}", [P, PCH, COLS]) for i in range(2)]
        x_hi = sb("x_hi", [P, PCH, COLS], F16)
        x_lo = sb("x_lo", [P, PCH, COLS], F16)
        h_buf = sb("h_buf", [HALF, TILES, DIM])
        stats = sb("stats", [HALF, TILES, 6])
        meanvar = sb("meanvar", [HALF, TILES, 2])
        var_eps = [sb(f"var_eps{i}", [HALF, TILES]) for i in range(2)]
        rstd = sb("rstd", [HALF, TILES])
        centred = sb("centred", [HALF, TILES, DIM])
        xn = sb("xn", [HALF, TILES, 2, P])
        xt_a = sb("xt_a", [P, COLS])
        xt_b = sb("xt_b", [P, COLS])
        x_ah = sb("x_ah", [P, COLS], BF16)
        x_al = sb("x_al", [P, COLS], BF16)
        x_b = sb("x_b", [P, COLS], BF16)
        padded = sb("padded", [P, 2 * GROUPS * PAIR, PW])
        beside = sb("beside", [P, 2 * GROUPS * PAIR, TOKENS])
        qk = sb("qk", [P, 2 * GROUPS * PAIR, TOKENS])
        qk_hi = sb("qk_hi", [P, 2 * GROUPS * PAIR, TOKENS], F16)
        qk_lo = sb("qk_lo", [P, 2 * GROUPS * PAIR, TOKENS], F16)
        q_stack = [sb(f"q_stack{i}", [STACK, HEADS, PAIR * TOKENS], F16) for i in range(2)]
        k_stack = [sb(f"k_stack{i}", [STACK, HEADS, PAIR * TOKENS], F16) for i in range(2)]
        v_buf = [sb(f"v_buf{i}", [HALF, TILES, HEADS, 32]) for i in range(2)]
        row_max = [sb(f"row_max{i}", [HALF, 2, HG]) for i in range(2)]
        max_parts = [sb(f"max_parts{i}", [HALF, 2, P], F16) for i in range(2)]
        probs = [sb(f"probs{i}", [HALF, HG, 2, TOKENS]) for i in range(2)]
        mixed = [sb(f"mixed{i}", [P, TOKENS]) for i in range(2)]
        recip = sb("recip", [HALF, 2, HG, 1])
        att = [sb(f"att{i}", [HALF, TILES, DIM]) for i in range(2)]

        s_bank = [ps(f"s_bank{i}", [P, 2, 256]) for i in range(2)]
        t_bank = [ps(f"t_bank{i}", [P, 2, 256]) for i in range(2)]
        o_bank = ps("o_bank", [P, 512])
        m_bank = ps("m_bank", [P, 512])
        p_bank = [ps(f"p_bank{i}", [P, 512]) for i in range(2)]
        back_tr = m_bank[0:HALF, 0:2 * P].rearrange("p (u h d) -> p u h d", u=2, h=HG)
        max_tr = m_bank[:, 2 * P:512].bitcast(F16).rearrange("p (u n) -> p u n", u=2)

        max_weights_set = sem("max_weights_set")
        wtok_in = sem("wtok_in")
        weights_in = sem("weights_in")
        consts_set = sem("consts_set")
        x_in = [sem(f"x_in{i}") for i in range(2)]
        wtok_split = sem("wtok_split")
        x_hi_ready = sem("x_hi_ready")
        x_lo_ready = [sem(f"x_lo_ready{i}") for i in range(2)]
        p_ready = [sem(f"p_ready{i}") for i in range(2)]
        h_ready = sem("h_ready")
        h_stored = sem("h_stored")
        stats_ready = sem("stats_ready")
        meanvar_ready = sem("meanvar_ready")
        var_ready = sem("var_ready")
        rstd_ready = sem("rstd_ready")
        centred_ready = sem("centred_ready")
        xn_ready = sem("xn_ready")
        xt_a_ready = sem("xt_a_ready")
        xt_b_ready = sem("xt_b_ready")
        x_high = sem("x_high")
        x_split = sem("x_split")
        v_ready = sem("v_ready")
        padded_ready = sem("padded_ready")
        beside_ready = sem("beside_ready")
        qk_ready = sem("qk_ready")
        hi_ready = sem("hi_ready")
        lo_ready = sem("lo_ready")
        q_stacked = sem("q_stacked")
        k_stacked = sem("k_stacked")
        s_ready = sem("s_ready")
        max_ready = sem("max_ready")
        max_hi_ready = sem("max_hi_ready")
        max_parts_ready = sem("max_parts_ready")
        max_tr_ready = sem("max_tr_ready")
        max_rows_ready = sem("max_rows_ready")
        t_ready = sem("t_ready")
        probs_ready = sem("probs_ready")
        o_ready = sem("o_ready")
        mixed_ready = sem("mixed_ready")
        back_ready = sem("back_ready")
        recip_ready = sem("recip_ready")
        att_ready = sem("att_ready")
        att_stored = [sem(f"att_stored{i}") for i in range(2)]

        LOADS = [(wqk_a, w_qk_a), (wqk_b, w_qk_b), (wv_a, w_v_a), (wv_b, w_v_b), (btok, b_tok),
                 (bqk, b_qk), (bv, b_v), (lnc, ln_cols), (rowc, row_consts), (ident, ident_in)]
        STACKED = 16 * 3 * HG
        USES = 6

        def patch_uses(u):
            return 1 if isinstance(u, int) and u == 0 else USES * u

        def v_uses(u):
            return USES * PAIRS if isinstance(u, int) and u == PAIRS - 1 else USES * u + USES + 1
        CONSTS = 10 + 2 + 8

        block = ctx.enter_context(nc.Block())

        @block.sync
        def _(sp):
            def load_x(pr):
                if pr.there:
                    if not isinstance(pr.u, int) or pr.u >= 2:
                        sp.wait_ge(p_ready[1], patch_uses(pr.u - 2))
                    sp.dma_start(x_buf[pr.q][:], x_t[bass.ds(pr.u, 1)].rearrange("o p c n -> (o p) c n")
                                 ).then_inc(x_in[pr.q], 16)

            def stack(pr, which):
                if pr.there:
                    dst = (q_stack, k_stack)[which][pr.q]
                    tiles = slice(which * GROUPS * PAIR, (which + 1) * GROUPS * PAIR)
                    for part, ready, blocks in ((qk_hi, hi_ready, ((0, 2), (0, 1))[which]),
                                                (qk_lo, lo_ready, ((1,), (2,))[which])):
                        sp.wait_ge(ready, 2 * pr.u + which + 1)
                        for r in blocks:
                            for hh in range(HG):
                                sp.dma_start(dst[32 * r:32 * r + 32, hh::HG, :],
                                             part[32 * hh:32 * hh + 32, tiles, :].rearrange(
                                                 "p (g i) n -> p g (i n)", i=PAIR)
                                             ).then_inc((q_stacked, k_stacked)[which], 16)

            def rows(dram, pr):
                return dram[bass.ds(pr.u, 1)].rearrange("o c p e -> p (o c) e")

            def store_h(pr):
                if pr.there:
                    sp.wait_ge(h_ready, 2 * pr.u + 2)
                    sp.dma_start(rows(h_dram, pr), h_buf[:]).then_inc(h_stored, 16)

            def store_att(pr):
                if pr.there:
                    sp.wait_ge(att_ready, (pr.u + 1) * STEPS)
                    sp.dma_start(rows(att_dram, pr), att[pr.q][:]).then_inc(att_stored[pr.q], 16)

            def step(body, kk):
                k = kk % STEPS
                if kk == -1:
                    sp.dma_start(wtok[:], w_tok).then_inc(wtok_in, 16)
                    load_x(Pair(0, 0, 0))
                    for dst, src in LOADS:
                        sp.dma_start(dst[:], src).then_inc(weights_in, 16)
                    load_x(Pair(0, 0, 1))
                    store_h(Pair(0, 0, 0))
                    stack(Pair(0, 0, 0), 0)
                    stack(Pair(0, 0, 0), 1)
                    store_h(Pair(0, 0, 1))
                elif k == 0:
                    load_x(Pair(body, kk, 2))
                elif k == 1:
                    stack(Pair(body, kk, 1), 0)
                    stack(Pair(body, kk, 1), 1)
                elif k == 2:
                    store_att(Pair(body, kk, -1))
                elif k == 4:
                    store_h(Pair(body, kk, 2))
            run_bodies(sp, step)
            sp.wait_ge(h_stored, 16 * PAIRS)
            for i in range(2):
                sp.wait_ge(att_stored[i], 16 * PAIRS // 2)

        @block.tensor
        def _(pe):
            pe.wait_ge(wtok_split, 2)

            def project_patches(pr, half, c):
                if pr.there:
                    if c == 0:
                        wait(pe, padded_ready, 2 * GROUPS * (pr.u - 1) + 5 + half)
                    tile = 2 * half + c
                    pe.wait_ge(x_lo_ready[half], 2 * pr.u + c + 1)
                    tokens = slice(tile * HALF, (tile + 1) * HALF)
                    out = p_bank[half][0:HALF, c * DIM:(c + 1) * DIM]
                    for f in range(PCH):
                        nc.tensor.matmul(out, x_hi[:, f, tokens], wtok_h[:, f, :], start=(f == 0), stop=False)
                        nc.tensor.matmul(out, x_hi[:, f, tokens], wtok_l[:, f, :], start=False, stop=False)
                        ins = nc.tensor.matmul(out, x_lo[:, f, tokens], wtok_h[:, f, :], start=False,
                                               stop=(f == PCH - 1))
                    if c == 1:
                        ins.then_inc(p_ready[half], 1)

            def claim(pr, n):
                if n < 2:
                    wait(pe, v_ready, PAIR * (pr.u - 1) + n + 1)
                elif n < 4:
                    pe.wait_ge((xt_a_ready, xt_b_ready)[n - 2], pr.u + 1)
                else:
                    pe.wait_ge(padded_ready, 2 * GROUPS * pr.u + n - 3)
                return p_bank[n % 2], p_ready[n % 2]

            def transpose_xn(pr, n):
                if pr.there:
                    if n == 0:
                        pe.wait_ge(xn_ready, pr.u + 1)
                    bank, ready = claim(pr, n)
                    for c in range(TILES):
                        last = nc.tensor.transpose(bank[:, c * HALF:(c + 1) * HALF], xn[:, c, n, :],
                                                   ident[0:HALF, 0:HALF])
                    last.then_inc(ready, 1)

            def project_qk(pr, i):
                if pr.there:
                    if i == 0:
                        pe.wait_ge(x_split, 4 * (pr.u + 1))
                    bank, ready = claim(pr, 2 + i)
                    out = bank[:, 0:COLS]
                    nc.tensor.matmul(out, wqk_ah[:, i, :], x_ah[:], start=True, stop=False)
                    nc.tensor.matmul(out, wqk_ah[:, i, :], x_al[:], start=False, stop=False)
                    nc.tensor.matmul(out, wqk_al[:, i, :], x_ah[:], start=False, stop=False)
                    nc.tensor.matmul(out, wqk_bh[:, i, :], x_b[:], start=False, stop=False)
                    nc.tensor.matmul(out, wqk_bl[:, i, :], x_b[0:HI, :], start=False, stop=True).then_inc(ready, 1)

            def project_v(pr, im, tiles):
                if pr.there and tiles[0] == 0:
                    if isinstance(pr.u, int) and pr.u == PAIRS - 1:
                        pe.wait_ge(padded_ready, 2 * GROUPS * pr.u + 5 + im)
                    else:
                        pe.wait_ge(h_ready, 2 * (pr.u + 1) + im + 1)
                if pr.there:
                    for c in tiles:
                        t0 = (2 * im + c) * HALF
                        tokens = slice(t0, t0 + HALF)
                        out = p_bank[im][0:HALF, c * DIM:(c + 1) * DIM]
                        nc.tensor.matmul(out, x_ah[:, tokens], wv_ah[:], start=True, stop=False)
                        nc.tensor.matmul(out, x_ah[:, tokens], wv_al[:], start=False, stop=False)
                        nc.tensor.matmul(out, x_al[:, tokens], wv_ah[:], start=False, stop=False)
                        nc.tensor.matmul(out, x_b[:, tokens], wv_bh[:], start=False, stop=False)
                        last = nc.tensor.matmul(out, x_b[0:HI, tokens], wv_bl[:], start=False, stop=True)
                    if c == 1:
                        last.then_inc(p_ready[im], 1)

            def transpose_back(st):
                if st.there:
                    pe.wait_ge(mixed_ready, st.s + 1)
                    pe.wait_ge(max_rows_ready, min(st.s + 3, ALL_STEPS) if isinstance(st.s, int) else st.s + 3)
                    wait(pe, att_ready, st.s)
                    for u in range(2):
                        last = nc.tensor.transpose(m_bank[0:HALF, u * P:(u + 1) * P],
                                                   mixed[st.odd][:, u * HALF:(u + 1) * HALF], ident[:])
                    last.then_inc(back_ready, 1)

            def head_cols(st, u=None):
                t0 = st.image * TOKENS + (0 if u is None else u * HALF)
                return slice(t0, t0 + (TOKENS if u is None else HALF))

            def scores(st, heads):
                if st.there:
                    if st.first and heads[0] == 0:
                        pe.wait_ge(q_stacked, (st.pair + 1) * STACKED)
                        pe.wait_ge(k_stacked, (st.pair + 1) * STACKED)
                    for hh in heads:
                        head = HG * st.group + hh
                        wait(pe, max_ready, HG * st.s + hh - 1)
                        for u in range(2):
                            last = nc.tensor.matmul(s_bank[hh % 2][0:HALF, u, 0:TOKENS],
                                                    q_stack[st.q][0:PARTS, head, head_cols(st, u)],
                                                    k_stack[st.q][0:PARTS, head, head_cols(st)],
                                                    start=True, stop=True)
                        last.then_inc(s_ready, 1)

            def scores_less_max(st, heads):
                if st.there:
                    if heads[0] == 0:
                        pe.wait_ge(max_rows_ready, st.s + 1)
                    for hh in heads:
                        head = HG * st.group + hh
                        wait(pe, probs_ready, HG * st.s + hh - 1)
                        for v in range(2):
                            out = t_bank[hh % 2][0:HALF, v, 0:TOKENS]
                            last = nc.tensor.matmul(out, k_stack[st.q][:, head, head_cols(st, v)],
                                                    q_stack[st.q][:, head, head_cols(st)], start=True, stop=True)
                        last.then_inc(t_ready, 1)

            def mix(st):
                if st.there:
                    pe.wait_ge(probs_ready, HG * (st.s + 1))
                    if st.first:
                        pe.wait_ge(v_ready, PAIR * (st.pair + 1))
                    wait(pe, mixed_ready, st.s)
                    for v in range(2):
                        for hh in range(HG):
                            last = nc.tensor.matmul(o_bank[32 * hh:32 * hh + 32, 0:TOKENS],
                                                    v_buf[st.q][:, 2 * st.image + v, HG * st.group + hh, :],
                                                    probs[st.odd][:, hh, v, :], start=(v == 0), stop=(v == 1))
                    last.then_inc(o_ready, 1)

            def transpose_max(st):
                if st.there:
                    pe.wait_ge(max_parts_ready, st.s + 1)
                    wait(pe, att_ready, st.s - 2)
                    for u in range(2):
                        last = nc.tensor.transpose(max_tr[:, u, 0:HALF], max_parts[st.odd][:, u, :],
                                                   ident16[0:HALF, 0:HALF])
                    last.then_inc(max_tr_ready, 1)

            def before_max(body, kk):
                k = kk % STEPS
                if k == 0:
                    project_qk(Pair(body, kk, 1), 3)
                    project_qk(Pair(body, kk, 1), 4)
                elif k in (1, 2):
                    project_patches(Pair(body, kk, 2), k - 1, 0)
                elif k == 3:
                    project_v(Pair(body, kk, 1), 0, (0, 1))
                elif k == 4:
                    project_v(Pair(body, kk, 1), 1, (1,))
                    transpose_xn(Pair(body, kk, 2), 0)
                elif k == 5:
                    project_qk(Pair(body, kk, 2), 0)
                    project_qk(Pair(body, kk, 2), 1)

            def after_max(body, kk):
                k = kk % STEPS
                if k == 0:
                    project_qk(Pair(body, kk, 1), 5)
                elif k in (1, 2):
                    project_patches(Pair(body, kk, 2), k - 1, 1)
                elif k == 3:
                    project_v(Pair(body, kk, 1), 1, (0,))
                elif k == 4:
                    transpose_xn(Pair(body, kk, 2), 1)
                elif k == 5:
                    project_qk(Pair(body, kk, 2), 2)

            def fill_pipeline():
                first, second = Pair(0, 0, 0), Pair(0, 0, 1)
                for pr in (first, second):
                    for half in range(2):
                        for c in range(2):
                            project_patches(pr, half, c)
                    if pr is first:
                        pe.wait_ge(weights_in, 16 * len(LOADS))
                        pe.wait_ge(consts_set, CONSTS)
                    else:
                        project_v(first, 0, (0, 1))
                        project_v(first, 1, (0, 1))
                    transpose_xn(pr, 0)
                    transpose_xn(pr, 1)
                    for i in range(2 * GROUPS if pr is first else GROUPS):
                        project_qk(pr, i)
                pe.wait_ge(max_weights_set, 2 * HG)

            def step(body, kk):
                if kk == -1:
                    fill_pipeline()
                scores(Step(body, kk, 1), (0, 1))
                mix(Step(body, kk, -1))
                transpose_back(Step(body, kk, -2))
                scores_less_max(Step(body, kk, 0), (0, 1))
                scores(Step(body, kk, 1), (2, 3))
                scores_less_max(Step(body, kk, 0), (2, 3))
                if kk >= 0:
                    before_max(body, kk)
                transpose_max(Step(body, kk, 1))
                if kk >= 0:
                    after_max(body, kk)
            run_bodies(pe, step)

        @block.vector
        def _(dve):
            dve.wait_ge(wtok_in, 16)
            nc.vector.tensor_scalar(wtok_h[:], wtok[:], W_SCALE, None, ALU.mult).then_inc(wtok_split, 1)
            dve.wait_ge(wtok_split, 1)
            nc.vector.scalar_tensor_tensor(wtok_l[:], wtok[:], W_SCALE, wtok_h[:], ALU.mult, ALU.subtract
                                           ).then_inc(wtok_split, 1)

            def split_patches(pr, tile):
                if pr.there:
                    cols = slice(tile * HALF, (tile + 1) * HALF)
                    dve.wait_ge(x_hi_ready, TILES * pr.u + tile + 1)
                    nc.vector.tensor_tensor(x_lo[:, :, cols], x_buf[pr.q][:, :, cols], x_hi[:, :, cols], ALU.subtract
                                            ).then_inc(x_lo_ready[0], 1)

            for tile in range(2):
                split_patches(Pair(0, 0, 0), tile)
            for i in range(2):
                nc.vector.memset(v_buf[i][:], 0.0).then_inc(consts_set, 1)
                nc.vector.memset(max_parts[i][:], 0.0).then_inc(consts_set, 1)
            nc.vector.memset(padded[:], 0.0).then_inc(consts_set, 1)
            nc.vector.memset(minus_half[:], -0.5).then_inc(consts_set, 1)
            nc.vector.memset(one_eps[:], 1.0 + EPS).then_inc(consts_set, 1)
            nc.vector.memset(eps_sq[:], EPS * EPS).then_inc(consts_set, 1)
            dve.wait_ge(consts_set, 8)
            for i in range(2):
                nc.vector.memset(v_buf[i][:, :, :, HEAD_DIM:HEAD_DIM + 1], 1.0).then_inc(consts_set, 1)
            dve.wait_ge(weights_in, 16 * len(LOADS))
            nc.vector.tensor_scalar(bq_scaled[:], bqk[:, 0:GROUPS], rowc[:, 0:1], None, ALU.mult
                                    ).then_inc(consts_set, 1)
            nc.vector.tensor_copy(ident16[:], ident[:]).then_inc(consts_set, 1)
            parts = ((wqk_a, wqk_ah, wqk_al, P), (wqk_b, wqk_bh, wqk_bl, HI), (wv_a, wv_ah, wv_al, P),
                     (wv_b, wv_bh, wv_bl, HI))
            for whole, high, low, n in parts:
                nc.vector.tensor_copy(high[:], whole[:]).then_inc(consts_set, 1)
            dve.wait_ge(consts_set, CONSTS - 4)
            for whole, high, low, n in parts:
                nc.vector.tensor_tensor(low[:], whole[0:n], high[0:n], ALU.subtract).then_inc(consts_set, 1)

            def row_maxima(st, heads):
                if st.there:
                    for hh in heads:
                        dve.wait_ge(s_ready, HG * st.s + hh + 1)
                        nc.vector.reduce_max(row_max[st.odd][:, :, hh:hh + 1], s_bank[hh % 2][0:HALF, :, 0:TOKENS],
                                             AX.X).then_inc(max_ready, 1)

            def split_maxima(st):
                if st.there:
                    dve.wait_ge(max_ready, HG * (st.s + 1))
                    wait(dve, max_tr_ready, st.s - 1)
                    parts = max_parts[st.odd][:, :, PARTS:STACK].rearrange("p u (h r) -> p u h r", h=HG)
                    nc.vector.tensor_scalar(parts[:, :, :, 0], row_max[st.odd][:], 1.0 / MAX_SCALE, None, ALU.mult
                                            ).then_inc(max_hi_ready, 1)
                    dve.wait_ge(max_hi_ready, st.s + 1)
                    nc.vector.scalar_tensor_tensor(parts[:, :, :, 1], row_max[st.odd][:], 1.0 / MAX_SCALE,
                                                   parts[:, :, :, 0], ALU.mult, ALU.subtract
                                                   ).then_inc(max_parts_ready, 1)

            def normalise(st):
                if st.there:
                    dve.wait_ge(back_ready, st.s + 1)
                    wait(dve, att_ready, st.s)
                    if st.first:
                        wait(dve, att_stored[st.q], 16 * st.before)
                    nc.vector.reciprocal(recip[:], back_tr[:, :, :, HEAD_DIM:HEAD_DIM + 1]).then_inc(recip_ready, 1)
                    dve.wait_ge(recip_ready, st.s + 1)
                    width = HG * HEAD_DIM
                    out = att[st.q][:, 2 * st.image:2 * st.image + 2, st.group * width:(st.group + 1) * width]
                    nc.vector.tensor_tensor(out.rearrange("p u (h d) -> p u h d", h=HG),
                                            back_tr[:, :, :, 0:HEAD_DIM],
                                            recip[:].to_broadcast([HALF, 2, HG, HEAD_DIM]), ALU.mult
                                            ).then_inc(att_ready, 1)

            def take_h(pr, half):
                if pr.there:
                    dve.wait_ge(p_ready[half], patch_uses(pr.u))
                    if half == 0:
                        wait(dve, h_stored, 16 * pr.u)
                        wait(dve, xn_ready, pr.u)
                    h2 = h_buf[:, 2 * half:2 * half + 2, :]
                    nc.vector.scalar_tensor_tensor(
                        h2, p_bank[half][0:HALF, 0:2 * DIM].rearrange("p (c e) -> p c e", c=2), 1.0 / W_SCALE,
                        btok[:].unsqueeze(1).to_broadcast([HALF, 2, DIM]), ALU.mult, ALU.add).then_inc(h_ready, 1)

            def statistics(pr, half):
                if pr.there:
                    dve.wait_ge(h_ready, 2 * pr.u + half + 1)
                    for c in (2 * half, 2 * half + 1):
                        nc.vector.bn_stats(stats[:, c, :], h_buf[:, c, :]).then_inc(stats_ready, 1)
                    if half == 1:
                        dve.wait_ge(stats_ready, TILES * (pr.u + 1))
                        wait(dve, rstd_ready, pr.u)
                        nc.vector.memset(spacer[:], 0.0)
                        for c in range(TILES):
                            nc.vector.bn_aggr(meanvar[:, c, :], stats[:, c, :]).then_inc(meanvar_ready, 1)

            def take_xt_a(pr):
                if pr.there:
                    dve.wait_ge(p_ready[0], USES * pr.u + 2)
                    wait(dve, x_split, 4 * pr.u)
                    nc.vector.tensor_scalar(xt_a[:], p_bank[0][:, 0:COLS], lnc[:, 0:1], lnc[:, 1:2], ALU.mult, ALU.add
                                            ).then_inc(xt_a_ready, 1)

            def split_low(pr):
                if pr.there:
                    dve.wait_ge(x_high, 2 * (pr.u + 1))
                    nc.vector.tensor_tensor(x_al[:], xt_a[:], x_ah[:], ALU.subtract).then_inc(x_split, 2)
                    nc.vector.tensor_tensor(x_b[HI:P, :], xt_b[HI:P, :], x_b[HI:P, :], ALU.subtract
                                            ).then_inc(x_split, 2)

            def take_v(pr, im):
                if pr.there:
                    if im == 0:
                        wait(dve, o_ready, STEPS * (pr.u - 1))
                    dve.wait_ge(p_ready[im], v_uses(pr.u))
                    out = v_buf[pr.q][:, 2 * im:2 * im + 2, :, 0:HEAD_DIM]
                    nc.vector.tensor_tensor(
                        out, p_bank[im][0:HALF, 0:2 * DIM].rearrange("p (c h d) -> p c h d", c=2, h=HEADS),
                        bv[:].rearrange("p (h d) -> p h d", h=HEADS).unsqueeze(1)
                        .to_broadcast([HALF, 2, HEADS, HEAD_DIM]), ALU.add).then_inc(v_ready, 1)

            def add_tilde(pr, which):
                if pr.there:
                    tiles = slice(which * GROUPS * PAIR, (which + 1) * GROUPS * PAIR)
                    dve.wait_ge(beside_ready, 2 * pr.u + which + 1)
                    wait(dve, lo_ready, 2 * pr.u + which - 1)
                    nc.vector.scalar_tensor_tensor(qk[:, tiles, :], beside[:, tiles, :], rowc[:, 1:2],
                                                   padded[:, tiles, 1:TOKENS + 1], ALU.mult, ALU.add
                                                   ).then_inc(qk_ready, 1)

            def fill_pipeline():
                first, second = Pair(0, 0, 0), Pair(0, 0, 1)
                for pr in (first, second):
                    if pr is second:
                        for tile in range(2):
                            split_patches(pr, tile)
                    for half in range(2):
                        take_h(pr, half)
                        statistics(pr, half)
                    if pr is second:
                        take_v(first, 0)
                        take_v(first, 1)
                    take_xt_a(pr)
                    split_low(pr)
                    if pr is first:
                        add_tilde(pr, 0)
                        add_tilde(pr, 1)

            def step(body, kk):
                k = kk % STEPS
                if kk == -1:
                    fill_pipeline()
                row_maxima(Step(body, kk, 1), (0, 1))
                normalise(Step(body, kk, -2))
                if kk >= 0:
                    if k == 1:
                        split_patches(Pair(body, kk, 2), 1)
                    elif k == 2:
                        take_h(Pair(body, kk, 2), 0)
                    elif k == 3:
                        statistics(Pair(body, kk, 2), 1)
                    elif k == 5:
                        split_low(Pair(body, kk, 2))
                row_maxima(Step(body, kk, 1), (2, 3))
                split_maxima(Step(body, kk, 1))
                if kk >= 0:
                    if k in (0, 1):
                        add_tilde(Pair(body, kk, 1), k)
                        if k == 0:
                            split_patches(Pair(body, kk, 2), 0)
                    elif k == 2:
                        statistics(Pair(body, kk, 2), 0)
                        take_h(Pair(body, kk, 2), 1)
                    elif k == 3:
                        take_v(Pair(body, kk, 1), 0)
                    elif k == 4:
                        take_v(Pair(body, kk, 1), 1)
                        take_xt_a(Pair(body, kk, 2))
            run_bodies(dve, step)

        @block.scalar
        def _(act):
            def high_patches(pr, tile):
                if pr.there:
                    if tile == 0:
                        act.wait_ge(x_in[pr.q], 16 * (pr.before + 1))
                    if not isinstance(pr.u, int) or pr.u > 0:
                        act.wait_ge(p_ready[tile // 2], patch_uses(pr.u - 1))
                    cols = slice(tile * HALF, (tile + 1) * HALF)
                    nc.scalar.copy(x_hi[:, :, cols], x_buf[pr.q][:, :, cols]).then_inc(x_hi_ready, 1)

            for tile in range(TILES):
                high_patches(Pair(0, 0, 0), tile)
            act.wait_ge(weights_in, 16 * len(LOADS))
            for i in range(2):
                for hh in range(HG):
                    nc.scalar.copy(k_stack[i][PARTS:STACK, hh::HG, :],
                                   rowc[PARTS:STACK, 2 + hh:3 + hh].unsqueeze(2).to_broadcast(
                                       [STACK - PARTS, GROUPS, COLS])).then_inc(max_weights_set, 1)
            act.wait_ge(consts_set, CONSTS)

            def exponentials(st, heads):
                if st.there:
                    if heads[0] == 0:
                        wait(act, o_ready, st.s - 1)
                    for hh in heads:
                        act.wait_ge(t_ready, HG * st.s + hh + 1)
                        nc.scalar.activation(probs[st.odd][:, hh], t_bank[hh % 2][0:HALF, :, 0:TOKENS], ACT.Exp
                                             ).then_inc(probs_ready, 1)

            def copy_mixed(st):
                if st.there:
                    act.wait_ge(o_ready, st.s + 1)
                    wait(act, back_ready, st.s - 1)
                    nc.scalar.copy(mixed[st.odd][:], o_bank[:, 0:TOKENS]).then_inc(mixed_ready, 1)

            def copy_max_rows(st):
                if st.there:
                    act.wait_ge(max_tr_ready, st.s + 1)
                    wait(act, t_ready, HG * (st.s - 1))
                    heads = slice(HG * st.group, HG * (st.group + 1))
                    cols = slice(st.image * TOKENS, (st.image + 1) * TOKENS)
                    out = q_stack[st.q][PARTS:STACK, heads, cols].rearrange("p h (u n) -> p h u n", u=2)
                    nc.scalar.copy(out, max_tr[PARTS:STACK, :, 0:HALF].unsqueeze(1)
                                   .to_broadcast([STACK - PARTS, HG, 2, HALF])).then_inc(max_rows_ready, 1)

            def take_xt_b(pr):
                if pr.there:
                    act.wait_ge(p_ready[1], USES * pr.u + 2)
                    wait(act, x_split, 4 * pr.u)
                    nc.scalar.activation(xt_b[:], p_bank[1][:, 0:COLS], ACT.Identity, bias=lnc[:, 3:4],
                                         scale=lnc[:, 2:3]).then_inc(xt_b_ready, 1)

            def split_high(pr):
                if pr.there:
                    act.wait_ge(xt_a_ready, pr.u + 1)
                    nc.scalar.copy(x_ah[:], xt_a[:]).then_inc(x_high, 1)
                    act.wait_ge(xt_b_ready, pr.u + 1)
                    nc.scalar.copy(x_b[:], xt_b[:]).then_inc(x_high, 1)

            def take_qk(pr, i):
                if pr.there:
                    which, n = i // GROUPS, 2 + i
                    if i % GROUPS == 0:
                        wait(act, qk_ready, 2 * pr.u + which - 1)
                    act.wait_ge(p_ready[n % 2], USES * pr.u + 2 + n // 2)
                    out = padded[:, PAIR * i:PAIR * (i + 1), 1:TOKENS + 1]
                    src = p_bank[n % 2][:, 0:COLS].rearrange("p (i n) -> p i n", i=PAIR)
                    if which == 0:
                        ins = nc.scalar.activation(out, src, ACT.Identity, bias=bq_scaled[:, i:i + 1],
                                                   scale=rowc[:, 0:1])
                    else:
                        ins = nc.scalar.activation(out, src, ACT.Identity, bias=bqk[:, i:i + 1])
                    ins.then_inc(padded_ready, 1)

            def take_high(pr, which):
                if pr.there:
                    tiles = slice(which * GROUPS * PAIR, (which + 1) * GROUPS * PAIR)
                    wait(act, t_ready, HG * STEPS * (pr.u - 1))
                    act.wait_ge(qk_ready, 2 * pr.u + which + 1)
                    wait(act, (q_stacked, k_stacked)[which], STACKED * pr.u)
                    nc.scalar.copy(qk_hi[:, tiles, :], qk[:, tiles, :]).then_inc(hi_ready, 1)

            def fill_pipeline():
                for u in range(2):
                    pr = Pair(0, 0, u)
                    if u == 1:
                        for tile in range(TILES):
                            high_patches(pr, tile)
                    take_xt_b(pr)
                    split_high(pr)
                    for i in range((2 - u) * GROUPS):
                        take_qk(pr, i)
                    if u == 0:
                        take_high(pr, 0)
                        take_high(pr, 1)

            def step(body, kk):
                k = kk % STEPS
                if kk == -1:
                    fill_pipeline()
                copy_mixed(Step(body, kk, -1))
                exponentials(Step(body, kk, 0), (0, 1))
                if kk >= 0 and k < 2:
                    high_patches(Pair(body, kk, 2), 2 * k)
                exponentials(Step(body, kk, 0), (2, 3))
                if kk >= 0:
                    if k == 0:
                        take_qk(Pair(body, kk, 1), 3)
                        take_qk(Pair(body, kk, 1), 4)
                    elif k == 2:
                        take_high(Pair(body, kk, 1), 1)
                    elif k == 5:
                        take_qk(Pair(body, kk, 2), 0)
                        take_qk(Pair(body, kk, 2), 1)
                copy_max_rows(Step(body, kk, 1))
                if kk >= 0:
                    if k == 0:
                        take_qk(Pair(body, kk, 1), 5)
                        take_high(Pair(body, kk, 1), 0)
                    if k < 2:
                        high_patches(Pair(body, kk, 2), 2 * k + 1)
                    elif k == 4:
                        take_xt_b(Pair(body, kk, 2))
                        split_high(Pair(body, kk, 2))
                    elif k == 5:
                        take_qk(Pair(body, kk, 2), 2)
            run_bodies(act, step)

        @block.gpsimd
        def _(pool):
            def inverse_deviation(pr):
                if pr.there:
                    pool.wait_ge(meanvar_ready, TILES * (pr.u + 1))
                    wait(pool, rstd_ready, pr.u)
                    nc.gpsimd.tensor_tensor(var_eps[0][:], meanvar[:, :, 1], one_eps[:], ALU.mult
                                            ).then_inc(var_ready, 1)
                    pool.wait_ge(var_ready, 2 * pr.u + 1)
                    nc.gpsimd.tensor_tensor(var_eps[1][:], var_eps[0][:], eps_sq[:], ALU.add).then_inc(var_ready, 1)
                    pool.wait_ge(var_ready, 2 * pr.u + 2)
                    wait(pool, xn_ready, pr.u)
                    nc.gpsimd.tensor_tensor(rstd[:], var_eps[1][:], minus_half[:], ALU.pow).then_inc(rstd_ready, 1)

            def layernorm(pr):
                if pr.there:
                    pool.wait_ge(h_ready, 2 * (pr.u + 1))
                    nc.gpsimd.tensor_tensor(centred[:], h_buf[:], meanvar[:, :, 0:1].to_broadcast([HALF, TILES, DIM]),
                                            ALU.subtract).then_inc(centred_ready, 1)
                    wait(pool, xt_b_ready, pr.u)
                    pool.wait_ge(rstd_ready, pr.u + 1)
                    pool.wait_ge(centred_ready, pr.u + 1)
                    for n, f0, c0, nf in ((0, 0, 0, P), (1, P, 0, HI), (1, P, HI, HI)):
                        ins = nc.gpsimd.tensor_tensor(xn[:, :, n, c0:c0 + nf], centred[:, :, f0:f0 + nf],
                                                      rstd[:].unsqueeze(2).to_broadcast([HALF, TILES, nf]), ALU.mult)
                    ins.then_inc(xn_ready, 1)

            def split_patches(pr):
                if pr.there:
                    for tile in (2, 3):
                        cols = slice(tile * HALF, (tile + 1) * HALF)
                        pool.wait_ge(x_hi_ready, TILES * pr.u + tile + 1)
                        nc.gpsimd.tensor_tensor(x_lo[:, :, cols], x_buf[pr.q][:, :, cols], x_hi[:, :, cols],
                                                ALU.subtract).then_inc(x_lo_ready[1], 1)

            def add_beside(pr, which):
                if pr.there:
                    tiles = slice(which * GROUPS * PAIR, (which + 1) * GROUPS * PAIR)
                    pool.wait_ge(padded_ready, 2 * GROUPS * pr.u + GROUPS * (which + 1))
                    wait(pool, qk_ready, 2 * pr.u + which - 1)
                    nc.gpsimd.tensor_tensor(beside[:, tiles, :], padded[:, tiles, 0:TOKENS], padded[:, tiles, 2:PW],
                                            ALU.add).then_inc(beside_ready, 1)

            def take_low(pr, which):
                if pr.there:
                    tiles = slice(which * GROUPS * PAIR, (which + 1) * GROUPS * PAIR)
                    wait(pool, t_ready, HG * STEPS * (pr.u - 1))
                    pool.wait_ge(hi_ready, 2 * pr.u + which + 1)
                    wait(pool, (q_stacked, k_stacked)[which], STACKED * pr.u)
                    nc.gpsimd.tensor_tensor(qk_lo[:, tiles, :], qk[:, tiles, :], qk_hi[:, tiles, :], ALU.subtract
                                            ).then_inc(lo_ready, 1)

            def step(body, kk):
                k = kk % STEPS
                if kk == -1:
                    first = Pair(0, 0, 0)
                    split_patches(first)
                    pool.wait_ge(consts_set, CONSTS)
                    inverse_deviation(first)
                    layernorm(first)
                    add_beside(first, 0)
                    add_beside(first, 1)
                    take_low(first, 0)
                    take_low(first, 1)
                    split_patches(Pair(0, 0, 1))
                    inverse_deviation(Pair(0, 0, 1))
                    layernorm(Pair(0, 0, 1))
                elif k == 0:
                    add_beside(Pair(body, kk, 1), 0)
                    add_beside(Pair(body, kk, 1), 1)
                    take_low(Pair(body, kk, 1), 0)
                elif k == 1:
                    split_patches(Pair(body, kk, 2))
                    take_low(Pair(body, kk, 1), 1)
                elif k == 3:
                    inverse_deviation(Pair(body, kk, 2))
                    layernorm(Pair(body, kk, 2))
            run_bodies(pool, step)


def expert_phase(nc, h_dram, att_dram, w1_a, w1_b, w2, b1, wr1_a, wr1_b, br1, wr2_a, wr2_b, br2, b2, expert_ids,
                 ident_in, b1_parts, out):
    ctx = ExitStack()
    with ctx:
        def sb(name, shape, dt=F32):
            return ctx.enter_context(nc.sbuf_tensor(name, shape, dt))

        def ps(name, shape, dt=F32):
            return ctx.enter_context(nc.psum_tensor(name, shape, dt))

        def sem(name):
            return ctx.enter_context(nc.semaphore(name))

        w1h_a = sb("w1h_a", [P, EXPERTS, HIDDEN], BF16)
        w1l_a = sb("w1l_a", [P, EXPERTS, HIDDEN], BF16)
        w1h_b = sb("w1h_b", [P, EXPERTS, HIDDEN], BF16)
        w1l_b = sb("w1l_b", [HI + 3, EXPERTS, HIDDEN], BF16)
        w2h = sb("w2h", [P, EXPERTS, FCH, DIM], BF16)
        w2l = sb("w2l", [P, EXPERTS, FCH, DIM], BF16)
        stage_a = [sb(f"stage_a{i}", [P, HIDDEN]) for i in range(STAGES)]
        stage_b = [sb(f"stage_b{i}", [P, HIDDEN]) for i in range(STAGES)]
        stage_2 = [sb(f"stage_2{i}", [P, FCH, DIM]) for i in range(STAGES)]
        b1_rows = sb("b1_rows", [EXPERTS * FCH, P])
        b1_rest = [sb(f"b1_rest{i}", [EXPERTS * FCH, P]) for i in range(2)]
        b1_split = sb("b1_split", [EXPERTS * FCH, 3, P], BF16)
        r1_a = sb("r1_a", [P, DIM])
        r1_b = sb("r1_b", [HI, DIM])
        r1_bias = sb("r1_bias", [P, 2])
        r2_a = sb("r2_a", [P, EXPERTS])
        r2_b = sb("r2_b", [HI, EXPERTS])
        r2_bias = sb("r2_bias", [P, GTILES, EXPERTS])
        b2_in = sb("b2_in", [GATE_BLOCKS * 32, DIM])
        b2_parts = sb("b2_parts", [GATE_BLOCKS * 32, DIM], F16)
        ids = sb("ids", [P, EXPERTS])
        ident = sb("ident2", [P, P])
        minus_half = sb("minus_half2", [P, GTILES])
        eps = sb("eps", [P, GTILES])
        spacer = sb("spacer2", [P, 1])

        h_in = [sb(f"h_in{i}", [P, GTILES, DIM]) for i in range(2)]
        a_in = [sb(f"a_in{i}", [P, GTILES, DIM]) for i in range(2)]
        y_buf = [sb(f"y_buf{i}", [P, GTILES, DIM]) for i in range(2)]
        stats = sb("stats2", [P, GTILES, 6])
        meanvar = sb("meanvar2", [P, GTILES, 2])
        var_eps = sb("var_eps2", [P, GTILES])
        rstd = sb("rstd2", [P, GTILES])
        xn = sb("xn2", [P, GTILES, 2, P])
        xt = sb("xt2", [P, 2, GT])
        xh = [sb(f"xh{i}", [P, 2, GT], BF16) for i in range(2)]
        xl = [sb(f"xl{i}", [P, GT], BF16) for i in range(2)]
        xe = [sb(f"xe{i}", [HI + 3, GT], BF16) for i in range(2)]
        rh = sb("rh", [P, 2, GT])
        score = sb("score", [P, GTILES, EXPERTS])
        best = sb("best", [P, GTILES, 1])
        top = sb("top", [P, GTILES, 8])
        top_at = sb("top_at", [P, GTILES, 8], U32)
        top_id = sb("top_id", [P, GTILES, 8])
        chosen = sb("chosen", [P, GTILES, EXPERTS])
        less_top = sb("less_top", [P, GTILES, EXPERTS])
        expd = sb("expd", [P, GTILES, EXPERTS])
        kept = sb("kept", [P, GTILES, EXPERTS])
        total = sb("total", [P, GTILES, 1])
        share = sb("share", [P, GTILES, 1])
        gate = [sb(f"gate{i}", [P, GTILES, GATE_BLOCKS, 32]) for i in range(2)]
        gate_t = sb("gate_t", [GATE_BLOCKS * 32, GT], F16)
        mh = [sb(f"mh{i}", [P, 2, GT], BF16) for i in range(MID)]
        ml = [sb(f"ml{i}", [P, 2, GT], BF16) for i in range(MID)]
        acc = [sb(f"acc{i}", [P, GTILES, DIM]) for i in range(2)]

        mid_bank = [ps(f"mid_bank{i}", [P, 2, GT]) for i in range(MID)]
        y_bank = [ps(f"y_bank{i}", [P, GTILES, 256]) for i in range(2)]
        x_bank = ps("x_bank", [P, 2, GT])
        r_bank = ps("r_bank", [P, 2, GT])

        small_in = sem("small_in")
        b1_in = sem("b1_in")
        b1_parts_ready = sem("b1_parts_ready")
        b1_parts_stored = sem("b1_parts_stored")
        bias_in = sem("bias_in")
        stage_in = [sem(f"stage_in{i}") for i in range(STAGES)]
        w_hi_ready = sem("w_hi_ready")
        w1_lo_ready = sem("w1_lo_ready")
        w2_lo_ready = sem("w2_lo_ready")
        consts_set = sem("consts_set2")
        rows_in = [sem(f"rows_in{i}") for i in range(2)]
        y_ready = sem("y_ready")
        stats_ready = sem("stats_ready2")
        meanvar_ready = sem("meanvar_ready2")
        var_ready = sem("var_ready2")
        rstd_ready = sem("rstd_ready2")
        xn_ready = sem("xn_ready2")
        xt_ps_ready = sem("xt_ps_ready")
        xt_ready = sem("xt_ready")
        xh_ready = sem("xh_ready")
        xl_ready = sem("xl_ready")
        r1_ready = sem("r1_ready")
        rh_ready = sem("rh_ready")
        score_ps_ready = sem("score_ps_ready")
        routed = sem("routed")
        expd_ready = sem("expd_ready")
        gate_ready = sem("gate_ready")
        gate_ps_ready = sem("gate_ps_ready")
        gate_high_ready = sem("gate_high_ready")
        gate_t_ready = sem("gate_t_ready")
        mid_ready = sem("mid_ready")
        mh_ready = sem("mh_ready")
        ml_ready = sem("ml_ready")
        mixed_in = sem("mixed_in")
        b2_split = sem("b2_split")
        y_bias_ready = sem("y_bias_ready")
        ye_taken = sem("ye_taken")
        out_stored = [sem(f"out_stored{i}") for i in range(2)]

        SMALL = [(r1_a, wr1_a), (r1_b, wr1_b), (r1_bias, br1), (r2_a, wr2_a), (r2_b, wr2_b), (r2_bias, br2), (b2_in, b2),
                 (ids, expert_ids), (ident, ident_in)]
        YU = 1 + EXPERTS
        ROUTE_OPS = 12
        CONSTS = 6

        block = ctx.enter_context(nc.Block())

        def run_groups(eng, group):
            for q in range(2):
                group(0, q)
            with eng.Fori(1, FGROUPS // 2) as body:
                for q in range(2):
                    group(body, q)
            group(FGROUPS // 2, 0)

        def in_range(g):
            return not isinstance(g, int) or g < FGROUPS

        def rows(dram, g):
            return dram[bass.ds(g, 1)].rearrange("o (p j) e -> p (o j) e", p=P)

        @block.sync
        def _(sp):
            def load_rows(body, q):
                g = 2 * body + q
                if in_range(g):
                    wait(sp, y_ready, g - 1)
                    sp.dma_start(h_in[q][:], rows(h_dram, g)).then_inc(rows_in[q], 16)
                    sp.dma_start(a_in[q][:], rows(att_dram, g)).then_inc(rows_in[q], 16)

            def load_expert(e):
                if e >= STAGES:
                    sp.wait_ge(w1_lo_ready, 2 * (e - STAGES + 1))
                    sp.wait_ge(w2_lo_ready, e - STAGES + 1)
                i = e % STAGES
                sp.dma_start(stage_a[i][:], w1_a[:, e]).then_inc(stage_in[i], 16)
                sp.dma_start(stage_b[i][:], w1_b[:, e]).then_inc(stage_in[i], 16)
                sp.dma_start(stage_2[i][:], w2[:, e]).then_inc(stage_in[i], 16)

            load_rows(0, 0)
            sp.dma_start(b1_rows[:], b1).then_inc(b1_in, 16)
            load_expert(0)
            for dst, src in SMALL:
                sp.dma_start(dst[:], src).then_inc(small_in, 16)
            sp.wait_ge(b1_parts_ready, 5)
            sp.dma_start(b1_parts.rearrange("r (c f) -> c r f", f=P), b1_split[:]).then_inc(b1_parts_stored, 16)
            sp.wait_ge(b1_parts_stored, 16)
            sp.dma_start(w1l_b[HI:HI + 3].rearrange("r e f -> r (e f)"), b1_parts).then_inc(bias_in, 16)
            load_expert(1)
            load_rows(0, 1)
            for e in range(2, EXPERTS):
                load_expert(e)

            def group(body, q):
                g = 2 * body + q
                if not isinstance(g, int) or g > 0:
                    load_rows(body + q, 1 - q)
                sp.wait_ge(ye_taken, YU * (g + 1))
                sp.dma_start(rows(out, g), acc[q][:]).then_inc(out_stored[q], 16)
            run_groups(sp, group)
            sp.wait_ge(out_stored[0], 16 * ((FGROUPS + 1) // 2))
            sp.wait_ge(out_stored[1], 16 * (FGROUPS // 2))

        @block.tensor
        def _(pe):
            pe.wait_ge(small_in, 16 * len(SMALL))

            def transpose_x(body, q):
                g = 2 * body + q
                if in_range(g):
                    pe.wait_ge(xn_ready, g + 1)
                    wait(pe, routed, ROUTE_OPS * (g - 1) + 1)
                    for b in range(2):
                        for j in range(GTILES):
                            last = nc.tensor.transpose(x_bank[:, b, j * P:(j + 1) * P], xn[:, j, b, :], ident[:])
                    last.then_inc(xt_ps_ready, 1)

            def router_hidden(body, q):
                g = 2 * body + q
                if in_range(g):
                    pe.wait_ge(xt_ready, g + 1)
                    wait(pe, gate_t_ready, g)
                    for b, (f0, nf) in enumerate(((0, P), (P, HI))):
                        nc.tensor.matmul(r_bank[0:nf, b, :], r1_a[:, f0:f0 + nf], xt[:, 0, :], start=True, stop=False)
                        last = nc.tensor.matmul(r_bank[0:nf, b, :], r1_b[:, f0:f0 + nf], xt[0:HI, 1, :], start=False,
                                                stop=True)
                    last.then_inc(r1_ready, 1)

            def router_scores(body, q):
                g = 2 * body + q
                if in_range(g):
                    pe.wait_ge(rh_ready, 2 * (g + 1))
                    pe.wait_ge(xh_ready, 3 * (g + 1))
                    for j in range(GTILES):
                        cols = slice(j * P, (j + 1) * P)
                        nc.tensor.matmul(x_bank[:, 0, j * 8:(j + 1) * 8], rh[:, 0, cols], r2_a[:], start=True,
                                         stop=False)
                        last = nc.tensor.matmul(x_bank[:, 0, j * 8:(j + 1) * 8], rh[0:HI, 1, cols], r2_b[:],
                                                start=False, stop=True)
                    last.then_inc(score_ps_ready, 1)

            def transpose_gates(body, q):
                g = 2 * body + q
                if in_range(g):
                    pe.wait_ge(gate_ready, g + 1)
                    for j in range(GTILES):
                        last = nc.tensor.transpose(r_bank[0:GATE_BLOCKS * 32, 0, j * P:(j + 1) * P],
                                                   gate[q][:, j].rearrange("p r e -> p (r e)"), ident[:])
                    last.then_inc(gate_ps_ready, 1)

            def gated_bias(g, q):
                pe.wait_ge(gate_t_ready, g + 1)
                use, bank = YU * g, y_bank[q * YU % 2]
                wait(pe, ye_taken, use - 1)
                for j in range(GTILES):
                    last = nc.tensor.matmul(bank[:, j, 0:DIM], gate_t[:, j * P:(j + 1) * P], b2_parts[:], start=True,
                                            stop=True)
                last.then_inc(y_bias_ready, 1)

            def hidden(g, q, n):
                e, c0 = n // UNITS, 2 * (n % UNITS)
                if n % UNITS == 0:
                    pe.wait_ge(w_hi_ready, 3 * (e + 1))
                    pe.wait_ge(w1_lo_ready, 2 * (e + 1))
                if n == 0:
                    pe.wait_ge(bias_in, 16)
                    pe.wait_ge(xl_ready, 2 * (g + 1))
                    pe.wait_ge(xh_ready, 3 * (g + 1))
                wait(pe, ml_ready, EU * g + n - MID + 1)
                for c in range(2):
                    f = slice((c0 + c) * P, (c0 + c + 1) * P)
                    o = mid_bank[n % MID][:, c, :]
                    nc.tensor.matmul(o, w1h_a[:, e, f], xh[q][:, 0, :], start=True, stop=False)
                    nc.tensor.matmul(o, w1h_a[:, e, f], xl[q][:], start=False, stop=False)
                    nc.tensor.matmul(o, w1l_a[:, e, f], xh[q][:, 0, :], start=False, stop=False)
                    nc.tensor.matmul(o, w1h_b[:, e, f], xh[q][:, 1, :], start=False, stop=False)
                    last = nc.tensor.matmul(o, w1l_b[:, e, f], xe[q][:], start=False, stop=True)
                last.then_inc(mid_ready, 1)

            def project(g, q, n):
                e, c0 = n // UNITS, 2 * (n % UNITS)
                use, bank = YU * g + 1 + e, y_bank[(q * YU + 1 + e) % 2]
                pe.wait_ge(ml_ready, EU * g + n + 1)
                if n % UNITS == 0:
                    wait(pe, ye_taken, use - 1)
                    pe.wait_ge(w2_lo_ready, e + 1)
                for j in range(GTILES):
                    cols = slice(j * P, (j + 1) * P)
                    for c in range(2):
                        first = n % UNITS == 0 and c == 0 and j == 0
                        end = n % UNITS == UNITS - 1 and c == 1
                        o = bank[:, j, 0:DIM]
                        nc.tensor.matmul(o, mh[n % MID][:, c, cols], w2h[:, e, c0 + c, :], start=first, stop=False,
                                         skip_group_check=True)
                        nc.tensor.matmul(o, mh[n % MID][:, c, cols], w2l[:, e, c0 + c, :], start=False, stop=False,
                                         skip_group_check=True)
                        last = nc.tensor.matmul(o, ml[n % MID][:, c, cols], w2h[:, e, c0 + c, :], start=False,
                                                stop=end, skip_group_check=True)
                last.then_inc(mixed_in, 1)

            def group(body, q):
                g = 2 * body + q
                nxt = (body + q, 1 - q)
                gated_bias(g, q)
                for n in range(EU):
                    if n == 7:
                        transpose_x(*nxt)
                    elif n == 10:
                        router_hidden(*nxt)
                    elif n == 13:
                        router_scores(*nxt)
                    elif n == 19:
                        transpose_gates(*nxt)
                    hidden(g, q, n)
                    if n >= LAG:
                        project(g, q, n - LAG)
                for n in range(EU - LAG, EU):
                    project(g, q, n)

            transpose_x(0, 0)
            router_hidden(0, 0)
            router_scores(0, 0)
            transpose_gates(0, 0)
            pe.wait_ge(b2_split, 2)
            run_groups(pe, group)

        @block.vector
        def _(dve):
            def b1_split_op(ins, n):
                ins.then_inc(b1_parts_ready, 1)
                dve.wait_ge(b1_parts_ready, n)

            dve.wait_ge(b1_in, 16)
            b1_split_op(nc.vector.tensor_copy(b1_split[:, 0], b1_rows[:]), 1)
            b1_split_op(nc.vector.tensor_tensor(b1_rest[0][:], b1_rows[:], b1_split[:, 0], ALU.subtract), 2)
            b1_split_op(nc.vector.tensor_copy(b1_split[:, 1], b1_rest[0][:]), 3)
            b1_split_op(nc.vector.tensor_tensor(b1_rest[1][:], b1_rest[0][:], b1_split[:, 1], ALU.subtract), 4)
            b1_split_op(nc.vector.tensor_copy(b1_split[:, 2], b1_rest[1][:]), 5)
            for i in range(2):
                nc.vector.memset(xe[i][HI:HI + 3, :], 1.0).then_inc(consts_set, 1)
            nc.vector.memset(minus_half[:], -0.5).then_inc(consts_set, 1)
            nc.vector.memset(eps[:], EPS).then_inc(consts_set, 1)
            for i in range(2):
                nc.vector.memset(gate[i][:], 0.0).then_inc(consts_set, 1)

            def split_low(e):
                i = e % STAGES
                dve.wait_ge(w_hi_ready, 3 * (e + 1))
                nc.vector.tensor_tensor(w1l_a[:, e], stage_a[i][:], w1h_a[:, e], ALU.subtract).then_inc(w1_lo_ready, 1)
                nc.vector.tensor_tensor(w1l_b[0:HI, e], stage_b[i][0:HI], w1h_b[0:HI, e], ALU.subtract
                                        ).then_inc(w1_lo_ready, 1)

            def statistics(body, q):
                g = 2 * body + q
                if in_range(g):
                    dve.wait_ge(y_ready, g + 1)
                    for j in range(GTILES):
                        nc.vector.bn_stats(stats[:, j, :], y_buf[q][:, j, :]).then_inc(stats_ready, 1)
                    dve.wait_ge(stats_ready, GTILES * (g + 1))
                    wait(dve, rstd_ready, g)
                    nc.vector.memset(spacer[:], 0.0)
                    for j in range(GTILES):
                        nc.vector.bn_aggr(meanvar[:, j, :], stats[:, j, :]).then_inc(meanvar_ready, 1)

            def layernorm(body, q):
                g = 2 * body + q
                if in_range(g):
                    dve.wait_ge(rstd_ready, g + 1)
                    wait(dve, xt_ps_ready, g)
                    for j in range(GTILES):
                        for b, f0, c0, nf in ((0, 0, 0, P), (1, P, 0, HI), (1, P, HI, HI)):
                            last = nc.vector.tensor_scalar(xn[:, j, b, c0:c0 + nf], y_buf[q][:, j, f0:f0 + nf],
                                                           meanvar[:, j, 0:1], rstd[:, j:j + 1],
                                                           ALU.subtract, ALU.mult)
                    last.then_inc(xn_ready, 1)

            def split_x(body, q):
                g = 2 * body + q
                if in_range(g):
                    dve.wait_ge(xt_ready, g + 1)
                    dve.wait_ge(xh_ready, 3 * (g + 1))
                    wait(dve, mid_ready, EU * (g - 1))
                    nc.vector.tensor_tensor(xl[q][:], xt[:, 0, :], xh[q][:, 0, :], ALU.subtract).then_inc(xl_ready, 1)
                    low = xh[q][HI:P, 1, :]
                    nc.vector.tensor_tensor(low, xt[HI:P, 1, :], low, ALU.subtract).then_inc(xl_ready, 1)

            def route(body, q):
                g = 2 * body + q
                if in_range(g):
                    dve.wait_ge(score_ps_ready, g + 1)
                    nc.vector.tensor_tensor(score[:], x_bank[:, 0, 0:GTILES * 8].rearrange(
                        "p (j e) -> p j e", j=GTILES), r2_bias[:], ALU.add).then_inc(routed, 1)
                    dve.wait_ge(routed, ROUTE_OPS * g + 1)
                    nc.vector.reduce_max(best[:], score[:], AX.X).then_inc(routed, 1)
                    for j in range(GTILES):
                        nc.vector.max(top[:, j, :], score[:, j, :]).then_inc(routed, 1)
                    dve.wait_ge(routed, ROUTE_OPS * g + 4)
                    wait(dve, expd_ready, 4 * g)
                    nc.vector.tensor_tensor(less_top[:], score[:], best[:].to_broadcast([P, GTILES, EXPERTS]),
                                            ALU.subtract).then_inc(routed, 1)
                    for j in range(GTILES):
                        nc.vector.max_index(top_at[:, j, :], top[:, j, :], score[:, j, :]).then_inc(routed, 1)
                    dve.wait_ge(routed, ROUTE_OPS * g + 7)
                    nc.vector.tensor_copy(top_id[:], top_at[:]).then_inc(routed, 1)
                    dve.wait_ge(routed, ROUTE_OPS * g + 8)
                    for j in range(GTILES):
                        nc.vector.tensor_scalar(chosen[:, j, :], ids[:], top_id[:, j, 0:1], None, ALU.is_equal
                                                ).then_inc(routed, 1)
                    dve.wait_ge(routed, ROUTE_OPS * g + 10)
                    for j in range(GTILES):
                        nc.vector.scalar_tensor_tensor(chosen[:, j, :], ids[:], top_id[:, j, 1:2], chosen[:, j, :],
                                                       ALU.is_equal, ALU.add).then_inc(routed, 1)

            def gates(body, q):
                g = 2 * body + q
                if in_range(g):
                    dve.wait_ge(expd_ready, 4 * g + 1)
                    dve.wait_ge(routed, ROUTE_OPS * (g + 1))
                    nc.vector.tensor_tensor(kept[:], expd[:], chosen[:], ALU.mult).then_inc(expd_ready, 1)
                    dve.wait_ge(expd_ready, 4 * g + 2)
                    nc.vector.reduce_sum(total[:], kept[:], AX.X).then_inc(expd_ready, 1)
                    dve.wait_ge(expd_ready, 4 * g + 3)
                    nc.vector.reciprocal(share[:], total[:]).then_inc(expd_ready, 1)
                    dve.wait_ge(expd_ready, 4 * g + 4)
                    shape = [P, GTILES, GATE_BLOCKS, EXPERTS]
                    nc.vector.tensor_tensor(gate[q][:, :, :, 0:EXPERTS], kept[:].unsqueeze(2).to_broadcast(shape),
                                            share[:].unsqueeze(2).to_broadcast(shape), ALU.mult
                                            ).then_inc(gate_ready, 1)

            def gates_low(body, q):
                g = 2 * body + q
                if in_range(g):
                    dve.wait_ge(gate_high_ready, g + 1)
                    low = gate_t[64:96, :]
                    nc.vector.tensor_tensor(low, r_bank[64:96, 0, :], low, ALU.subtract).then_inc(gate_t_ready, 1)

            def take_bias(g, q, body):
                dve.wait_ge(y_bias_ready, g + 1)
                wait(dve, ye_taken, YU * g)
                wait(dve, out_stored[q], 16 * body)
                nc.vector.tensor_tensor(acc[q][:], y_bank[q * YU % 2][:, :, 0:DIM], y_buf[q][:], ALU.add
                                        ).then_inc(ye_taken, 1)

            def take_expert(g, q, e):
                dve.wait_ge(mixed_in, EU * g + (e + 1) * UNITS)
                dve.wait_ge(ye_taken, YU * g + 1 + e)
                for j in range(GTILES):
                    last = nc.vector.scalar_tensor_tensor(acc[q][:, j, :], y_bank[(q * YU + 1 + e) % 2][:, j, 0:DIM],
                                                          gate[q][:, j, 0, e:e + 1], acc[q][:, j, :], ALU.mult, ALU.add)
                last.then_inc(ye_taken, 1)

            def take_low(g, n):
                dve.wait_ge(mh_ready, EU * g + n + 1)
                wait(dve, mixed_in, EU * g + n - MID + 1)
                nc.vector.scalar_tensor_tensor(ml[n % MID][:], mid_bank[n % MID][:], 0.0, mh[n % MID][:],
                                               ALU.max, ALU.subtract).then_inc(ml_ready, 1)

            def group(body, q):
                g = 2 * body + q
                nxt = (body + q, 1 - q)
                take_bias(g, q, body)
                for n in range(EU):
                    if isinstance(g, int) and g == 0 and n % UNITS == 1 and n // UNITS + 2 < EXPERTS:
                        split_low(n // UNITS + 2)
                    take_low(g, n)
                    e = (n - LAG - UNITS + 1) // UNITS
                    if n >= LAG + UNITS and (n - LAG) % UNITS == 0:
                        take_expert(g, q, e)
                    if n == 2:
                        statistics(*nxt)
                    elif n == 4:
                        layernorm(*nxt)
                    elif n == 8:
                        split_x(*nxt)
                    elif n == 13:
                        route(*nxt)
                    elif n == 16:
                        gates(*nxt)
                    elif n == 21:
                        gates_low(*nxt)
                take_expert(g, q, EXPERTS - 1)

            statistics(0, 0)
            layernorm(0, 0)
            split_low(0)
            split_x(0, 0)
            dve.wait_ge(small_in, 16 * len(SMALL))
            route(0, 0)
            gates(0, 0)
            nc.vector.tensor_copy(b2_parts[:], b2_in[:]).then_inc(b2_split, 1)
            dve.wait_ge(b2_split, 1)
            nc.vector.tensor_tensor(b2_parts[32:64], b2_in[32:64], b2_parts[32:64], ALU.subtract).then_inc(b2_split, 1)
            gates_low(0, 0)
            split_low(1)
            run_groups(dve, group)

        @block.scalar
        def _(act):
            def split_high(e):
                i = e % STAGES
                act.wait_ge(stage_in[i], 48 * (e // STAGES + 1))
                nc.scalar.copy(w1h_a[:, e], stage_a[i][:]).then_inc(w_hi_ready, 1)
                nc.scalar.copy(w1h_b[:, e], stage_b[i][:]).then_inc(w_hi_ready, 1)
                nc.scalar.copy(w2h[:, e], stage_2[i][:]).then_inc(w_hi_ready, 1)

            def take_xt(body, q):
                g = 2 * body + q
                if in_range(g):
                    act.wait_ge(xt_ps_ready, g + 1)
                    wait(act, r1_ready, g)
                    wait(act, xl_ready, 2 * g)
                    nc.scalar.copy(xt[:], x_bank[:]).then_inc(xt_ready, 1)
                    wait(act, mid_ready, EU * (g - 1))
                    for b in range(2):
                        nc.scalar.copy(xh[q][:, b, :], x_bank[:, b, :]).then_inc(xh_ready, 1)
                    nc.scalar.copy(xe[q][0:HI, :], x_bank[0:HI, 1, :]).then_inc(xh_ready, 1)

            def router_relu(body, q):
                g = 2 * body + q
                if in_range(g):
                    act.wait_ge(r1_ready, g + 1)
                    wait(act, score_ps_ready, g)
                    for b, nf in enumerate((P, HI)):
                        nc.scalar.activation(rh[0:nf, b, :], r_bank[0:nf, b, :], ACT.Relu, bias=r1_bias[0:nf, b:b + 1]
                                             ).then_inc(rh_ready, 1)

            def exponentials(body, q):
                g = 2 * body + q
                if in_range(g):
                    act.wait_ge(routed, ROUTE_OPS * g + 5)
                    nc.scalar.activation(expd[:], less_top[:], ACT.Exp).then_inc(expd_ready, 1)

            def take_gates(body, q):
                g = 2 * body + q
                if in_range(g):
                    act.wait_ge(gate_ps_ready, g + 1)
                    wait(act, y_bias_ready, g)
                    nc.scalar.copy(gate_t[:], r_bank[0:GATE_BLOCKS * 32, 0, :]).then_inc(gate_high_ready, 1)

            def take_high(g, n):
                act.wait_ge(mid_ready, EU * g + n + 1)
                wait(act, mixed_in, EU * g + n - MID + 1)
                nc.scalar.activation(mh[n % MID][:], mid_bank[n % MID][:], ACT.Relu).then_inc(mh_ready, 1)

            def group(body, q):
                g = 2 * body + q
                nxt = (body + q, 1 - q)
                for n in range(EU):
                    if isinstance(g, int) and g == 0 and n % UNITS == 1 and n // UNITS + 2 < EXPERTS:
                        split_high(n // UNITS + 2)
                    take_high(g, n)
                    if n == 6:
                        take_xt(*nxt)
                    elif n == 10:
                        router_relu(*nxt)
                    elif n == 14:
                        exponentials(*nxt)
                    elif n == 19:
                        take_gates(*nxt)

            split_high(0)
            take_xt(0, 0)
            act.wait_ge(small_in, 16 * len(SMALL))
            router_relu(0, 0)
            exponentials(0, 0)
            take_gates(0, 0)
            split_high(1)
            run_groups(act, group)

        @block.gpsimd
        def _(pool):
            pool.wait_ge(consts_set, CONSTS)

            def sum_rows(body, q):
                g = 2 * body + q
                if in_range(g):
                    pool.wait_ge(rows_in[q], 32 * (body + 1))
                    wait(pool, ye_taken, YU * (g - 2) + 1)
                    nc.gpsimd.tensor_tensor(y_buf[q][:], h_in[q][:], a_in[q][:], ALU.add).then_inc(y_ready, 1)

            def inverse_deviation(body, q):
                g = 2 * body + q
                if in_range(g):
                    pool.wait_ge(meanvar_ready, GTILES * (g + 1))
                    nc.gpsimd.tensor_tensor(var_eps[:], meanvar[:, :, 1], eps[:], ALU.add).then_inc(var_ready, 1)
                    pool.wait_ge(var_ready, g + 1)
                    wait(pool, xn_ready, g)
                    nc.gpsimd.tensor_tensor(rstd[:], var_eps[:], minus_half[:], ALU.pow).then_inc(rstd_ready, 1)

            def prepare(body, q):
                sum_rows(body, q)
                inverse_deviation(body, q)

            def split_low(e):
                pool.wait_ge(w_hi_ready, 3 * (e + 1))
                nc.gpsimd.tensor_tensor(w2l[:, e], stage_2[e % STAGES][:], w2h[:, e], ALU.subtract
                                        ).then_inc(w2_lo_ready, 1)

            def group(body, q):
                prepare(body + q, 1 - q)
                if isinstance(body, int) and body + q == 0:
                    for e in range(2, EXPERTS):
                        split_low(e)

            prepare(0, 0)
            split_low(0)
            split_low(1)
            run_groups(pool, group)


def build(nc, x_t, w_tok, w_qk_a, w_qk_b, w_v_a, w_v_b, b_tok, b_qk, b_v, ln_cols, row_consts, ident, w1_a, w1_b, w2, b1,
          wr1_a, wr1_b, br1, wr2_a, wr2_b, br2, b2, expert_ids, out):
    h_rows = nc.dram_tensor("h_rows", (PAIRS, TILES, HALF, DIM), F32).ap()
    att_rows = nc.dram_tensor("att_rows", (PAIRS, TILES, HALF, DIM), F32).ap()
    b1_parts = nc.dram_tensor("b1_parts", (3, EXPERTS * HIDDEN), BF16).ap()
    attention_phase(nc, x_t, w_tok, w_qk_a, w_qk_b, w_v_a, w_v_b, b_tok, b_qk, b_v, ln_cols, row_consts, ident,
                    h_rows, att_rows)

    def by_group(t):
        return t.rearrange("u c p e -> (u c p) e").rearrange("(g t) e -> g t e", t=GT)

    expert_phase(nc, by_group(h_rows), by_group(att_rows), w1_a, w1_b, w2, b1, wr1_a, wr1_b, br1, wr2_a, wr2_b, br2, b2,
                 expert_ids, ident, b1_parts, out.rearrange("(g t) e -> g t e", t=GT))


def layout(x, L0_tok_W, L0_tok_b, L0_attn_qkv_w, L0_attn_qkv_b, L0_attn_ln_g, L0_attn_ln_b, L0_ffn_W1, L0_ffn_b1,
           L0_ffn_W2, L0_ffn_b2, L0_ffn_Wr1, L0_ffn_br1, L0_ffn_Wr2, L0_ffn_br2):
    import numpy as np

    x = np.asarray(x).reshape(IMAGES, 3, 14, 16, 14, 16).transpose(0, 1, 2, 4, 5, 3)
    x = x.reshape(PAIRS, COLS, PCH, P).transpose(0, 3, 2, 1)
    order = np.arange(2 * DIM).reshape(2 * GROUPS, HG, 1, HEAD_DIM)
    order = np.broadcast_to(order, (2 * GROUPS, HG, 2, HEAD_DIM)).reshape(2 * GROUPS, P)
    qkv_w, qkv_b = np.asarray(L0_attn_qkv_w), np.asarray(L0_attn_qkv_b)
    w_qk = qkv_w[order].transpose(2, 0, 1)
    w_v = qkv_w[2 * DIM:].T
    g, b = np.asarray(L0_attn_ln_g), np.asarray(L0_attn_ln_b)
    ln_cols = np.stack([g[:P], b[:P], np.tile(g[P:], 2), np.tile(b[P:], 2)], axis=1)
    row_consts = np.zeros((P, 2 + HG), np.float32)
    tilde = np.arange(P) % ROWS >= HEAD_DIM
    row_consts[:, 0] = np.where(tilde, -BETA * SCALE, (1.0 + BETA) * SCALE)
    row_consts[:, 1] = tilde
    for hh in range(HG):
        row_consts[PARTS + 2 * hh:PARTS + 2 * hh + 2, 2 + hh] = -MAX_SCALE
    w1 = np.asarray(L0_ffn_W1).transpose(2, 0, 1)
    w2 = np.asarray(L0_ffn_W2).reshape(EXPERTS, DIM, FCH, P).transpose(3, 0, 2, 1)
    wr1, wr2 = np.asarray(L0_ffn_Wr1).T, np.asarray(L0_ffn_Wr2).T
    br1 = np.asarray(L0_ffn_br1)
    return {
        "x_t": x,
        "w_tok": np.asarray(L0_tok_W).T.reshape(PCH, P, DIM).transpose(1, 0, 2),
        "w_qk_a": w_qk[:P], "w_qk_b": np.concatenate([w_qk[P:], w_qk[P:]]),
        "w_v_a": w_v[:P], "w_v_b": np.concatenate([w_v[P:], w_v[P:]]),
        "b_tok": np.tile(np.asarray(L0_tok_b), (HALF, 1)),
        "b_qk": qkv_b[order].T,
        "b_v": np.tile(qkv_b[2 * DIM:], (HALF, 1)),
        "ln_cols": ln_cols, "row_consts": row_consts, "ident": np.eye(P, dtype=np.float32),
        "w1_a": w1[:P], "w1_b": np.concatenate([w1[P:], w1[P:]]), "w2": w2,
        "b1": np.asarray(L0_ffn_b1).reshape(EXPERTS * FCH, P),
        "wr1_a": wr1[:P], "wr1_b": wr1[P:],
        "br1": np.stack([br1[:P], np.tile(br1[P:], 2)], axis=1),
        "wr2_a": wr2[:P], "wr2_b": wr2[P:],
        "br2": np.tile(np.asarray(L0_ffn_br2), (P, GTILES, 1)),
        "b2": np.pad(np.broadcast_to(np.asarray(L0_ffn_b2), (GATE_BLOCKS, EXPERTS, DIM)),
                     ((0, 0), (0, 32 - EXPERTS), (0, 0))).reshape(GATE_BLOCKS * 32, DIM),
        "expert_ids": np.tile(np.arange(EXPERTS, dtype=np.float32), (P, 1)),
    }


def kernel(**inputs):
    import numpy as np
    import concourse.bacc as bacc
    from concourse.bass_utils import run_bass_kernel_spmd

    nc = bacc.Bacc("TRN2", target_bir_lowering=False, num_devices=1)
    arrays, args = {}, {}
    for name, a in layout(**inputs).items():
        a = np.ascontiguousarray(a)
        arrays[f"in_{name}"] = a
        args[name] = nc.dram_tensor(f"in_{name}", a.shape, mybir.dt.from_np(a.dtype), kind="ExternalInput").ap()
    out = nc.dram_tensor("out_rows", (IMAGES * TOKENS, DIM), F32, kind="ExternalOutput").ap()
    build(nc, out=out, **args)
    result = run_bass_kernel_spmd(nc, [arrays], core_ids=[0])
    return result.results[0]["out_rows"].reshape(IMAGES, TOKENS, DIM)
```
